# Optimizing a Trainium2 kernel written in Bass

```python
import numpy as np
import jax
import jax.numpy as jnp

def _softmax(x, axis=-1):
    return jax.nn.softmax(x, axis=axis)

def _gelu(x):
    return jax.nn.gelu(x, approximate=True)

def _silu(x):
    return jax.nn.silu(x)

def _sigmoid(x):
    return jax.nn.sigmoid(x)

def _layernorm(x, axis=-1, eps=1e-05):
    m = jnp.mean(x, axis=axis, keepdims=True)
    v = jnp.var(x, axis=axis, keepdims=True)
    return (x - m) / jnp.sqrt(v + eps)

def _scatter_add(tgt, idx, src, axis=0):
    return tgt.at[idx].add(src)

def _segment_sum(src, seg, n):
    return jax.ops.segment_sum(src, seg, n)
kernel_name = 'mk_early_fusion_embed_d1_tok_img768_r4_0c78fc'

def setup_inputs(seed: int=0):
    np.random.seed(seed)
    _w = jnp.asarray

    def _rec_inputs():
        import jax
        import jax.numpy as jnp
        _rk = jax.random.key(seed)
        x = -0.00040386 + 0.999972 * jax.random.normal(jax.random.fold_in(_rk, 1), (32, 64, 64, 3), jnp.float32)
        x_txt = jax.random.randint(jax.random.fold_in(_rk, 51), (32, 77), 0, 12500, jnp.int32)
        itok_BS_0_99 = jax.random.randint(jax.random.fold_in(_rk, 71), (32, 77), 0, 100, jnp.int32)
        itok_BS_1_36498 = jax.random.randint(jax.random.fold_in(_rk, 72), (32, 77), 1, 36499, jnp.int32)
        itok_BS_0_2047 = jax.random.randint(jax.random.fold_in(_rk, 73), (32, 77), 0, 512, jnp.int32)
        fside_BS_concept_values = 0.00458123 + 1.00259 * jax.random.normal(jax.random.fold_in(_rk, 74), (32, 77), jnp.float32)
        mask_BS_f1_0 = jnp.where(jnp.ones((32, 77), dtype=bool), 1.0, 0.0).astype(jnp.float32)
        mask_BS_i2_0 = jnp.where(jnp.ones((32, 77), dtype=bool), 2, 0).astype(jnp.int32)
        return (x, x_txt, itok_BS_0_99, itok_BS_1_36498, itok_BS_0_2047, fside_BS_concept_values, mask_BS_f1_0, mask_BS_i2_0)
    x, x_txt, itok_BS_0_99, itok_BS_1_36498, itok_BS_0_2047, fside_BS_concept_values, mask_BS_f1_0, mask_BS_i2_0 = _rec_inputs()

    def _L0_tok_setup():
        import jax, jax.numpy as jnp
        import numpy as np
        PATCH = 16
        key = jax.random.key(seed)
        k1, k2, k3 = jax.random.split(key, 3)
        B, H, Wd, C = (64, 64, 64, 3)
        patch_dim = PATCH * PATCH * C
        hidden = 192
        num_patches = H // PATCH * (Wd // PATCH)
        img = jax.random.normal(k1, (B, H, Wd, C), dtype=jnp.float32)
        W = jax.random.normal(k2, (patch_dim, hidden), dtype=jnp.float32) * (1.0 / np.sqrt(patch_dim))
        b = jnp.zeros((hidden,), dtype=jnp.float32)
        pos_emb = jax.random.normal(k3, (num_patches, hidden), dtype=jnp.float32) * 0.02
        return {'img': img, 'W': W, 'b': b, 'pos_emb': pos_emb}
    _L0_tok_all = _L0_tok_setup()
    _L0_tok_in = {k: v for k, v in _L0_tok_all.items() if k in ('W', 'b', 'pos_emb')}
    del _L0_tok_all

    def _L0_txt_setup():
        import jax, jax.numpy as jnp
        import numpy as np
        import math
        B, S = (32, 512)
        H = 192
        T = 16
        VOCAB = 12500
        N_SEG = 3
        MAX_POS = 512

        def make_pe(max_len, dim):
            pos = np.arange(max_len, dtype=np.float32)[:, None]
            div = np.exp(np.arange(0, dim, 2, dtype=np.float32) * (-math.log(10000.0) / dim))
            pe = np.zeros((max_len, dim), dtype=np.float32)
            pe[:, 0::2] = np.sin(pos * div)
            pe[:, 1::2] = np.cos(pos * div)
            return jnp.asarray(pe)
        PE = make_pe(MAX_POS, T)

        def time_embed(t, w, phi):
            return jnp.sin(t.astype(jnp.float32)[..., None] * w[0] + phi[0])
        key = jax.random.key(seed)
        ks = jax.random.split(key, 16)
        inp = {'input_ids': jax.random.randint(ks[0], (B, S), 0, VOCAB), 'ages': jax.random.randint(ks[1], (B, S), 0, 100), 'dates': jax.random.randint(ks[2], (B, S), 0, 9125), 'visit_concept_orders': jax.random.randint(ks[3], (B, S), 0, MAX_POS), 'concept_values': jax.random.normal(ks[4], (B, S), dtype=jnp.float32), 'concept_value_masks': (jax.random.uniform(ks[5], (B, S)) < 0.5).astype(jnp.float32), 'visit_segments': jax.random.randint(ks[6], (B, S), 0, N_SEG), 'concept_emb': jax.random.normal(ks[7], (VOCAB, H), dtype=jnp.float32) * 0.02, 'segment_emb': jax.random.normal(ks[8], (N_SEG, H), dtype=jnp.float32) * 0.02, 'w_age': jax.random.normal(ks[9], (1, T), dtype=jnp.float32), 'phi_age': jax.random.normal(ks[10], (1, T), dtype=jnp.float32), 'merge_w': jax.random.normal(ks[11], (H + 1, H), dtype=jnp.float32) * 0.02, 'merge_b': jnp.zeros((H,), dtype=jnp.float32), 'proj_w': jax.random.normal(ks[12], (H + 3 * T, H), dtype=jnp.float32) * 0.02, 'proj_b': jnp.zeros((H,), dtype=jnp.float32)}
        return inp
    _L0_txt_all = _L0_txt_setup()
    _L0_txt_in = {k: v for k, v in _L0_txt_all.items() if k in ('concept_emb', 'segment_emb', 'w_age', 'phi_age', 'merge_w', 'merge_b', 'proj_w', 'proj_b')}
    del _L0_txt_all

    def _L0_attn_setup():
        import jax, jax.numpy as jnp
        import numpy as np
        import math
        D_MODEL, N_HEADS, D_HEAD, SEQ, BATCH = (192, 12, 64, 256, 8)
        INIT_RANGE = 0.02
        key = jax.random.key(seed)
        ks = jax.random.split(key, 6)
        x = jax.random.normal(ks[0], (BATCH, SEQ, D_MODEL), dtype=jnp.float32)
        W_Q = jax.random.normal(ks[1], (N_HEADS, D_MODEL, D_HEAD), dtype=jnp.float32) * INIT_RANGE
        W_K = jax.random.normal(ks[2], (N_HEADS, D_MODEL, D_HEAD), dtype=jnp.float32) * INIT_RANGE
        W_V = jax.random.normal(ks[3], (N_HEADS, D_MODEL, D_HEAD), dtype=jnp.float32) * INIT_RANGE
        W_O = jax.random.normal(ks[4], (N_HEADS, D_HEAD, D_MODEL), dtype=jnp.float32) * INIT_RANGE
        b_Q = jnp.zeros((N_HEADS, D_HEAD), dtype=jnp.float32)
        b_K = jnp.zeros((N_HEADS, D_HEAD), dtype=jnp.float32)
        b_V = jnp.zeros((N_HEADS, D_HEAD), dtype=jnp.float32)
        b_O = jnp.zeros((D_MODEL,), dtype=jnp.float32)
        return {'normalized_resid_pre': x, 'W_Q': W_Q, 'b_Q': b_Q, 'W_K': W_K, 'b_K': b_K, 'W_V': W_V, 'b_V': b_V, 'W_O': W_O, 'b_O': b_O}
    _L0_attn_all = _L0_attn_setup()
    _L0_attn_in = {k: v for k, v in _L0_attn_all.items() if k in ('W_Q', 'b_Q', 'W_K', 'b_K', 'W_V', 'b_V', 'W_O', 'b_O')}
    del _L0_attn_all

    def _L0_ffn_setup():
        import jax, jax.numpy as jnp
        import numpy as np
        DIM = 192
        HEADS = 12
        HIDDEN = 768
        E = 8
        TOPK = 2
        EPS = 1e-05

        def _ln(x, g, b):
            m = x.mean(-1, keepdims=True)
            v = jnp.mean((x - m) ** 2, axis=-1, keepdims=True)
            return (x - m) * jax.lax.rsqrt(v + EPS) * g + b
        key = jax.random.key(seed)
        ks = jax.random.split(key, 10)
        s = 0.02
        return {'x': jax.random.normal(ks[0], (8, 256, DIM), jnp.float32), 'ln1_g': jnp.ones((DIM,), jnp.float32), 'ln1_b': jnp.zeros((DIM,), jnp.float32), 'qkv_w': jax.random.normal(ks[1], (DIM, 3 * DIM), jnp.float32) * s, 'proj_w': jax.random.normal(ks[2], (DIM, DIM), jnp.float32) * s, 'proj_b': jnp.zeros((DIM,), jnp.float32), 'ln2_g': jnp.ones((DIM,), jnp.float32), 'ln2_b': jnp.zeros((DIM,), jnp.float32), 'gate_w': jax.random.normal(ks[3], (DIM, E), jnp.float32) * s, 'gate_b': jnp.zeros((E,), jnp.float32), 'w1': jax.random.normal(ks[4], (E, DIM, HIDDEN), jnp.float32) * s, 'b1': jnp.zeros((E, HIDDEN), jnp.float32), 'w2': jax.random.normal(ks[5], (E, HIDDEN, DIM), jnp.float32) * s, 'b2': jnp.zeros((E, DIM), jnp.float32)}
    _L0_ffn_all = _L0_ffn_setup()
    _L0_ffn_in = {k: v for k, v in _L0_ffn_all.items() if k in ('ln1_g', 'ln1_b', 'qkv_w', 'proj_w', 'proj_b', 'ln2_g', 'ln2_b', 'gate_w', 'gate_b', 'w1', 'b1', 'w2', 'b2')}
    del _L0_ffn_all
    return {'x': x, 'x_txt': x_txt, 'itok_BS_0_99': itok_BS_0_99, 'itok_BS_1_36498': itok_BS_1_36498, 'itok_BS_0_2047': itok_BS_0_2047, 'fside_BS_concept_values': fside_BS_concept_values, 'mask_BS_f1_0': mask_BS_f1_0, 'mask_BS_i2_0': mask_BS_i2_0, 'L0_tok_W': _L0_tok_in['W'], 'L0_tok_b': _L0_tok_in['b'], 'L0_tok_pos_emb': _L0_tok_in['pos_emb'], 'L0_txt_concept_emb': _L0_txt_in['concept_emb'], 'L0_txt_segment_emb': _L0_txt_in['segment_emb'], 'L0_txt_w_age': _L0_txt_in['w_age'], 'L0_txt_phi_age': _L0_txt_in['phi_age'], 'L0_txt_merge_w': _L0_txt_in['merge_w'], 'L0_txt_merge_b': _L0_txt_in['merge_b'], 'L0_txt_proj_w': _L0_txt_in['proj_w'], 'L0_txt_proj_b': _L0_txt_in['proj_b'], 'L0_attn_W_Q': _L0_attn_in['W_Q'], 'L0_attn_b_Q': _L0_attn_in['b_Q'], 'L0_attn_W_K': _L0_attn_in['W_K'], 'L0_attn_b_K': _L0_attn_in['b_K'], 'L0_attn_W_V': _L0_attn_in['W_V'], 'L0_attn_b_V': _L0_attn_in['b_V'], 'L0_attn_W_O': _L0_attn_in['W_O'], 'L0_attn_b_O': _L0_attn_in['b_O'], 'L0_ffn_ln1_g': _L0_ffn_in['ln1_g'], 'L0_ffn_ln1_b': _L0_ffn_in['ln1_b'], 'L0_ffn_qkv_w': _L0_ffn_in['qkv_w'], 'L0_ffn_proj_w': _L0_ffn_in['proj_w'], 'L0_ffn_proj_b': _L0_ffn_in['proj_b'], 'L0_ffn_ln2_g': _L0_ffn_in['ln2_g'], 'L0_ffn_ln2_b': _L0_ffn_in['ln2_b'], 'L0_ffn_gate_w': _L0_ffn_in['gate_w'], 'L0_ffn_gate_b': _L0_ffn_in['gate_b'], 'L0_ffn_w1': _L0_ffn_in['w1'], 'L0_ffn_b1': _L0_ffn_in['b1'], 'L0_ffn_w2': _L0_ffn_in['w2'], 'L0_ffn_b2': _L0_ffn_in['b2']}

def reference(x, x_txt, itok_BS_0_99, itok_BS_1_36498, itok_BS_0_2047, fside_BS_concept_values, mask_BS_f1_0, mask_BS_i2_0, L0_tok_W, L0_tok_b, L0_tok_pos_emb, L0_txt_concept_emb, L0_txt_segment_emb, L0_txt_w_age, L0_txt_phi_age, L0_txt_merge_w, L0_txt_merge_b, L0_txt_proj_w, L0_txt_proj_b, L0_attn_W_Q, L0_attn_b_Q, L0_attn_W_K, L0_attn_b_K, L0_attn_W_V, L0_attn_b_V, L0_attn_W_O, L0_attn_b_O, L0_ffn_ln1_g, L0_ffn_ln1_b, L0_ffn_qkv_w, L0_ffn_proj_w, L0_ffn_proj_b, L0_ffn_ln2_g, L0_ffn_ln2_b, L0_ffn_gate_w, L0_ffn_gate_b, L0_ffn_w1, L0_ffn_b1, L0_ffn_w2, L0_ffn_b2):
    import jax
    import jax.numpy as jnp

    def _L0_tok_ref(img, W, b, pos_emb):
        import jax, jax.numpy as jnp
        import numpy as np
        PATCH = 16
        B, H, Wd, C = img.shape
        ph, pw = (H // PATCH, Wd // PATCH)
        p = img.reshape(B, ph, PATCH, pw, PATCH, C)
        p = p.transpose(0, 1, 3, 2, 4, 5).reshape(B, ph * pw, PATCH * PATCH * C)
        out = jnp.einsum('bnk,kh->bnh', p, W) + b + pos_emb[None, :, :]
        return out

    def _L0_txt_ref(input_ids, ages, dates, visit_concept_orders, concept_values, concept_value_masks, visit_segments, concept_emb, segment_emb, w_age, phi_age, merge_w, merge_b, proj_w, proj_b):
        import jax, jax.numpy as jnp
        import numpy as np
        import math
        B, S = (32, 512)
        H = 192
        T = 16
        VOCAB = 12500
        N_SEG = 3
        MAX_POS = 512

        def make_pe(max_len, dim):
            pos = np.arange(max_len, dtype=np.float32)[:, None]
            div = np.exp(np.arange(0, dim, 2, dtype=np.float32) * (-math.log(10000.0) / dim))
            pe = np.zeros((max_len, dim), dtype=np.float32)
            pe[:, 0::2] = np.sin(pos * div)
            pe[:, 1::2] = np.cos(pos * div)
            return jnp.asarray(pe)
        PE = make_pe(MAX_POS, T)

        def time_embed(t, w, phi):
            return jnp.sin(t.astype(jnp.float32)[..., None] * w[0] + phi[0])
        x = concept_emb[input_ids]
        xv = jnp.concatenate([x, concept_values[..., None]], axis=-1)
        xv = xv @ merge_w + merge_b
        x = jnp.where(concept_value_masks[..., None].astype(bool), xv, x)
        age_e = time_embed(ages, w_age, phi_age)
        time_e = time_embed(dates, w_age, phi_age)
        mins = jnp.min(visit_concept_orders, axis=-1, keepdims=True)
        orders = jnp.abs(visit_concept_orders - mins)
        pos_e = PE[orders]
        h = jnp.concatenate([x, time_e, age_e, pos_e], axis=-1)
        h = jax.nn.gelu(h @ proj_w + proj_b, approximate=False)
        return h + segment_emb[visit_segments]

    def _L0_attn_ref(normalized_resid_pre, W_Q, b_Q, W_K, b_K, W_V, b_V, W_O, b_O):
        import jax, jax.numpy as jnp
        import numpy as np
        import math
        D_MODEL, N_HEADS, D_HEAD, SEQ, BATCH = (192, 12, 64, 256, 8)
        INIT_RANGE = 0.02
        x = normalized_resid_pre
        q = jnp.einsum('bsd,hde->bshe', x, W_Q) + b_Q
        k = jnp.einsum('bsd,hde->bshe', x, W_K) + b_K
        v = jnp.einsum('bsd,hde->bshe', x, W_V) + b_V
        scores = jnp.einsum('bqhe,bkhe->bhqk', q, k) / math.sqrt(D_HEAD)
        s = x.shape[1]
        causal = jnp.tril(jnp.ones((s, s), dtype=bool))
        scores = jnp.where(causal[None, None], scores, -jnp.inf)
        pattern = jax.nn.softmax(scores, axis=-1)
        pattern = jnp.where(jnp.isnan(pattern), 0.0, pattern)
        z = jnp.einsum('bhqk,bkhe->bqhe', pattern, v)
        attn_out = jnp.einsum('bqhe,hed->bqd', z, W_O) + b_O
        return attn_out

    def _L0_ffn_ref(x, ln1_g, ln1_b, qkv_w, proj_w, proj_b, ln2_g, ln2_b, gate_w, gate_b, w1, b1, w2, b2):
        import jax, jax.numpy as jnp
        import numpy as np
        DIM = 192
        HEADS = 12
        HIDDEN = 768
        E = 8
        TOPK = 2
        EPS = 1e-05

        def _ln(x, g, b):
            m = x.mean(-1, keepdims=True)
            v = jnp.mean((x - m) ** 2, axis=-1, keepdims=True)
            return (x - m) * jax.lax.rsqrt(v + EPS) * g + b
        B, S, D = x.shape
        hd = D // HEADS
        h = _ln(x, ln1_g, ln1_b)
        qkv = (h @ qkv_w).reshape(B, S, 3, HEADS, hd).transpose(2, 0, 3, 1, 4)
        q, k, v = (qkv[0], qkv[1], qkv[2])
        att = jax.nn.softmax(jnp.einsum('bhqd,bhkd->bhqk', q, k) * hd ** (-0.5), axis=-1)
        o = jnp.einsum('bhqk,bhkd->bhqd', att, v).transpose(0, 2, 1, 3).reshape(B, S, D)
        x = x + o @ proj_w + proj_b
        h2 = _ln(x, ln2_g, ln2_b).reshape(B * S, D)
        logits = h2 @ gate_w + gate_b
        wts, sel = jax.lax.top_k(logits, TOPK)
        wts = jax.nn.softmax(wts.astype(jnp.float32), axis=-1).astype(x.dtype)
        cw = (jax.nn.one_hot(sel, E, dtype=x.dtype) * wts[..., None]).sum(axis=1)
        res = jnp.zeros_like(h2)
        for e in range(E):
            he = jax.nn.gelu(h2 @ w1[e] + b1[e], approximate=False)
            res = res + cw[:, e:e + 1] * (he @ w2[e] + b2[e])
        return x + res.reshape(B, S, D)
    h = _L0_tok_ref(x, L0_tok_W, L0_tok_b, L0_tok_pos_emb)
    h = jnp.concatenate([h, _L0_txt_ref(x_txt, itok_BS_0_99, itok_BS_1_36498, itok_BS_0_2047, fside_BS_concept_values, mask_BS_f1_0, mask_BS_i2_0, L0_txt_concept_emb, L0_txt_segment_emb, L0_txt_w_age, L0_txt_phi_age, L0_txt_merge_w, L0_txt_merge_b, L0_txt_proj_w, L0_txt_proj_b)], axis=1)
    h = h + _L0_attn_ref(_layernorm(h, axis=-1), L0_attn_W_Q, L0_attn_b_Q, L0_attn_W_K, L0_attn_b_K, L0_attn_W_V, L0_attn_b_V, L0_attn_W_O, L0_attn_b_O)
    h = h + _L0_ffn_ref(_layernorm(h, axis=-1), L0_ffn_ln1_g, L0_ffn_ln1_b, L0_ffn_qkv_w, L0_ffn_proj_w, L0_ffn_proj_b, L0_ffn_ln2_g, L0_ffn_ln2_b, L0_ffn_gate_w, L0_ffn_gate_b, L0_ffn_w1, L0_ffn_b1, L0_ffn_w2, L0_ffn_b2)
    return h

_drawn_inputs = setup_inputs


def setup_inputs(seed=0):
    import zlib

    import numpy as np

    out = dict(_drawn_inputs(seed))
    spreads = {'L0_tok_b': (0.0, 0.1),
     'L0_txt_merge_b': (0.0, 0.1),
     'L0_txt_proj_b': (0.0, 0.1),
     'L0_attn_b_Q': (0.0, 0.8),
     'L0_attn_b_K': (0.0, 0.8),
     'L0_attn_b_V': (0.0, 0.1),
     'L0_attn_b_O': (0.0, 0.1),
     'L0_ffn_ln1_g': (1.0, 0.6),
     'L0_ffn_ln1_b': (0.0, 0.799),
     'L0_ffn_proj_b': (0.0, 0.1),
     'L0_ffn_ln2_g': (1.0, 0.2),
     'L0_ffn_ln2_b': (0.0, 0.1),
     'L0_ffn_gate_b': (0.0, 0.1),
     'L0_ffn_b1': (0.0, 0.49),
     'L0_ffn_b2': (0.0, 0.1)}
    factors = {'fside_BS_concept_values': 3.563,
     'L0_tok_pos_emb': 4.274,
     'L0_txt_concept_emb': 8.0,
     'L0_txt_merge_w': 3.527,
     'L0_attn_W_Q': 3.704,
     'L0_attn_W_K': 3.447}
    for name, (base, spread) in spreads.items():
        noise = np.random.default_rng([zlib.crc32(name.encode()), seed]).standard_normal(out[name].shape)
        drawn = base * np.exp(spread * noise) if base else spread * noise
        out[name] = jnp.asarray(drawn.astype(out[name].dtype))
    for name, factor in factors.items():
        out[name] = (out[name] * factor).astype(out[name].dtype)
    return out
```

```python
import math
from contextlib import ExitStack

import numpy as np

import concourse.bass as bass
from concourse import mybir

ALU = mybir.AluOpType
ACT = mybir.ActivationFunctionType
AX = mybir.AxisListType
F32 = mybir.dt.float32
I32 = mybir.dt.int32

B, S_TXT, N_PATCH = 32, 77, 16
S = S_TXT + N_PATCH
D = 192
HALF = D // 2
VOCAB, N_SEG, T_EMB, MAX_POS = 12500, 3, 16, 512
HEADS, DH1, DH2 = 12, 64, 16
E, FF = 8, 768
EPS = 1e-5
NEG = -1e30

TT = 112
NT = B * S_TXT // TT
assert NT * TT == B * S_TXT
PATCH, IMG = 16, 64
KP = PATCH * PATCH * 3
F1W = D + 2
F2W = D + 3 * T_EMB + 2
C1, C2 = F1W // 2, F2W // 2

G = 4
NG = B // G
SL = 96
GT = G * SL
UH = 4
UN = HEADS // UH
PAIRS = HEADS * DH1 // 128
QUADS = HEADS * 32 // 128

TOPK = 2
ROW = D + 2
REGION = -(-(B * S + 128) // 128) * 128
SLOTS = TOPK * B * S
NTILE = -(-SLOTS // 128) + E - 1 + (-(-SLOTS // 128) + E - 1) % 2
SPARE = NTILE - SLOTS // 128 + 1
XS_ROWS = E * REGION + SPARE * 128
Y_ROWS = SLOTS + (E + SPARE) * 128

LP, CJ = 124, 6
NP_ = B * S // (LP * CJ)

ROUTE = 28
ROUTE_SEL = 17

MAGIC = 1.5 * 2.0 ** 23
TP1 = 6.28125
TP2 = math.floor((2 * math.pi - TP1) * 2 ** 18) / 2 ** 18
TP3 = 2 * math.pi - TP1 - TP2


def at_least(eng, sem, value):
    if not isinstance(value, int) or value > 0:
        eng.wait_ge(sem, value)


class Body:

    def __init__(self, n, i):
        self.n, self.i = n, i
        self.has_a, self.has_b, self.has_c, self.has_n = parts_of(n)
        self.fills, self.units = fills_of(n), units_of(n)
        self.steps = len(self.units) + LAG_PROJ + 2
        self.units_before = count_before(n, i, units_of, 1)
        self.fills_before = count_before(n, i, fills_of, 1) + 2
        self.bank_fills_before = count_before(n, i, fills_of, 2) + 1

    def fill(self, *label):
        k = self.fills.index(label)
        return k % 2, self.fills_before + k, self.bank_fills_before + k // 2


FIRST_FULL, LAST_FULL = 2, NG - 2
LAG_T, LAG_PV, LAG_PROJ = 3, 4, 6


def parts_of(n):
    return n < NG, 1 <= n <= NG, n >= 2, n < NG - 1


def count_before(n, i, of, per):
    first = sum(len(of(m)) for m in range(n)) // per
    if isinstance(i, int):
        return first
    each = len(of(n)) // per
    return i * each + (first - n * each)


def units_of(n):
    a, b, _, _ = parts_of(n)
    return [(kind, g, u) for g in range(G) for u in range(UN) for kind, on in (("a", a), ("b", b)) if on]


def posts_of(n, step):
    units, found = units_of(n), []
    for lag in (LAG_PROJ + 1, LAG_PROJ):
        k = step - lag
        if 0 <= k < len(units) and units[k][2] == UN - 1:
            kind, g, _ = units[k]
            if lag == LAG_PROJ:
                found += [("zT", g, 0), ("zT", g, 1)] if kind == "a" else [("z2T", g)]
            else:
                found += [("wo", g)] if kind == "a" else [("pj", g)]
    return found


def fills_of(n):
    a, b, c, nxt = parts_of(n)
    f = [(w, k) for k in range(PAIRS) for w in ("q", "k")] if a else []
    f += [("h2T", 0), ("h2T", 1)] if c else []
    f += [("yT", 0), ("yT", 1)] if b else []
    f += [("v", g, h) for g in range(G) for h in range(2)] if a else []
    f += [("gate",)] if c else []
    f += [(w, k) for k in range(QUADS) for w in ("q2", "k2")] + [("v2", 0), ("v2", 1)] if b else []
    f += [("rank",)] if c else []
    for step in range(len(units_of(n)) + LAG_PROJ + 2):
        f += posts_of(n, step)
    return f + ([("nT", 0), ("nT", 1)] if nxt else [])


def program(nc, t, out):
    def dram(name, shape):
        return nc.dram_tensor(name, shape, F32, kind="Internal").ap()

    txt_d = dram("txt_d", [B * S_TXT, D])
    img_d = dram("img_d", [B * N_PATCH, D])
    ord_d = dram("ord_d", [B, S_TXT])
    r_d = dram("r_d", [B * S, D])
    xs_d = dram("xs_d", [XS_ROWS, ROW])
    y_d = dram("y_d", [Y_ROWS, D])

    ctx = ExitStack()
    with ctx:
        scope = [ctx]

        def sb(name, shape, dt=F32):
            return scope[0].enter_context(nc.sbuf_tensor(name, shape, dt))

        def sem(name):
            return ctx.enter_context(nc.semaphore(name))

        banks = [ctx.enter_context(nc.psum_tensor(f"bank{k}", [128, 512], F32)) for k in range(8)]

        ident = sb("ident", [128, 128])
        zero_rows = sb("zero_rows", [128, E + SPARE, ROW])
        tail_at = sb("tail_at", [128, E], I32)
        counts = sb("counts", [128, E])
        tile_expert = sb("tile_expert", [1, NTILE], I32)
        tile_row = sb("tile_row", [1, NTILE], I32)
        ones_first = sb("ones_first", [SL, 128])
        g2col = sb("g2col", [HALF, 2])
        b2col = sb("b2col", [HALF, 2])
        base_row = sb("base_row", [128, E])
        part_id = sb("part_id", [128, 1])

        text_scope = ctx.enter_context(ExitStack())
        scope[0] = text_scope
        xpatch = sb("xpatch", [128, 4, KP])
        w_img = sb("w_img", [128, KP // 128, D])
        img_add = sb("img_add", [128, D])
        tok_b = sb("tok_b", [128, D])
        patchT = sb("patchT", [128, 2, KP // 128, 128])
        img_h = sb("img_h", [128, 4, D])
        tok_i = sb("tok_i", [NT, 6, TT], I32)
        tok_f = sb("tok_f", [NT, 7, TT])
        tok = sb("tok", [TT, 7, NT])
        ids = sb("ids", [TT, NT], I32)
        keep = sb("keep", [TT, NT, 2])
        segm = sb("segm", [TT, N_SEG, NT])
        vco_i = sb("vco_i", [B, S_TXT], I32)
        vco = sb("vco", [B, S_TXT])
        vmin = sb("vmin", [B, 1])
        order = sb("order", [B, S_TXT])
        frow = sb("frow", [TT, 3, T_EMB])
        prow = sb("prow", [TT, 3, T_EMB])
        qrow = sb("qrow", [TT, 3, T_EMB])
        arg = sb("arg", [TT, NT, 3 * T_EMB])
        turns = sb("turns", [TT, NT, 3 * T_EMB])
        f1all = sb("f1all", [TT, NT, F1W])
        f1 = sb("f1", [TT, 2, F1W])
        f1T = sb("f1T", [C1, 2, 2, TT])
        f2 = sb("f2", [TT, 2, F2W])
        f2T = sb("f2T", [C2, 2, 2, TT])
        blend = sb("blend", [TT, 2, D])
        txt_h = sb("txt_h", [TT, 2, D])
        w_merge = sb("w_merge", [C1, 2, D])
        w_feat = sb("w_feat", [C2, 2, D])
        seg_rows = sb("seg_rows", [TT, N_SEG, D])
        text_scope.close()

        attn_scope = ctx.enter_context(ExitStack())
        scope[0] = attn_scope
        wq, wk_, wo = sb("wq", [HALF, 2, HEADS * DH1]), sb("wk", [HALF, 2, HEADS * DH1]), sb("wo", [128, PAIRS, D])
        wv = sb("wv", [HALF + 1, 2, HEADS * DH1])
        bq, bk = sb("bq", [128, PAIRS]), sb("bk", [128, PAIRS])
        wq2, wk2 = sb("wq2", [HALF, 2, HEADS * 32]), sb("wk2", [HALF, 2, HEADS * 32])
        wv2, wp2 = sb("wv2", [HALF, 2, D]), sb("wp2", [HALF, 2, D])
        wgate = sb("wgate", [HALF, 2, E])
        g1col, b1col = sb("g1col", [HALF, 2]), sb("b1col", [HALF, 2])
        bo_row, pb_row = sb("bo_row", [SL, D]), sb("pb_row", [SL, D])
        gb_row = sb("gb_row", [SL, E])
        causal, padded = sb("causal", [SL, UH, SL]), sb("padded", [SL, UH, SL])
        earlier = sb("earlier", [SL, SL])
        neg_half = sb("neg_half", [SL, G])
        from_end = sb("from_end", [SL, E])
        dest0 = sb("dest0", [SL, G, TOPK])
        h_in = sb("h_in", [SL, G, D])
        n0 = sb("n0", [SL, G, D])
        h_res = sb("h_res", [SL, G, D])
        n1 = sb("n1", [SL, G, D])
        y0 = sb("y0", [SL, G, D])
        n1_pb = sb("n1_pb", [SL, G, D])
        h_keep = sb("h_keep", [SL, G, D])
        x2 = sb("x2", [SL, G, D])
        r_out = sb("r_out", [SL, G, D])
        rows = sb("rows", [SL, TOPK, G, ROW])
        lns = [{"stats": sb(f"ln{k}_stats", [SL, G, 6]), "mv": sb(f"ln{k}_mv", [SL, G, 2]),
                "var": sb(f"ln{k}_var", [SL, G]), "rstd": sb(f"ln{k}_rstd", [SL, G])} for k in range(4)]
        nT = sb("nT", [HALF + 1, 2, GT])
        yT = sb("yT", [HALF, 2, GT])
        h2T = sb("h2T", [HALF, 2, GT])
        qT = sb("qT", [128, PAIRS, GT])
        kbd = sb("kbd", [128, PAIRS, G, 2, SL])
        v1 = sb("v1", [SL, G, HEADS, DH1 + 1])
        q2T = sb("q2T", [128, QUADS, GT])
        k2bd = sb("k2bd", [128, QUADS, G, 4, SL])
        v2 = sb("v2", [SL, G, HEADS, DH2 + 1])
        score = sb("score", [SL, 4, UH, SL])
        smax = sb("smax", [SL, 4, UH])
        eT = sb("eT", [SL, 2, UH * SL])
        zinv = sb("zinv", [SL, 2, UH])
        z1 = sb("z1", [SL, 2, HEADS * DH1])
        z2 = sb("z2", [SL, 2, D])
        z1T = sb("z1T", [128, PAIRS, SL])
        z2T = sb("z2T", [HALF, 2, SL])
        rt = {n: sb(f"rt_{n}", [SL, G, E]) for n in ("logit", "eq", "mark", "pick1", "rest", "pick2", "sel", "before", "pos", "at")}
        rc = {n: sb(f"rc_{n}", [SL, G]) for n in ("m1", "i1", "m2", "i2", "gap", "ex", "den", "w1", "w2")}
        posf = sb("posf", [SL, TOPK, G])
        posi = sb("posi", [SL, TOPK, G], I32)
        runsum = sb("runsum", [SL, E])
        tb = {n: sb(f"tb_{n}", [1, E]) for n in ("x", "up", "nt", "end", "jump", "one")}
        tt_ = {n: sb(f"tt_{n}", [1, NTILE]) for n in ("t", "e", "s", "row", "ec")}
        past = sb("past", [1, NTILE, E])
        jumps = sb("jumps", [1, NTILE, E])
        attn_scope.close()

        moe_scope = ctx.enter_context(ExitStack())
        scope[0] = moe_scope
        w1 = sb("w1", [HALF + 1, E, 2, FF])
        w2 = sb("w2", [128, E, FF // 128, D])
        b2_rows = sb("b2_rows", [128, E, D])
        xt = sb("xt", [128, 4, ROW])
        xT = sb("xT", [HALF + 1, 2, 2, 128])
        hid = sb("hid", [128, 2, FF])
        hidT = sb("hidT", [128, 2, FF])
        y_raw = sb("y_raw", [128, 2, D])
        y_row = sb("y_row", [128, 2, D])
        last_r, last_ya = sb("last_r", [LP, NP_, CJ, D]), sb("last_ya", [LP, NP_, CJ, D])
        last_yb = sb("last_yb", [LP, 2, CJ, D])
        moe_scope.close()
        s = {n: sem(n) for n in """vco_loaded tokens_loaded sine_rows_loaded text_w_loaded img_loaded img_w_loaded
            order_chain order_stored order_loaded tok_staged tokT_done tok_ready ids_ready masks_ready arg_chain arg_ready sines_ready
            f1_cols_ready gathered_first gathered_rest ident_ready pool_chain pool_consts attn_pool_consts
            patchT_done patchT_out img_done img_added img_ready img_stored
            f1_ready f1T_done f1T_ready merge_done blend_half merged sines_copied f2T_done f2T_ready feat_done gelu_done seg_chain text_ready
            text_stored0 text_stored1 attn_w_loaded attn_vec_ready attn_zeroed w2_zeroed
            h_loaded res_ready keep_ready n1pb_ready
            fill_done fill_free0 fill_free1 score_done score_out smax_done shifted exp_done et_done et_out pv_done zinv_done z_out
            r_ready r_stored route gap_ready ex_ready pos_ready rows_copied scattered runsum_ready counts_done tables
            tables_ready tails_stored spare_stored attn_end expert_loaded moe_ones
            xt_loaded0 xt_loaded1 xt_loaded2 xt_loaded3 xT_done xT_ready up_done0 up_done1 hid_ready0 hid_ready1 hidT_done hidT_ready0 hidT_ready1
            down_done y_biased y_ready y_stored0 y_stored1
            r_loaded0 r_loaded1 r_loaded2 r_loaded3 ya_loaded0 ya_loaded1 ya_loaded2 ya_loaded3 yb_loaded0 yb_loaded1
            last_chain last_out out_stored apart""".split()}
        for k in range(4):
            for n in ("stats", "mv", "var", "rstd", "norm"):
                s[f"ln{k}_{n}"] = sem(f"ln{k}_{n}")

        g_bank, s_bank, t_bank, z_bank = banks[0:2], banks[2:4], banks[4:6], banks[6:8]


        def patch_source(k):
            return t["x"][8 * k:8 * k + 8].rearrange("b (ph i) (pw j) c -> (b ph) pw i (j c)", i=PATCH, j=PATCH)

        def text_loads():
            pairs = [(w_img[:], t["L0_tok_W"].rearrange("(c p) d -> p c d", p=128)),
                     (tok_b[:], t["L0_tok_b"].unsqueeze(0).broadcast_to([128, D])),
                     (w_merge[:, 0, :], t["L0_txt_merge_w"][0:C1, :]),
                     (w_merge[0:C1 - 1, 1, :], t["L0_txt_merge_w"][C1:D + 1, :]),
                     (w_merge[C1 - 1:C1, 1, :], t["L0_txt_merge_b"].unsqueeze(0)),
                     (w_feat[:, 0, :], t["L0_txt_proj_w"][0:C2, :]),
                     (w_feat[0:C2 - 2, 1, :], t["L0_txt_proj_w"][C2:, :]),
                     (w_feat[C2 - 2:C2 - 1, 1, :], t["L0_txt_proj_b"].unsqueeze(0)),
                     (w_feat[C2 - 1:C2, 1, :], t["L0_txt_proj_b"].unsqueeze(0)),
                     (g2col[:], t["L0_ffn_ln2_g"].rearrange("(c p) -> p c", p=HALF)),
                     (b2col[:], t["L0_ffn_ln2_b"].rearrange("(c p) -> p c", p=HALF))]
            pairs += [(seg_rows[:, k, :], t["L0_txt_segment_emb"][k:k + 1, :].broadcast_to([TT, D])) for k in range(N_SEG)]
            pairs += [(img_add[k * N_PATCH:(k + 1) * N_PATCH, :], t["L0_tok_pos_emb"]) for k in range(128 // N_PATCH)]
            return pairs

        def attn_loads():
            pairs = []
            for c in range(2):
                rows_c = slice(c * HALF, (c + 1) * HALF)
                for to, name in ((wq, "L0_attn_W_Q"), (wk_, "L0_attn_W_K"), (wv, "L0_attn_W_V")):
                    pairs.append((to[0:HALF, c, :].rearrange("p (h e) -> p h e", h=HEADS), t[name][:, rows_c, :].rearrange("h d e -> d h e")))
                pairs += [(wv2[:, c, :], t["L0_ffn_qkv_w"][rows_c, 2 * D:]), (wp2[:, c, :], t["L0_ffn_proj_w"][rows_c, :]),
                          (wgate[:, c, :], t["L0_ffn_gate_w"][rows_c, :])]
            pairs += [(wv[HALF:HALF + 1, 1, :], t["L0_attn_b_V"].rearrange("h e -> (h e)").unsqueeze(0)),
                      (wo[:], t["L0_attn_W_O"].rearrange("h e d -> (h e) d").rearrange("(c p) d -> p c d", p=128)),
                      (bq[:], t["L0_attn_b_Q"].rearrange("h e -> (h e)").rearrange("(c p) -> p c", p=128)),
                      (bk[:], t["L0_attn_b_K"].rearrange("h e -> (h e)").rearrange("(c p) -> p c", p=128)),
                      (g1col[:], t["L0_ffn_ln1_g"].rearrange("(c p) -> p c", p=HALF)),
                      (b1col[:], t["L0_ffn_ln1_b"].rearrange("(c p) -> p c", p=HALF)),
                      (bo_row[:], t["L0_attn_b_O"].unsqueeze(0).broadcast_to([SL, D])),
                      (pb_row[:], t["L0_ffn_proj_b"].unsqueeze(0).broadcast_to([SL, D])),
                      (gb_row[:], t["L0_ffn_gate_b"].unsqueeze(0).broadcast_to([SL, E]))]
            for c in range(2):
                for k, to in enumerate((wq2, wk2)):
                    pairs.append((to[:, c, :].rearrange("p (h e) -> p h e", h=HEADS)[:, :, 0:DH2],
                                  t["L0_ffn_qkv_w"][c * HALF:(c + 1) * HALF, k * D:(k + 1) * D].rearrange("p (h e) -> p h e", h=HEADS)))
            return pairs

        def text_steps(eng, step):
            for k in range(6):
                step(k // 2, k % 2)
            with eng.Fori(3, NT // 2) as i:
                for p in range(2):
                    step(i, p)
            for k in range(NT, NT + 6):
                step(k // 2, k % 2)

        def tile_at(i, p, lag):
            if isinstance(i, int) and not 0 <= 2 * i + p - lag < NT:
                return None
            return i * 2 + (p - lag), (p - lag) % 2

        def attn_bodies(eng, body):
            for n in range(FIRST_FULL + 1):
                body(Body(n, n))
            with eng.Fori(FIRST_FULL + 1, LAST_FULL + 1) as i:
                body(Body(FIRST_FULL, i))
            for n in range(LAST_FULL + 1, NG + 2):
                body(Body(n, n))

        def expert_steps(eng, step):
            for p in range(4):
                step(0, p)
            with eng.Fori(1, NTILE // 4) as i:
                for p in range(4):
                    step(i, p)
            for k in range(NTILE // 4 * 4, NTILE + 2):
                step(k // 4, k % 4)

        def xtile_at(i, p, lag):
            if isinstance(i, int) and not 0 <= 4 * i + p - lag < NTILE:
                return None
            return i * 4 + (p - lag), (p - lag) % 4

        def half_count(i, p, lag):
            return i * 2 + (p - lag) // 2

        def evacuated(eng, b, *label):
            bank, _, before = b.fill(*label)
            eng.wait_ge(s[f"fill_free{bank}"], before + 1)

        def filled(eng, b, *label):
            bank, before, _ = b.fill(*label)
            eng.wait_ge(s["fill_done"], before + 1)
            return g_bank[bank], s[f"fill_free{bank}"]

        def wait_apart(eng, sem, value):
            at_least(eng, sem, value)
            if not isinstance(value, int):
                eng.sem_inc(s["apart"], 1)

        block = ctx.enter_context(nc.Block())

        @block.sync
        def _(sp):
            def flat_tokens(a):
                return a.rearrange("b s -> (b s)").rearrange("(n k) -> n k", k=TT)

            sp.dma_start(vco_i[:], t["itok_BS_0_2047"]).then_inc(s["vco_loaded"], 16)
            for slot, name in enumerate(("x_txt", "itok_BS_1_36498", "itok_BS_0_99", "mask_BS_i2_0")):
                sp.dma_start(tok_i[:, slot, :], flat_tokens(t[name])).then_inc(s["tokens_loaded"], 16)
            sp.dma_start(tok_f[:, 4, :], flat_tokens(t["fside_BS_concept_values"])).then_inc(s["tokens_loaded"], 16)
            sp.dma_start(tok_f[:, 5, :], flat_tokens(t["mask_BS_f1_0"])).then_inc(s["tokens_loaded"], 16)
            for k in range(2):
                sp.dma_start(frow[:, k, :], t["L0_txt_w_age"].broadcast_to([TT, T_EMB])).then_inc(s["sine_rows_loaded"], 16)
                sp.dma_start(prow[:, k, :], t["L0_txt_phi_age"].broadcast_to([TT, T_EMB])).then_inc(s["sine_rows_loaded"], 16)
            sp.dma_start(frow[:, 2, :], t["pos_freq"].broadcast_to([TT, T_EMB])).then_inc(s["sine_rows_loaded"], 16)
            sp.dma_start(qrow[:].rearrange("p a b -> p (a b)"), t["quarter"].broadcast_to([TT, 3 * T_EMB])).then_inc(s["sine_rows_loaded"], 16)
            sp.wait_ge(s["order_chain"], 4)
            sp.dma_start(ord_d, order[:]).then_inc(s["order_stored"], 16)
            sp.wait_ge(s["order_stored"], 16)
            sp.dma_start(tok_f[:, 3, :], flat_tokens(ord_d)).then_inc(s["order_loaded"], 16)

            for k in range(4):
                sp.wait_ge(s["img_ready"], k + 1)
                sp.dma_start(img_d[k * 128:(k + 1) * 128, :], img_h[:, k, :]).then_inc(s["img_stored"], 16)

            def store_text(i, p):
                if (at := tile_at(i, p, 5)) is not None:
                    tile, par = at
                    sp.wait_ge(s["text_ready"], tile + 1)
                    sp.dma_start(txt_d[bass.ds(tile * TT, TT), :], txt_h[:, par, :]).then_inc(s[f"text_stored{par}"], 16)
            text_steps(sp, store_text)

            sp.wait_ge(s["img_stored"], 64)
            for par in range(2):
                sp.wait_ge(s[f"text_stored{par}"], 16 * (NT // 2))
            for k, (to, of) in enumerate(attn_loads()):
                if k == len(attn_loads()) - 4:
                    sp.wait_ge(s["w2_zeroed"], 2)
                sp.dma_start(to, of, allow_slow_non_contiguous=True).then_inc(s["attn_w_loaded"], 16)

            def load_h(g):
                at_least(sp, s["ln0_norm"], g * G)
                at_least(sp, s["res_ready"], g)
                sp.dma_start(h_in[0:N_PATCH, :, :], img_d.rearrange("(b s) d -> s b d", s=N_PATCH)[:, bass.ds(g * G, G), :]).then_inc(s["h_loaded"], 16)
                sp.dma_start(h_in[N_PATCH:S, :, :], txt_d.rearrange("(b s) d -> s b d", s=S_TXT)[:, bass.ds(g * G, G), :]).then_inc(s["h_loaded"], 16)
            sp.wait_ge(s["attn_zeroed"], 1)
            load_h(0)

            def body(b):
                if b.has_n:
                    load_h(b.i + 1)
                if b.has_b:
                    g = b.i - 1
                    sp.wait_ge(s["r_ready"], (g + 1) * G)
                    sp.dma_start(r_d.rearrange("(b s) d -> s b d", s=S)[:, bass.ds(g * G, G), :], r_out[0:S, :, :]).then_inc(s["r_stored"], 16)
            attn_bodies(sp, body)

            sp.wait_ge(s["attn_end"], 1)
            sp.wait_ge(s["r_stored"], 16 * NG)
            sp.wait_ge(s["scattered"], 16 * TOPK * B)
            for e in range(E):
                sp.dma_start(w1[0:HALF, e, :, :], t["L0_ffn_w1"][e].rearrange("(c p) f -> p c f", p=HALF)).then_inc(s["expert_loaded"], 16)
                sp.dma_start(w1[HALF:HALF + 1, e, 1, :], t["L0_ffn_b1"][e:e + 1, :]).then_inc(s["expert_loaded"], 16)
                sp.dma_start(w2[:, e, :, :], t["L0_ffn_w2"][e].rearrange("(c p) d -> p c d", p=128)).then_inc(s["expert_loaded"], 16)
                sp.dma_start(b2_rows[:, e, :], t["L0_ffn_b2"][e:e + 1, :].broadcast_to([128, D])).then_inc(s["expert_loaded"], 16)
            def pieces(a, k):
                return a.rearrange("(p j) d -> p j d", p=LP)[:, k * CJ:(k + 1) * CJ, :]
            for k in range(NP_):
                sp.dma_start(last_r[:, k], pieces(r_d, k)).then_inc(s[f"r_loaded{k}"], 16)
            sp.wait_ge(s["tails_stored"], 16 * E)
            sp.wait_ge(s["spare_stored"], 16)

            def load_tile(tile, place):
                row = sp.value_load(tile_row[0:1, bass.ds(tile, 1)], min_val=0, max_val=XS_ROWS - 128)
                sp.dma_start(xt[:, place, :], xs_d[bass.ds(row, 128), :]).then_inc(s[f"xt_loaded{place}"], 16)
            for k in range(2):
                load_tile(k, k)

            def load_ahead(i, p):
                if (at := xtile_at(i, p, -2)) is not None:
                    at_least(sp, s[f"y_stored{p % 2}"], half_count(i, p, 0) * 16)
                    load_tile(*at)
            expert_steps(sp, load_ahead)

            sp.wait_ge(s["y_stored0"], 16 * (NTILE // 2))
            sp.wait_ge(s["y_stored1"], 16 * (NTILE // 2))
            for k in range(NP_):
                sp.dma_start(last_ya[:, k], pieces(y_d[0:B * S, :], k)).then_inc(s[f"ya_loaded{k}"], 16)
                at_least(sp, s["last_out"], k - 1)
                sp.dma_start(last_yb[:, k % 2], pieces(y_d[B * S:SLOTS, :], k)).then_inc(s[f"yb_loaded{k % 2}"], 16)
            for k in range(NP_):
                sp.wait_ge(s["last_out"], k + 1)
                sp.dma_start(pieces(out.rearrange("b s d -> (b s) d"), k), last_ya[:, k]).then_inc(s["out_stored"], 16)
            sp.wait_ge(s["out_stored"], 16 * NP_)

        @block.gpsimd
        def _(pool):
            links = [0]

            def link(ins):
                links[0] += 1
                ins.then_inc(s["pool_chain"], 1)
                pool.wait_ge(s["pool_chain"], links[0])

            link(pool.memset(ident[:], 0.0))
            pool.affine_select(out=ident[:], in_=ident[:], compare_op=ALU.not_equal, fill=1.0, base=0,
                               pattern=[[-1, 128]], channel_multiplier=1).then_inc(s["ident_ready"], 1)
            pool.memset(f2[:, :, F2W - 2:F2W - 1], 1.0).then_inc(s["pool_consts"], 1)
            pool.memset(f2[:, :, F2W - 1:F2W], 0.0).then_inc(s["pool_consts"], 1)
            pool.memset(f1all[:, :, F1W - 1:F1W], 1.0).then_inc(s["pool_consts"], 1)
            link(pool.memset(zero_rows[:], 0.0))
            link(pool.iota(zero_rows[:, :, D:D + 1].bitcast(I32), pattern=[[128, E + SPARE], [0, 1]], base=SLOTS, channel_multiplier=1))
            pool.dma_start(xs_d[E * REGION:XS_ROWS, :].rearrange("(j p) w -> p j w", p=128), zero_rows[:, E:, :]).then_inc(s["spare_stored"], 16)
            link(pool.memset(ones_first[:], 1.0))
            link(pool.affine_select(out=ones_first[:], in_=ones_first[:], compare_op=ALU.is_ge, fill=0.0, base=S - 1,
                                    pattern=[[0, 128]], channel_multiplier=-1))
            link(pool.iota(part_id[:], pattern=[[0, 1]], base=0, channel_multiplier=1, allow_small_or_imprecise_dtypes=True))
            link(pool.iota(base_row[:], pattern=[[REGION, E]], base=0, channel_multiplier=0, allow_small_or_imprecise_dtypes=True))
            pool.wait_ge(s["ids_ready"], 1)
            for tile in range(NT):
                name = "gathered_first" if tile < 6 else "gathered_rest"
                pool.indirect_dma_start(out=f1all[:, tile, 0:D], out_offset=None, in_=t["L0_txt_concept_emb"],
                                        in_offset=bass.IndirectOffsetOnAxis(ap=ids[:, tile:tile + 1], axis=0)).then_inc(s[name], 16)

            for par in range(2):
                pool.wait_ge(s[f"text_stored{par}"], 16 * (NT // 2))
            pool.wait_ge(s["img_stored"], 64)
            pool.memset(wq2[:], 0.0).then_inc(s["w2_zeroed"], 1)
            pool.memset(wk2[:], 0.0).then_inc(s["w2_zeroed"], 1)
            link(pool.memset(h_in[:], 0.0))
            pool.memset(kbd[:], 0.0).then_inc(s["attn_zeroed"], 1)
            pool.memset(k2bd[:], 0.0).then_inc(s["attn_zeroed"], 1)
            link(pool.memset(causal[:], 0.0))
            link(pool.affine_select(out=causal[:], in_=causal[:], compare_op=ALU.is_ge, fill=NEG, base=0,
                                    pattern=[[0, UH], [-1, SL]], channel_multiplier=1))
            link(pool.memset(padded[:], 0.0))
            link(pool.affine_select(out=padded[:], in_=padded[:], compare_op=ALU.is_ge, fill=NEG, base=S - 1,
                                    pattern=[[0, UH], [-1, SL]], channel_multiplier=0))
            link(pool.memset(earlier[:], 1.0))
            link(pool.affine_select(out=earlier[:], in_=earlier[:], compare_op=ALU.is_gt, fill=0.0, base=0,
                                    pattern=[[1, SL]], channel_multiplier=-1))
            link(pool.affine_select(out=earlier[:], in_=earlier[:], compare_op=ALU.is_ge, fill=0.0, base=S - 1,
                                    pattern=[[0, SL]], channel_multiplier=-1))
            link(pool.memset(neg_half[:], -0.5))
            link(pool.iota(from_end[:], pattern=[[-1, E]], base=E, channel_multiplier=0, allow_small_or_imprecise_dtypes=True))
            link(pool.iota(dest0[:], pattern=[[B * S, TOPK], [S, G]], base=0, channel_multiplier=1, allow_small_or_imprecise_dtypes=True))
            link(pool.iota(tt_["t"][:], pattern=[[1, NTILE]], base=0, channel_multiplier=0, allow_small_or_imprecise_dtypes=True))
            link(pool.memset(runsum[:], 0.0))
            link(pool.memset(nT[HALF:HALF + 1, 1, :], 1.0))
            link(pool.memset(v1[:, :, :, DH1:DH1 + 1], 1.0))
            pool.memset(v2[:, :, :, DH2:DH2 + 1], 1.0).then_inc(s["attn_pool_consts"], 1)

            def power(k, g):
                pool.wait_ge(s[f"ln{k}_var"], g + 1)
                pool.tensor_tensor(lns[k]["rstd"][:], lns[k]["var"][:], neg_half[:], ALU.pow).then_inc(s[f"ln{k}_rstd"], 1)

            def next_residual(g):
                at_least(pool, s["ln1_norm"], g * G)
                at_least(pool, s["keep_ready"], g)
                pool.wait_ge(s["h_loaded"], (g + 1) * 32)
                pool.tensor_tensor(h_res[:], h_in[:], bo_row[:].unsqueeze(1).broadcast_to([SL, G, D]), ALU.add).then_inc(s["res_ready"], 1)

            pool.wait_ge(s["attn_w_loaded"], 16 * len(attn_loads()))
            power(0, 0)
            next_residual(0)

            def shift(b, k):
                if 0 <= k < len(b.units):
                    at = k % 4
                    pool.wait_ge(s["smax_done"], b.units_before + k + 1)
                    pool.tensor_tensor(score[:, at], score[:, at], smax[:, at].unsqueeze(2).broadcast_to([SL, UH, SL]),
                                       ALU.subtract).then_inc(s["shifted"], 1)

            def scatter(b, k):
                if b.has_c and k < TOPK * G:
                    g, choice = k // TOPK, k % TOPK
                    if k == 0:
                        pool.wait_ge(s["pos_ready"], b.i - 1)
                        wait_apart(pool, s["rows_copied"], b.i - 1)
                    pool.indirect_dma_start(out=xs_d, out_offset=bass.IndirectOffsetOnAxis(ap=posi[0:S, choice, g:g + 1], axis=0),
                                            in_=rows[0:S, choice, g, :], in_offset=None).then_inc(s["scattered"], 16)

            def residual_row(b, step):
                for label in posts_of(b.n, step):
                    if label[0] == "pj":
                        g = label[1]
                        evacuated(pool, b, "pj", g)
                        if g == 0:
                            at_least(pool, s["r_stored"], (b.i - 1) * 16)
                        pool.tensor_tensor(r_out[:, g], x2[:, g], h_keep[:, g], ALU.add).then_inc(s["r_ready"], 1)

            def body(b):
                if b.has_n:
                    power(0, b.i + 1)
                for step in range(b.steps + 1):
                    shift(b, step)
                    scatter(b, step)
                    residual_row(b, step - 1)
                if b.has_a:
                    power(1, b.i)
                if b.has_b:
                    power(3, b.i - 1)
                if b.has_a:
                    evacuated(pool, b, "wo", G - 1)
                    wait_apart(pool, s["r_ready"], b.i * G)
                    pool.tensor_copy(h_keep[:], h_res[:]).then_inc(s["keep_ready"], 1)
                    power(2, b.i)
                    pool.tensor_tensor(n1_pb[:], n1[:], pb_row[:].unsqueeze(1).broadcast_to([SL, G, D]), ALU.add).then_inc(s["n1pb_ready"], 1)
                if b.has_b:
                    pool.wait_ge(s["ln3_norm"], b.i * G)
                    wait_apart(pool, s["scattered"], (b.i - 1) * (16 * TOPK * G))
                    pool.tensor_copy(rows[:, 1, :, 0:D], rows[:, 0, :, 0:D]).then_inc(s["rows_copied"], 1)
                if b.has_n:
                    next_residual(b.i + 1)
            attn_bodies(pool, body)

            pool.wait_ge(s["tables_ready"], 1)
            for e in range(E):
                pool.indirect_dma_start(out=xs_d, out_offset=bass.IndirectOffsetOnAxis(ap=tail_at[:, e:e + 1], axis=0),
                                        in_=zero_rows[:, e, :], in_offset=None).then_inc(s["tails_stored"], 16)

            def scatter_rows(i, p):
                if (at := xtile_at(i, p, 1)) is not None:
                    tile, place = at
                    wait_apart(pool, s["y_ready"], tile + 1)
                    pool.indirect_dma_start(out=y_d, out_offset=bass.IndirectOffsetOnAxis(ap=xt[:, place, D:D + 1].bitcast(I32), axis=0),
                                            in_=y_row[:, place % 2, :], in_offset=None).then_inc(s[f"y_stored{place % 2}"], 16)
            expert_steps(pool, scatter_rows)

        @block.scalar
        def _(act):
            for k in range(4):
                for w in range(IMG // PATCH):
                    act.dma_start(xpatch[w::IMG // PATCH, k, :].rearrange("q (i c) -> q i c", i=PATCH), patch_source(k)[:, w]).then_inc(s["img_loaded"], 16)
            for to, of in text_loads():
                act.dma_start(to, of, allow_slow_non_contiguous=True).then_inc(s["text_w_loaded"], 16)

            for k in range(4):
                for h in range(2):
                    act.wait_ge(s["patchT_done"], 2 * k + h + 1)
                    at_least(act, s["img_done"], k - 1)
                    act.copy(patchT[:, k % 2, 3 * h:3 * h + 3, :].rearrange("p a b -> p (a b)"), t_bank[h][:, 0:384]).then_inc(s["patchT_out"], 1)

            act.wait_ge(s["arg_ready"], 1)
            act.activation(turns[:], arg[:], ACT.Sin).then_inc(s["sines_ready"], 1)
            act.wait_ge(s["sines_ready"], 1)

            def text(i, p):
                if (at := tile_at(i, p, 4)) is not None:
                    tile, par = at
                    act.wait_ge(s["feat_done"], tile + 1)
                    at_least(act, s[f"text_stored{par}"], 16 * (i + (p - 4 - par) // 2))
                    act.activation(txt_h[:, par, :], banks[6 + par][0:TT, 0:D], ACT.Gelu).then_inc(s["gelu_done"], 1)
                if (at := tile_at(i, p, 0)) is not None:
                    tile, par = at
                    if isinstance(i, int):
                        act.wait_ge(s["gathered_first"], 16 * 6)
                        act.wait_ge(s["f1_cols_ready"], 1)
                        act.wait_ge(s["pool_consts"], 3)
                    else:
                        act.wait_ge(s["gathered_rest"], 16 * (NT - 6))
                    at_least(act, s["f1T_done"], tile - 1)
                    at_least(act, s["merged"], tile - 1)
                    act.copy(f1[:, par, :], f1all[:, bass.ds(tile, 1), :].rearrange("p a b -> p (a b)")).then_inc(s["f1_ready"], 1)
                    at_least(act, s["f2T_done"], tile - 1)
                    act.copy(f2[:, par, D:F2W - 2], turns[:, bass.ds(tile, 1), :].rearrange("p a b -> p (a b)")).then_inc(s["sines_copied"], 1)
            text_steps(act, text)

            def copy_nT(bank, pair):
                return act.copy(nT[0:HALF, :, pair * 2 * SL:(pair + 1) * 2 * SL].rearrange("p c (g t) -> p c g t", g=2),
                                bank[0:HALF, 0:4 * SL].rearrange("p (g c t) -> p c g t", g=2, c=2))
            act.wait_ge(s["attn_pool_consts"], 1)
            act.wait_ge(s["attn_vec_ready"], 1)
            for pair in range(2):
                act.wait_ge(s["fill_done"], pair + 1)
                copy_nT(g_bank[pair], pair).then_inc(s[f"fill_free{pair}"], 1)

            def body(b):
                if b.has_a:
                    for k in range(PAIRS):
                        bank, free = filled(act, b, "q", k)
                        act.activation(qT[:, k, :], bank[:, 0:GT], ACT.Identity, bias=bq[:, k:k + 1], scale=DH1 ** -0.5).then_inc(free, 1)
                        bank, free = filled(act, b, "k", k)
                        for j in range(2):
                            ins = act.activation(kbd[64 * j:64 * j + 64, k, :, j, :], bank[64 * j:64 * j + 64, 0:GT].rearrange("p (g t) -> p g t", g=G),
                                                 ACT.Identity, bias=bk[64 * j:64 * j + 64, k:k + 1])
                        ins.then_inc(free, 1)
                    for g in range(G):
                        for h in range(2):
                            bank, free = filled(act, b, "v", g, h)
                            act.copy(v1[:, g, 6 * h:6 * h + 6, 0:DH1], bank[0:SL, 0:6 * DH1].rearrange("p (h e) -> p h e", h=6)).then_inc(free, 1)
                if b.has_b:
                    for k in range(QUADS):
                        bank, free = filled(act, b, "q2", k)
                        act.mul(q2T[:, k, :], bank[:, 0:GT], DH2 ** -0.5).then_inc(free, 1)
                        bank, free = filled(act, b, "k2", k)
                        for j in range(4):
                            ins = act.copy(k2bd[32 * j:32 * j + 32, k, :, j, :], bank[32 * j:32 * j + 32, 0:GT].rearrange("p (g t) -> p g t", g=G))
                        ins.then_inc(free, 1)
                    for pair in range(2):
                        bank, free = filled(act, b, "v2", pair)
                        act.copy(v2[:, 2 * pair:2 * pair + 2, :, 0:DH2].rearrange("p g h e -> p (g h) e"),
                                 bank[0:SL, 0:2 * D].rearrange("p (h e) -> p h e", e=DH2)).then_inc(free, 1)
                if b.has_c:
                    act.wait_ge(s["gap_ready"], b.i - 1)
                    act.activation(rc["ex"][:], rc["gap"][:], ACT.Exp).then_inc(s["ex_ready"], 1)
                for step in range(b.steps):
                    k = step - LAG_T
                    if 0 <= k < len(b.units):
                        act.wait_ge(s["et_done"], b.units_before + k + 1)
                        at_least(act, s["pv_done"], b.units_before + k - 1)
                        act.copy(eT[:, k % 2, :], t_bank[k % 2][0:SL, 0:UH * SL]).then_inc(s["et_out"], 1)
                    k = step - LAG_T + 1
                    if 0 <= k < len(b.units):
                        act.wait_ge(s["shifted"], b.units_before + k + 1)
                        act.activation(score[:, k % 4], score[:, k % 4], ACT.Exp).then_inc(s["exp_done"], 1)
                    for label in posts_of(b.n, step):
                        if label[0] == "zT":
                            bank, free = filled(act, b, *label)
                            act.copy(z1T[:, 3 * label[2]:3 * label[2] + 3, :].rearrange("p a b -> p (a b)"), bank[:, 0:3 * SL]).then_inc(free, 1)
                        if label[0] == "z2T":
                            bank, free = filled(act, b, *label)
                            act.copy(z2T[:].rearrange("p a b -> p (a b)"), bank[0:HALF, 0:2 * SL]).then_inc(free, 1)
                if b.has_n:
                    for pair in range(2):
                        bank, free = filled(act, b, "nT", pair)
                        copy_nT(bank, pair).then_inc(free, 1)
            attn_bodies(act, body)

            act.wait_ge(s["attn_end"], 1)
            act.wait_ge(s["scattered"], 16 * TOPK * B)
            act.wait_ge(s["r_stored"], 16 * NG)

            def expert(i, p):
                tile = i * 4 + p
                if xtile_at(i, p, 0) is not None:
                    act.wait_ge(s["up_done0"], tile + 1)
                    at_least(act, s["hidT_done"], tile - 1)
                    act.activation(hid[:, p % 2, 0:FF // 2], banks[2][:, 0:FF // 2], ACT.Gelu).then_inc(s["hid_ready0"], 1)
                if xtile_at(i, p, 1) is not None:
                    act.wait_ge(s["hidT_done"], tile)
                    at_least(act, s["down_done"], tile - 2)
                    act.copy(hidT[:, (p - 1) % 2, 0:FF // 2], banks[4][:, 0:FF // 2]).then_inc(s["hidT_ready0"], 1)
                if xtile_at(i, p, 0) is not None:
                    act.wait_ge(s["up_done1"], tile + 1)
                    act.activation(hid[:, p % 2, FF // 2:], banks[3][:, 0:FF // 2], ACT.Gelu).then_inc(s["hid_ready1"], 1)
            expert_steps(act, expert)

        @block.vector
        def _(dve):
            dve.wait_ge(s["vco_loaded"], 16)
            dve.tensor_copy(vco[:], vco_i[:]).then_inc(s["order_chain"], 1)
            dve.wait_ge(s["order_chain"], 1)
            dve.tensor_reduce(vmin[:], vco[:], AX.X, ALU.min).then_inc(s["order_chain"], 1)
            dve.wait_ge(s["order_chain"], 2)
            dve.tensor_scalar(order[:], vco[:], vmin[:, 0:1], 0.0, ALU.subtract, ALU.max).then_inc(s["order_chain"], 1)
            dve.wait_ge(s["order_chain"], 3)
            dve.tensor_scalar(order[:], order[:], float(MAX_POS - 1), None, ALU.min).then_inc(s["order_chain"], 1)
            dve.wait_ge(s["tokens_loaded"], 16 * 6)
            dve.tensor_copy(tok_f[:, 0:3, :], tok_i[:, 0:3, :]).then_inc(s["tok_staged"], 1)
            dve.tensor_copy(tok_f[:, 6, :], tok_i[:, 3, :]).then_inc(s["tok_staged"], 1)
            dve.wait_ge(s["tokT_done"], 1)
            dve.tensor_copy(tok[:].rearrange("p a b -> p (a b)"), banks[0][0:TT, 0:7 * NT]).then_inc(s["tok_ready"], 1)
            dve.wait_ge(s["tok_ready"], 1)
            dve.tensor_copy(ids[:], tok[:, 0, :]).then_inc(s["ids_ready"], 1)
            dve.tensor_copy(f1all[:, :, D:D + 1].rearrange("p a b -> p (a b)"), tok[:, 4, :]).then_inc(s["f1_cols_ready"], 1)
            dve.tensor_scalar(keep[:, :, 0], tok[:, 5, :], 0.0, None, ALU.not_equal).then_inc(s["masks_ready"], 1)
            dve.tensor_scalar(keep[:, :, 1], tok[:, 5, :], 0.0, None, ALU.is_equal).then_inc(s["masks_ready"], 1)
            for k in range(N_SEG):
                dve.tensor_scalar(segm[:, k, :], tok[:, 6, :], float(k), None, ALU.is_equal).then_inc(s["masks_ready"], 1)

            dve.wait_ge(s["sine_rows_loaded"], 16 * 6)
            chain = [0]

            def link(ins):
                chain[0] += 1
                ins.then_inc(s["arg_chain"], 1)
                dve.wait_ge(s["arg_chain"], chain[0])
            wide = [TT, NT, 3, T_EMB]
            a4 = arg[:].rearrange("p n (k c) -> p n k c", k=3)
            a3, u3 = arg[:], turns[:]
            link(dve.memset(prow[:, 2, :], 0.0))
            link(dve.tensor_tensor(a4, tok[:, 1:4, :].rearrange("p k n -> p n k").unsqueeze(3).broadcast_to(wide), frow[:].unsqueeze(1).broadcast_to(wide), ALU.mult))
            rows3 = [TT, NT, 3 * T_EMB]
            phases = prow[:].rearrange("p k c -> p (k c)").unsqueeze(1).broadcast_to(rows3)
            quarters = qrow[:].rearrange("p k c -> p (k c)").unsqueeze(1).broadcast_to(rows3)
            link(dve.tensor_tensor(a3, a3, phases, ALU.add))
            link(dve.tensor_scalar(u3, a3, 1 / (2 * math.pi), None, ALU.mult))
            link(dve.scalar_tensor_tensor(u3, quarters, 0.25, u3, ALU.mult, ALU.add))
            link(dve.tensor_scalar(u3, u3, MAGIC, None, ALU.add))
            link(dve.tensor_scalar(u3, u3, -MAGIC, None, ALU.add))
            for part in (TP1, TP2, TP3):
                link(dve.scalar_tensor_tensor(a3, u3, -part, a3, ALU.mult, ALU.add))
            link(dve.scalar_tensor_tensor(a3, quarters, math.pi / 2, a3, ALU.mult, ALU.add))
            dve.tensor_scalar(a3, a3, 3.1415925, -3.1415925, ALU.min, ALU.max).then_inc(s["arg_ready"], 1)

            dve.wait_ge(s["text_w_loaded"], 16 * len(text_loads()))
            dve.tensor_tensor(img_add[:], img_add[:], tok_b[:], ALU.add).then_inc(s["img_added"], 1)
            dve.wait_ge(s["img_added"], 1)
            for k in range(4):
                dve.wait_ge(s["img_done"], k + 1)
                dve.tensor_tensor(img_h[:, k, :], banks[2 + k % 2][:, 0:D], img_add[:], ALU.add).then_inc(s["img_ready"], 1)

            def text(i, p):
                if (at := tile_at(i, p, 0)) is not None:
                    tile, par = at
                    dve.wait_ge(s["f1T_done"], tile + 1)
                    at_least(dve, s["merge_done"], tile - 1)
                    dve.tensor_copy(f1T[:, par].rearrange("p c t -> p (c t)"), banks[par][0:C1, 0:2 * TT]).then_inc(s["f1T_ready"], 1)
                if (at := tile_at(i, p, 1)) is not None:
                    tile, par = at
                    dve.wait_ge(s["merge_done"], tile + 1)
                    if isinstance(i, int):
                        dve.wait_ge(s["masks_ready"], 2 + N_SEG)
                    dve.tensor_scalar(blend[:, par, :], banks[2 + par][0:TT, 0:D], keep[:, bass.ds(tile, 1), 0], None, ALU.mult).then_inc(s["blend_half"], 1)
                    dve.wait_ge(s["blend_half"], tile + 1)
                    at_least(dve, s["f2T_done"], tile - 1)
                    dve.scalar_tensor_tensor(f2[:, par, 0:D], f1[:, par, 0:D], keep[:, bass.ds(tile, 1), 1], blend[:, par, :], ALU.mult, ALU.add).then_inc(s["merged"], 1)
                if (at := tile_at(i, p, 2)) is not None:
                    tile, par = at
                    dve.wait_ge(s["f2T_done"], tile + 1)
                    at_least(dve, s["feat_done"], tile - 1)
                    dve.tensor_copy(f2T[:, par].rearrange("p c t -> p (c t)"), banks[4 + par][0:C2, 0:2 * TT]).then_inc(s["f2T_ready"], 1)
                if (at := tile_at(i, p, 5)) is not None:
                    tile, par = at
                    dve.wait_ge(s["gelu_done"], tile + 1)
                    for k in range(N_SEG):
                        ins = dve.scalar_tensor_tensor(txt_h[:, par, :], seg_rows[:, k, :], segm[:, k, bass.ds(tile, 1)], txt_h[:, par, :], ALU.mult, ALU.add)
                        if k < N_SEG - 1:
                            ins.then_inc(s["seg_chain"], 1)
                            dve.wait_ge(s["seg_chain"], tile * (N_SEG - 1) + k + 1)
                        else:
                            ins.then_inc(s["text_ready"], 1)
            text_steps(dve, text)

            dve.wait_ge(s["attn_w_loaded"], 16 * len(attn_loads()))
            dve.tensor_scalar(bq[:], bq[:], DH1 ** -0.5, None, ALU.mult).then_inc(s["attn_vec_ready"], 1)
            dve.wait_ge(s["attn_zeroed"], 2)

            def stats_of(k, g, src):
                ln = lns[k]
                for j in range(G):
                    dve.bn_stats(ln["stats"][:, j], src[:, j]).then_inc(s[f"ln{k}_stats"], 1)
                wait_apart(dve, s[f"ln{k}_stats"], (g + 1) * G)
                for j in range(G):
                    dve.bn_aggr(ln["mv"][:, j], ln["stats"][:, j]).then_inc(s[f"ln{k}_mv"], 1)
                dve.wait_ge(s[f"ln{k}_mv"], (g + 1) * G)
                dve.tensor_scalar(ln["var"][:], ln["mv"][:, :, 1], EPS, None, ALU.add).then_inc(s[f"ln{k}_var"], 1)

            def normalise(k, g, dst, src):
                ln = lns[k]
                dve.wait_ge(s[f"ln{k}_rstd"], g + 1)
                for j in range(G):
                    dve.tensor_scalar(dst[:, j], src[:, j], ln["mv"][:, j, 0:1], ln["rstd"][:, j:j + 1], ALU.subtract, ALU.mult).then_inc(s[f"ln{k}_norm"], 1)

            dve.wait_ge(s["h_loaded"], 32)
            dve.wait_ge(s["attn_pool_consts"], 1)
            stats_of(0, 0, h_in)
            normalise(0, 0, n0, h_in)

            def affine_copy(bank, free, pair, dst, scale, shift):
                for c in range(2):
                    ins = dve.tensor_scalar(dst[:, c, pair * 2 * SL:(pair + 1) * 2 * SL].rearrange("p (g t) -> p g t", g=2),
                                            bank[0:HALF, 0:4 * SL].rearrange("p (g c t) -> p c g t", g=2, c=2)[:, c],
                                            scale[:, c:c + 1], shift[:, c:c + 1], ALU.mult, ALU.add)
                ins.then_inc(free, 1)

            wide3 = [SL, G, E]

            def bc(a):
                return a.unsqueeze(2).broadcast_to(wide3)

            def route(b):
                g, n = b.i - 2, [0]

                def link(ins):
                    n[0] += 1
                    ins.then_inc(s["route"], 1)
                    dve.wait_ge(s["route"], g * ROUTE + n[0])
                bank, free = filled(dve, b, "gate")
                ends = from_end[:].unsqueeze(1).broadcast_to(wide3)
                dve.tensor_tensor(rt["logit"][:], bank[0:SL, 0:G * E].rearrange("p (g e) -> p g e", g=G), gb_row[:].unsqueeze(1).broadcast_to(wide3), ALU.add).then_inc(free, 1)
                evacuated(dve, b, "gate")
                link(dve.tensor_reduce(rc["m1"][:], rt["logit"][:], AX.X, ALU.max))
                link(dve.tensor_tensor(rt["eq"][:], rt["logit"][:], bc(rc["m1"][:]), ALU.is_equal))
                link(dve.tensor_tensor(rt["mark"][:], rt["eq"][:], ends, ALU.mult))
                link(dve.tensor_reduce(rc["i1"][:], rt["mark"][:], AX.X, ALU.max))
                link(dve.tensor_tensor(rt["pick1"][:], bc(rc["i1"][:]), ends, ALU.is_equal))
                link(dve.scalar_tensor_tensor(rt["rest"][:], rt["pick1"][:], NEG, rt["logit"][:], ALU.mult, ALU.add))
                link(dve.tensor_reduce(rc["m2"][:], rt["rest"][:], AX.X, ALU.max))
                dve.tensor_tensor(rc["gap"][:], rc["m2"][:], rc["m1"][:], ALU.subtract).then_inc(s["gap_ready"], 1)
                link(dve.tensor_tensor(rt["eq"][:], rt["rest"][:], bc(rc["m2"][:]), ALU.is_equal))
                link(dve.tensor_tensor(rt["mark"][:], rt["eq"][:], ends, ALU.mult))
                link(dve.tensor_reduce(rc["i2"][:], rt["mark"][:], AX.X, ALU.max))
                link(dve.tensor_tensor(rt["pick2"][:], bc(rc["i2"][:]), ends, ALU.is_equal))
                link(dve.tensor_tensor(rt["sel"][:], rt["pick1"][:], rt["pick2"][:], ALU.add))
                link(dve.tensor_copy(rt["before"][:, 0], runsum[:]))
                for j in range(1, G):
                    link(dve.tensor_tensor(rt["before"][:, j], rt["before"][:, j - 1], rt["sel"][:, j - 1], ALU.add))
                link(dve.tensor_tensor(runsum[:], rt["before"][:, G - 1], rt["sel"][:, G - 1], ALU.add))
                dve.wait_ge(s["ex_ready"], g + 1)
                link(dve.tensor_scalar(rc["den"][:], rc["ex"][:], 1.0, None, ALU.add))
                link(dve.reciprocal(rc["w1"][:], rc["den"][:]))
                link(dve.tensor_tensor(rc["w2"][:], rc["ex"][:], rc["w1"][:], ALU.mult))
                at_least(dve, s["scattered"], g * (16 * TOPK * G))
                link(dve.tensor_copy(rows[:, 0, :, D + 1], rc["w1"][:]))
                link(dve.tensor_copy(rows[:, 1, :, D + 1], rc["w2"][:]))
                link(dve.tensor_copy(rows[:, :, :, D].bitcast(I32), dest0[:]))
                link(dve.tensor_scalar(dest0[:], dest0[:], float(G * S), None, ALU.add))
                bank, free = filled(dve, b, "rank")
                dve.tensor_tensor(rt["pos"][:], bank[0:SL, 0:G * E].rearrange("p (g e) -> p g e", g=G), base_row[0:SL].unsqueeze(1).broadcast_to(wide3), ALU.add).then_inc(free, 1)
                evacuated(dve, b, "rank")
                for k, pick in enumerate(("pick1", "pick2")):
                    link(dve.tensor_tensor(rt["at"][:], rt["pos"][:], rt[pick][:], ALU.mult))
                    link(dve.tensor_reduce(posf[:, k], rt["at"][:], AX.X, ALU.add))
                dve.tensor_copy(posi[:], posf[:]).then_inc(s["pos_ready"], 1)
                assert n[0] == ROUTE, n[0]

            def body(b):
                if b.has_c:
                    for pair in range(2):
                        affine_copy(*filled(dve, b, "h2T", pair), pair, h2T, g2col, b2col)
                if b.has_b:
                    for pair in range(2):
                        affine_copy(*filled(dve, b, "yT", pair), pair, yT, g1col, b1col)
                if b.has_n:
                    dve.wait_ge(s["h_loaded"], (b.i + 2) * 32)
                    stats_of(0, b.i + 1, h_in)
                    dve.wait_ge(s["fill_done"], b.fills_before)
                    normalise(0, b.i + 1, n0, h_in)
                if b.has_c:
                    route(b)
                for step in range(b.steps):
                    k = step
                    if 0 <= k < len(b.units):
                        kind, g, u = b.units[k]
                        dve.wait_ge(s["score_done"], b.units_before + k + 1)
                        at_least(dve, s["et_done"], b.units_before + k - 3)
                        dve.tensor_tensor(score[:, k % 4].rearrange("p a b -> p (a b)"), s_bank[k % 2][0:SL, 0:UH * SL],
                                          (causal if kind == "a" else padded)[:].rearrange("p a b -> p (a b)"), ALU.add).then_inc(s["score_out"], 1)
                        dve.wait_ge(s["score_out"], b.units_before + k + 1)
                        dve.tensor_reduce(smax[:, k % 4], score[:, k % 4], AX.X, ALU.max).then_inc(s["smax_done"], 1)
                    k = step - LAG_PV
                    if 0 <= k < len(b.units):
                        kind, g, u = b.units[k]
                        w = DH1 if kind == "a" else DH2
                        z = z_bank[k % 2][0:SL, 0:UH * (w + 1)].rearrange("p (h e) -> p h e", h=UH)
                        dve.wait_ge(s["pv_done"], b.units_before + k + 1)
                        dve.reciprocal(zinv[:, k % 2], z[:, :, w]).then_inc(s["zinv_done"], 1)
                        dve.wait_ge(s["zinv_done"], b.units_before + k + 1)
                        dst = (z1 if kind == "a" else z2)[:, g % 2, u * UH * w:(u + 1) * UH * w].rearrange("p (h e) -> p h e", h=UH)
                        dve.tensor_tensor(dst, z[:, :, 0:w], zinv[:, k % 2].unsqueeze(2).broadcast_to([SL, UH, w]), ALU.mult).then_inc(s["z_out"], 1)
                    for label in posts_of(b.n, step):
                        if label[0] == "wo":
                            g = label[1]
                            bank, free = filled(dve, b, *label)
                            if g == 0:
                                dve.wait_ge(s["res_ready"], b.i + 1)
                            dve.tensor_tensor(h_res[:, g], bank[0:SL, 0:D], h_res[:, g], ALU.add).then_inc(free, 1)
                        if label[0] == "pj":
                            g = label[1]
                            bank, free = filled(dve, b, *label)
                            if g == 0:
                                dve.wait_ge(s["n1pb_ready"], b.i)
                                at_least(dve, s["r_ready"], (b.i - 1) * G)
                            dve.tensor_tensor(x2[:, g], bank[0:SL, 0:D], n1_pb[:, g], ALU.add).then_inc(free, 1)
                if b.has_a:
                    evacuated(dve, b, "wo", G - 1)
                    stats_of(1, b.i, h_res)
                if b.has_b:
                    evacuated(dve, b, "pj", G - 1)
                    stats_of(3, b.i - 1, x2)
                if b.has_a:
                    at_least(dve, s["n1pb_ready"], b.i)
                    normalise(1, b.i, n1, h_res)
                    dve.wait_ge(s["ln1_norm"], (b.i + 1) * G)
                    stats_of(2, b.i, n1)
                if b.has_b:
                    at_least(dve, s["scattered"], (b.i - 1) * (16 * TOPK * G))
                    at_least(dve, s["rows_copied"], b.i - 1)
                    normalise(3, b.i - 1, rows[:, 0, :, 0:D], x2)
                if b.has_a:
                    normalise(2, b.i, y0, n1)
            attn_bodies(dve, body)

            links = [0]

            def link(ins):
                links[0] += 1
                ins.then_inc(s["tables"], 1)
                dve.wait_ge(s["tables"], links[0])
            link(dve.memset(tb["one"][:], 1.0))
            dve.wait_ge(s["counts_done"], 1)
            link(dve.tensor_copy(counts[:], s_bank[0][:, 0:E]))
            link(dve.scalar_tensor_tensor(tail_at[:], counts[:], part_id[:, 0:1], base_row[:], ALU.add, ALU.add))
            link(dve.tensor_scalar(tb["x"][:], counts[0:1, :], 1 / 128, 127 / 256, ALU.mult, ALU.add))
            link(dve.tensor_scalar(tb["up"][:], tb["x"][:], MAGIC, None, ALU.add))
            link(dve.tensor_scalar(tb["nt"][:], tb["up"][:], -MAGIC, None, ALU.add))
            link(dve.tensor_tensor_scan(tb["end"][:], tb["one"][:], tb["nt"][:], 0.0, ALU.mult, ALU.add))
            link(dve.tensor_scalar(tb["jump"][:], tb["nt"][:], -128.0, float(REGION), ALU.mult, ALU.add))
            w54 = [1, NTILE, E]
            link(dve.tensor_tensor(past[:], tt_["t"][:].unsqueeze(2).broadcast_to(w54), tb["end"][:].unsqueeze(1).broadcast_to(w54), ALU.is_ge))
            link(dve.tensor_reduce(tt_["e"][:], past[:], AX.X, ALU.add))
            link(dve.tensor_scalar(tile_expert[:], tt_["e"][:], float(E - 1), None, ALU.min))
            link(dve.tensor_tensor(jumps[:], past[:], tb["jump"][:].unsqueeze(1).broadcast_to(w54), ALU.mult))
            link(dve.tensor_reduce(tt_["s"][:], jumps[:], AX.X, ALU.add))
            link(dve.scalar_tensor_tensor(tile_row[:], tt_["t"][:], 128.0, tt_["s"][:], ALU.mult, ALU.add))
            dve.memset(tb["x"][:], 0.0).then_inc(s["tables_ready"], 1)
            dve.wait_ge(s["tables_ready"], 1)
            dve.memset(tb["up"][:], 0.0).then_inc(s["attn_end"], 1)

            dve.wait_ge(s["attn_end"], 1)
            dve.wait_ge(s["scattered"], 16 * TOPK * B)
            dve.wait_ge(s["r_stored"], 16 * NG)
            dve.wait_ge(s["expert_loaded"], 16 * 4 * E)
            for k in range(2):
                dve.memset(xT[HALF:HALF + 1, k, 1, :], 1.0).then_inc(s["moe_ones"], 1)

            def features(tile, par):
                dve.wait_ge(s["xT_done"], tile + 1)
                at_least(dve, s["up_done1"], tile - 1)
                for c in range(2):
                    ins = dve.tensor_scalar(xT[0:HALF, par, c, :], banks[par][0:HALF, c * 128:(c + 1) * 128], g2col[:, c:c + 1], b2col[:, c:c + 1], ALU.mult, ALU.add)
                ins.then_inc(s["xT_ready"], 1)

            features(0, 0)

            def expert(i, p):
                if (at := xtile_at(i, p, 1)) is not None:
                    tile, place = at
                    dve.wait_ge(s["hidT_done"], tile + 1)
                    at_least(dve, s["down_done"], tile - 1)
                    dve.tensor_copy(hidT[:, place % 2, FF // 2:], banks[5][:, 0:FF // 2]).then_inc(s["hidT_ready1"], 1)
                if (at := xtile_at(i, p, -1)) is not None:
                    features(at[0], at[1] % 2)
                if (at := xtile_at(i, p, 1)) is not None:
                    tile, place = at
                    e = dve.value_load(tile_expert[0:1, bass.ds(tile, 1)], min_val=0, max_val=E - 1)
                    dve.wait_ge(s["down_done"], tile + 1)
                    dve.tensor_tensor(y_raw[:, place % 2, :], banks[6 + place % 2][:, 0:D], b2_rows[:, bass.ds(e, 1), :].rearrange("p a b -> p (a b)"), ALU.add).then_inc(s["y_biased"], 1)
                    dve.wait_ge(s["y_biased"], tile + 1)
                    at_least(dve, s[f"y_stored{place % 2}"], half_count(i, p, 1) * 16)
                    dve.tensor_scalar(y_row[:, place % 2, :], y_raw[:, place % 2, :], xt[:, place, D + 1:D + 2], None, ALU.mult).then_inc(s["y_ready"], 1)
            expert_steps(dve, expert)

            for k in range(NP_):
                dve.wait_ge(s[f"r_loaded{k}"], 16)
                dve.wait_ge(s[f"ya_loaded{k}"], 16)
                dve.tensor_tensor(last_ya[:, k], last_ya[:, k], last_r[:, k], ALU.add).then_inc(s["last_chain"], 1)
                dve.wait_ge(s["last_chain"], k + 1)
                dve.wait_ge(s[f"yb_loaded{k % 2}"], 16 * (k // 2 + 1))
                dve.tensor_tensor(last_ya[:, k], last_ya[:, k], last_yb[:, k % 2], ALU.add).then_inc(s["last_out"], 1)

        @block.tensor
        def _(pe):
            pe.wait_ge(s["ident_ready"], 1)
            pe.wait_ge(s["tok_staged"], 2)
            pe.wait_ge(s["order_loaded"], 16)
            for k in range(7):
                ins = pe.transpose(banks[0][0:TT, k * NT:(k + 1) * NT], tok_f[:, k, :], ident[0:NT, 0:NT])
            ins.then_inc(s["tokT_done"], 1)

            pe.wait_ge(s["img_loaded"], 16 * 4 * (IMG // PATCH))
            pe.wait_ge(s["text_w_loaded"], 16 * len(text_loads()))
            for k in range(4):
                for h in range(2):
                    at_least(pe, s["patchT_out"], 2 * k + h - 1)
                    for c in range(3):
                        ins = pe.transpose(t_bank[h][:, c * 128:(c + 1) * 128], xpatch[:, k, (3 * h + c) * 128:(3 * h + c + 1) * 128], ident[:])
                    ins.then_inc(s["patchT_done"], 1)
                pe.wait_ge(s["patchT_out"], 2 * k + 2)
                at_least(pe, s["img_ready"], k - 1)
                for c in range(KP // 128):
                    ins = pe.matmul(banks[2 + k % 2][:, 0:D], patchT[:, k % 2, c, :], w_img[:, c, :], start=c == 0, stop=c == KP // 128 - 1)
                ins.then_inc(s["img_done"], 1)
            pe.wait_ge(s["img_ready"], 4)
            pe.wait_ge(s["tok_ready"], 1)

            def text(i, p):
                if (at := tile_at(i, p, 0)) is not None:
                    tile, par = at
                    pe.wait_ge(s["f1_ready"], tile + 1)
                    at_least(pe, s["f1T_ready"], tile - 1)
                    for c in range(2):
                        ins = pe.transpose(banks[par][0:C1, c * TT:(c + 1) * TT], f1[:, par, c * C1:(c + 1) * C1], ident[0:TT, 0:TT])
                    ins.then_inc(s["f1T_done"], 1)
                if (at := tile_at(i, p, 1)) is not None:
                    tile, par = at
                    pe.wait_ge(s["f1T_ready"], tile + 1)
                    at_least(pe, s["merged"], tile - 1)
                    for c in range(2):
                        ins = pe.matmul(banks[2 + par][0:TT, 0:D], f1T[:, par, c, :], w_merge[:, c, :], start=c == 0, stop=c == 1)
                    ins.then_inc(s["merge_done"], 1)
                if (at := tile_at(i, p, 2)) is not None:
                    tile, par = at
                    pe.wait_ge(s["merged"], tile + 1)
                    pe.wait_ge(s["sines_copied"], tile + 1)
                    at_least(pe, s["f2T_ready"], tile - 1)
                    for c in range(2):
                        ins = pe.transpose(banks[4 + par][0:C2, c * TT:(c + 1) * TT], f2[:, par, c * C2:(c + 1) * C2], ident[0:TT, 0:TT])
                    ins.then_inc(s["f2T_done"], 1)
                if (at := tile_at(i, p, 3)) is not None:
                    tile, par = at
                    pe.wait_ge(s["f2T_ready"], tile + 1)
                    at_least(pe, s["gelu_done"], tile - 1)
                    for c in range(2):
                        ins = pe.matmul(banks[6 + par][0:TT, 0:D], f2T[:, par, c, :], w_feat[:, c, :], start=c == 0, stop=c == 1)
                    ins.then_inc(s["feat_done"], 1)
            text_steps(pe, text)

            pe.wait_ge(s["gelu_done"], NT)
            pe.wait_ge(s["attn_w_loaded"], 16 * len(attn_loads()))
            pe.wait_ge(s["attn_pool_consts"], 1)
            pe.wait_ge(s["attn_vec_ready"], 1)

            def turn_pair(bank, src, pair):
                for j in range(2):
                    for c in range(2):
                        ins = pe.transpose(bank[0:HALF, (2 * j + c) * SL:(2 * j + c + 1) * SL], src[:, 2 * pair + j, c * HALF:(c + 1) * HALF], ident[0:SL, 0:SL])
                return ins
            pe.wait_ge(s["ln0_norm"], G)
            for pair in range(2):
                turn_pair(g_bank[pair], n0, pair).then_inc(s["fill_done"], 1)

            def open_fill(b, *label, reads=()):
                bank, _, before = b.fill(*label)
                pe.wait_ge(s[f"fill_free{bank}"], before)
                for other in reads:
                    if b.fill(*other)[0] != bank:
                        evacuated(pe, b, *other)
                return g_bank[bank]

            def body(b):
                if b.has_a:
                    for bank in range(2):
                        pe.wait_ge(s[f"fill_free{bank}"], b.bank_fills_before)
                    for k in range(PAIRS):
                        for w, weight in (("q", wq), ("k", wk_)):
                            bank = open_fill(b, w, k)
                            for c in range(2):
                                ins = pe.matmul(bank[:, 0:GT], weight[:, c, k * 128:(k + 1) * 128], nT[0:HALF, c, :], start=c == 0, stop=c == 1)
                            ins.then_inc(s["fill_done"], 1)
                if b.has_c:
                    pe.wait_ge(s["ln3_norm"], (b.i - 1) * G)
                    for pair in range(2):
                        turn_pair(open_fill(b, "h2T", pair), rows[:, 0], pair).then_inc(s["fill_done"], 1)
                if b.has_b:
                    pe.wait_ge(s["ln2_norm"], b.i * G)
                    for pair in range(2):
                        turn_pair(open_fill(b, "yT", pair), y0, pair).then_inc(s["fill_done"], 1)
                if b.has_a:
                    for g in range(G):
                        for h in range(2):
                            bank = open_fill(b, "v", g, h)
                            for c in range(2):
                                ins = pe.matmul(bank[0:SL, 0:6 * DH1], nT[0:HALF + c, c, g * SL:(g + 1) * SL], wv[0:HALF + c, c, h * 6 * DH1:(h + 1) * 6 * DH1],
                                                start=c == 0, stop=c == 1)
                            ins.then_inc(s["fill_done"], 1)
                if b.has_c:
                    bank = open_fill(b, "gate", reads=[("h2T", 0), ("h2T", 1)])
                    for g in range(G):
                        for c in range(2):
                            ins = pe.matmul(bank[0:SL, g * E:(g + 1) * E], h2T[:, c, g * SL:(g + 1) * SL], wgate[:, c, :], start=c == 0, stop=c == 1)
                    ins.then_inc(s["fill_done"], 1)
                if b.has_b:
                    for k in range(QUADS):
                        for w, weight in (("q2", wq2), ("k2", wk2)):
                            bank = open_fill(b, w, k, reads=[("yT", 0), ("yT", 1)] if (w, k) == ("q2", 0) else [])
                            for c in range(2):
                                ins = pe.matmul(bank[:, 0:GT], weight[:, c, k * 128:(k + 1) * 128], yT[:, c, :], start=c == 0, stop=c == 1)
                            ins.then_inc(s["fill_done"], 1)
                    for pair in range(2):
                        bank = open_fill(b, "v2", pair)
                        for j in range(2):
                            g = 2 * pair + j
                            for c in range(2):
                                ins = pe.matmul(bank[0:SL, j * D:(j + 1) * D], yT[:, c, g * SL:(g + 1) * SL], wv2[:, c, :], start=c == 0, stop=c == 1)
                        ins.then_inc(s["fill_done"], 1)
                if b.has_c:
                    pe.wait_ge(s["route"], (b.i - 2) * ROUTE + ROUTE_SEL)
                    bank = open_fill(b, "rank")
                    pe.matmul(bank[0:SL, 0:G * E], earlier[:], rt["sel"][:].rearrange("p a b -> p (a b)"), start=True, stop=False)
                    pe.matmul(bank[0:SL, 0:G * E], ones_first[:, 0:SL], rt["before"][:].rearrange("p a b -> p (a b)"), start=False, stop=True).then_inc(s["fill_done"], 1)

                for step in range(b.steps):
                    k = step
                    if k < len(b.units):
                        kind, g, u = b.units[k]
                        if k == 0:
                            for last in range(2):
                                evacuated(pe, b, *(("v2", last) if b.has_b else ("v", G - 1, last)))
                        at_least(pe, s["score_out"], b.units_before + k - 1)
                        bank = s_bank[k % 2]
                        if kind == "a":
                            for j in range(2):
                                c = 2 * u + j
                                ins = pe.matmul(bank[0:SL, j * 2 * SL:(j + 1) * 2 * SL], qT[:, c, g * SL:(g + 1) * SL],
                                                kbd[:, c, g].rearrange("p a b -> p (a b)"), start=True, stop=True)
                        else:
                            ins = pe.matmul(bank[0:SL, 0:UH * SL], q2T[:, u, g * SL:(g + 1) * SL], k2bd[:, u, g].rearrange("p a b -> p (a b)"), start=True, stop=True)
                        ins.then_inc(s["score_done"], 1)
                    k = step - LAG_T
                    if 0 <= k < len(b.units):
                        pe.wait_ge(s["exp_done"], b.units_before + k + 1)
                        at_least(pe, s["et_out"], b.units_before + k - 1)
                        for h in range(UH):
                            ins = pe.transpose(t_bank[k % 2][0:SL, h * SL:(h + 1) * SL], score[:, k % 4, h, :], ident[0:SL, 0:SL])
                        ins.then_inc(s["et_done"], 1)
                    k = step - LAG_PV
                    if 0 <= k < len(b.units):
                        kind, g, u = b.units[k]
                        v, w = (v1, DH1 + 1) if kind == "a" else (v2, DH2 + 1)
                        pe.wait_ge(s["et_out"], b.units_before + k + 1)
                        at_least(pe, s["z_out"], b.units_before + k - 1)
                        for h in range(UH):
                            ins = pe.matmul(z_bank[k % 2][0:SL, h * w:(h + 1) * w], eT[:, k % 2, h * SL:(h + 1) * SL], v[:, g, u * UH + h, :], start=True, stop=True)
                        ins.then_inc(s["pv_done"], 1)
                    for label in posts_of(b.n, step):
                        what, g = label[0], label[1]
                        bank = open_fill(b, *label, reads={"wo": [("zT", g, 0), ("zT", g, 1)], "pj": [("z2T", g)]}.get(what, []))
                        if what == "zT":
                            pe.wait_ge(s["z_out"], b.units_before + b.units.index(("a", g, UN - 1)) + 1)
                            for j in range(3):
                                c = 3 * label[2] + j
                                ins = pe.transpose(bank[:, j * SL:(j + 1) * SL], z1[:, g % 2, c * 128:(c + 1) * 128], ident[0:SL, 0:SL])
                        elif what == "z2T":
                            pe.wait_ge(s["z_out"], b.units_before + b.units.index(("b", g, UN - 1)) + 1)
                            for c in range(2):
                                ins = pe.transpose(bank[0:HALF, c * SL:(c + 1) * SL], z2[:, g % 2, c * HALF:(c + 1) * HALF], ident[0:SL, 0:SL])
                        elif what == "wo":
                            for c in range(PAIRS):
                                ins = pe.matmul(bank[0:SL, 0:D], z1T[:, c, :], wo[:, c, :], start=c == 0, stop=c == PAIRS - 1)
                        else:
                            for c in range(2):
                                ins = pe.matmul(bank[0:SL, 0:D], z2T[:, c, :], wp2[:, c, :], start=c == 0, stop=c == 1)
                        ins.then_inc(s["fill_done"], 1)
                if b.has_n:
                    pe.wait_ge(s["ln0_norm"], (b.i + 2) * G)
                    for pair in range(2):
                        turn_pair(open_fill(b, "nT", pair), n0, pair).then_inc(s["fill_done"], 1)
            attn_bodies(pe, body)

            pe.wait_ge(s["route"], NG * ROUTE)
            pe.matmul(s_bank[0][:, 0:E], ones_first[:], runsum[:], start=True, stop=True).then_inc(s["counts_done"], 1)

            pe.wait_ge(s["expert_loaded"], 16 * 4 * E)
            pe.wait_ge(s["moe_ones"], 2)

            def turn_rows(tile, place, loads):
                pe.wait_ge(s[f"xt_loaded{place}"], loads * 16)
                at_least(pe, s["xT_ready"], tile - 1)
                for c in range(2):
                    ins = pe.transpose(banks[place % 2][0:HALF, c * 128:(c + 1) * 128], xt[:, place, c * HALF:(c + 1) * HALF], ident[:])
                ins.then_inc(s["xT_done"], 1)
            turn_rows(0, 0, 1)

            def expert(i, p):
                up = xtile_at(i, p, 0) is not None
                down = xtile_at(i, p, 1) is not None
                tile = i * 4 + p
                if up:
                    e = pe.value_load(tile_expert[0:1, bass.ds(tile, 1)], min_val=0, max_val=E - 1)
                for h in range(2):
                    if up:
                        if h == 0:
                            pe.wait_ge(s["xT_ready"], tile + 1)
                        at_least(pe, s[f"hid_ready{h}"], tile)
                        for c in range(2):
                            ins = pe.matmul(banks[2 + h][:, 0:FF // 2], xT[0:HALF + c, p % 2, c, :],
                                            w1[0:HALF + c, bass.ds(e, 1), c, h * (FF // 2):(h + 1) * (FF // 2)].rearrange("p a b -> p (a b)"),
                                            start=c == 0, stop=c == 1)
                        ins.then_inc(s[f"up_done{h}"], 1)
                    if down and h == 0:
                        for k in range(2):
                            pe.wait_ge(s[f"hid_ready{k}"], tile)
                            at_least(pe, s[f"hidT_ready{k}"], tile - 1)
                        for c in range(FF // 128):
                            ins = pe.transpose(banks[4 + c // 3][:, c % 3 * 128:(c % 3 + 1) * 128], hid[:, (p - 1) % 2, c * 128:(c + 1) * 128], ident[:])
                        ins.then_inc(s["hidT_done"], 1)
                if (at := xtile_at(i, p, -1)) is not None:
                    turn_rows(*at, i + (1 if p < 3 else 2))
                if down:
                    e = pe.value_load(tile_expert[0:1, bass.ds(tile - 1, 1)], min_val=0, max_val=E - 1)
                    par = (p - 1) % 2
                    for k in range(2):
                        pe.wait_ge(s[f"hidT_ready{k}"], tile)
                    at_least(pe, s["y_biased"], tile - 2)
                    for c in range(FF // 128):
                        ins = pe.matmul(banks[6 + par][:, 0:D], hidT[:, par, c * 128:(c + 1) * 128],
                                        w2[:, bass.ds(e, 1), c, :].rearrange("p a b -> p (a b)"), start=c == 0, stop=c == FF // 128 - 1)
                    ins.then_inc(s["down_done"], 1)
            expert_steps(pe, expert)


_INS = """x x_txt itok_BS_0_99 itok_BS_1_36498 itok_BS_0_2047 fside_BS_concept_values mask_BS_f1_0 mask_BS_i2_0 L0_tok_W L0_tok_b
L0_tok_pos_emb L0_txt_concept_emb L0_txt_segment_emb L0_txt_w_age L0_txt_phi_age L0_txt_merge_w L0_txt_merge_b L0_txt_proj_w
L0_txt_proj_b L0_attn_W_Q L0_attn_b_Q L0_attn_W_K L0_attn_b_K L0_attn_W_V L0_attn_b_V L0_attn_W_O L0_attn_b_O L0_ffn_ln1_g
L0_ffn_ln1_b L0_ffn_qkv_w L0_ffn_proj_w L0_ffn_proj_b L0_ffn_ln2_g L0_ffn_ln2_b L0_ffn_gate_w L0_ffn_gate_b L0_ffn_w1 L0_ffn_b1
L0_ffn_w2 L0_ffn_b2""".split()


def kernel(**inputs):
    import numpy as _np
    import concourse.bacc as _bacc
    from concourse import mybir as _mybir
    from concourse.bass_utils import run_bass_kernel_spmd as _run

    nc = _bacc.Bacc("TRN2", target_bir_lowering=False, num_devices=1)
    arrays, args = {}, {}

    def give(name, a):
        arrays[f"in_{name}"] = a
        args[name] = nc.dram_tensor(f"in_{name}", a.shape, _mybir.dt.from_np(a.dtype), kind="ExternalInput").ap()
    for name in _INS:
        give(name, _np.ascontiguousarray(inputs[name]))
    freq = _np.exp(_np.arange(0, T_EMB, 2, dtype=_np.float32) * (-math.log(10000.0) / T_EMB)).astype(_np.float32)
    give("pos_freq", _np.repeat(freq, 2)[None, :])
    quarter = _np.zeros((1, 3 * T_EMB), _np.float32)
    quarter[0, 2 * T_EMB + 1::2] = 1.0
    give("quarter", quarter)
    out = nc.dram_tensor("out_0", (B, S, D), _mybir.dt.float32, kind="ExternalOutput").ap()
    program(nc, args, out)
    r = _run(nc, [arrays], core_ids=[0])
    return r.results[0]["out_0"]
```

```python
import math
from contextlib import ExitStack

import numpy as np

import concourse.bass as bass
from concourse import mybir

ALU = mybir.AluOpType
ACT = mybir.ActivationFunctionType
AX = mybir.AxisListType
F32 = mybir.dt.float32
I32 = mybir.dt.int32
F32R = mybir.dt.float32r

B, S_TXT, N_PATCH = 32, 77, 16
S = S_TXT + N_PATCH
D = 192
HALF = D // 2
VOCAB, N_SEG, T_EMB, MAX_POS = 12500, 3, 16, 512
HEADS, DH1, DH2 = 12, 64, 16
E, FF = 8, 768
EPS = 1e-5
NEG = -1e30

TT = 112
NT = B * S_TXT // TT
assert NT * TT == B * S_TXT
PEEL = 8
PATCH, IMG = 16, 64
KP = PATCH * PATCH * 3
F1W = D + 2
F2W = D + 3 * T_EMB + 2
C1, C2 = F1W // 2, F2W // 2

G = 4
NG = B // G
SL = 96
GT = G * SL
UH = 4
UN = HEADS // UH
PAIRS = HEADS * DH1 // 128
SIXES = 2

TOPK = 2
ROW = D + 2
REGION = -(-(B * S + 128) // 128) * 128
SLOTS = TOPK * B * S
NTILE = -(-SLOTS // 128) + E - 1 + (-(-SLOTS // 128) + E - 1) % 2
W_COLS = 2 * FF + FF // 128 * D + D
SPARE = NTILE - SLOTS // 128 + 1
XS_ROWS = E * REGION + SPARE * 128
Y_ROWS = SLOTS + (E + SPARE) * 128

LP, CJ = 124, 6
NP_ = B * S // (LP * CJ)

ROUTE = 28
ROUTE_SEL = 17

MAGIC = 1.5 * 2.0 ** 23
TP1 = 6.28125
TP2 = math.floor((2 * math.pi - TP1) * 2 ** 18) / 2 ** 18
TP3 = 2 * math.pi - TP1 - TP2


def at_least(eng, sem, value):
    if not isinstance(value, int) or value > 0:
        eng.wait_ge(sem, value)


class Body:

    def __init__(self, n, i):
        self.n, self.i = n, i
        self.has_a, self.has_b, self.has_c, self.has_n = parts_of(n)
        self.fills, self.units = fills_of(n), units_of(n)
        self.steps = len(self.units) + LAG_PROJ + 2
        self.units_before = count_before(n, i, units_of, 1)
        self.fills_before = count_before(n, i, fills_of, 1) + 2
        self.bank_fills_before = count_before(n, i, fills_of, 2) + 1

    def fill(self, *label):
        k = self.fills.index(label)
        return k % 2, self.fills_before + k, self.bank_fills_before + k // 2


FIRST_FULL, LAST_FULL = 2, NG - 2
LAG_T, LAG_PV, LAG_PROJ = 3, 4, 6


def parts_of(n):
    return n < NG, 1 <= n <= NG, n >= 2, n < NG - 1


def count_before(n, i, of, per):
    first = sum(len(of(m)) for m in range(n)) // per
    if isinstance(i, int):
        return first
    each = len(of(n)) // per
    return i * each + (first - n * each)


def units_of(n):
    a, b, _, _ = parts_of(n)
    return [(kind, g, u) for g in range(G) for u in range(UN) for kind, on in (("a", a), ("b", b)) if on]


def posts_of(n, step):
    units, found = units_of(n), []
    for lag in (LAG_PROJ + 1, LAG_PROJ):
        k = step - lag
        if 0 <= k < len(units) and units[k][2] == UN - 1:
            kind, g, _ = units[k]
            if lag == LAG_PROJ:
                found += [("zT", g, 0), ("zT", g, 1)] if kind == "a" else [("z2T", g)]
            else:
                found += [("wo", g)] if kind == "a" else [("pj", g)]
    if parts_of(n)[3] and step == len(units) + 1:
        found += [("nT", 0), ("nT", 1)]
    return found


def fills_of(n):
    a, b, c, _ = parts_of(n)
    f = [(w, k) for k in range(PAIRS) for w in ("q", "k")] if a else []
    f += [("h2T", 0), ("h2T", 1)] if c else []
    f += [("yT", 0), ("yT", 1)] if b else []
    f += [("v", g, h) for g in range(G) for h in range(2)] if a else []
    f += [("gate",)] if c else []
    f += [(w, k) for k in range(SIXES) for w in ("q2", "k2")] + [("v2", 0), ("v2", 1)] if b else []
    f += [("rank",)] if c else []
    for step in range(len(units_of(n)) + LAG_PROJ + 2):
        f += posts_of(n, step)
    return f


def program(nc, t, out):
    def dram(name, shape):
        return nc.dram_tensor(name, shape, F32, kind="Internal").ap()

    txt_d = dram("txt_d", [B * S_TXT, D])
    img_d = dram("img_d", [B * N_PATCH, D])
    ord_d = dram("ord_d", [B, S_TXT])
    r_d = dram("r_d", [B * S, D])
    xs_d = dram("xs_d", [XS_ROWS, ROW])
    y_d = dram("y_d", [Y_ROWS, D])

    ctx = ExitStack()
    with ctx:
        scope = [ctx]

        def sb(name, shape, dt=F32):
            return scope[0].enter_context(nc.sbuf_tensor(name, shape, dt))

        def sem(name):
            return ctx.enter_context(nc.semaphore(name))

        banks = [ctx.enter_context(nc.psum_tensor(f"bank{k}", [128, 512], F32)) for k in range(8)]

        ident = sb("ident", [128, 128])
        zero_rows = sb("zero_rows", [128, max(E, SPARE), ROW])
        tail_row = sb("tail_row", [1, E], I32)
        rows = sb("rows", [SL, TOPK, G, ROW])
        posi = sb("posi", [SL, TOPK, G], I32)
        counts = sb("counts", [128, E])
        tile_expert = sb("tile_expert", [1, NTILE], I32)
        tile_row = sb("tile_row", [1, NTILE], I32)
        ones_first = sb("ones_first", [SL, 128])
        g2col = sb("g2col", [HALF, 2])
        b2col = sb("b2col", [HALF, 2])
        base_row = sb("base_row", [128, E])
        part_id = sb("part_id", [128, 1])

        weights_scope = ctx.enter_context(ExitStack())
        scope[0] = weights_scope
        (wq_hi, wq_lo), (wk_hi, wk_lo), (wv_hi, wv_lo) = (
            [sb(f"{n}_{part}", [HALF + more, 2, HEADS * DH1]) for part in ("hi", "lo")] for n, more in (("wq", 0), ("wk", 0), ("wv", 1)))
        wo = sb("wo", [128, PAIRS, D])
        bq, bk = sb("bq", [128, PAIRS]), sb("bk", [128, PAIRS])
        wqkv2, wp2 = sb("wqkv2", [HALF, 2, 3 * D]), sb("wp2", [HALF, 2, D])
        wgate = sb("wgate", [HALF, 2, E])
        g1col, b1col = sb("g1col", [HALF, 2]), sb("b1col", [HALF, 2])
        bo_row, pb_row = sb("bo_row", [SL, D]), sb("pb_row", [SL, D])
        gb_row = sb("gb_row", [SL, E])
        causal, padded = sb("causal", [SL, UH, SL]), sb("padded", [SL, UH, SL])
        earlier = sb("earlier", [SL, SL])
        head_rows = sb("head_rows", [HALF, HEADS // SIXES])
        neg_half = sb("neg_half", [SL, G])
        from_end = sb("from_end", [SL, E])
        dest0 = sb("dest0", [SL, G, TOPK])
        h_in = sb("h_in", [SL, G, D])
        nT = sb("nT", [HALF + 1, 2, GT])
        v1 = sb("v1", [SL, G, HEADS, DH1 + 1])
        k2bd = sb("k2bd", [HALF, HEADS, G, SL])
        v2 = sb("v2", [SL, G, HEADS, DH2 + 1])
        runsum = sb("runsum", [SL, E])
        lns = [{"stats": sb(f"ln{k}_stats", [SL, G, 6]), "mv": sb(f"ln{k}_mv", [SL, G, 2]),
                "var": sb(f"ln{k}_var", [SL, G]), "rstd": sb(f"ln{k}_rstd", [SL, G])} for k in range(4)]
        tb = {n: sb(f"tb_{n}", [1, E]) for n in ("x", "up", "whole", "nt", "end", "jump", "one")}
        tt_ = {n: sb(f"tt_{n}", [1, NTILE]) for n in ("t", "e", "s")}

        image_scope = ctx.enter_context(ExitStack())
        scope[0] = image_scope
        xpatch = sb("xpatch", [128, 4, KP])
        w_img = sb("w_img", [128, KP // 128, D])
        patchT = sb("patchT", [128, 2, KP // 128, 128])
        img_h = sb("img_h", [128, 4, D])
        image_scope.close()
        whole_scope = ctx.enter_context(ExitStack())
        scope[0] = whole_scope
        wq, wk_, wv = sb("wq", [HALF, 2, HEADS * DH1]), sb("wk", [HALF, 2, HEADS * DH1]), sb("wv", [HALF + 1, 2, HEADS * DH1])
        whole_scope.close()
        scope[0] = weights_scope
        kbd = sb("kbd", [128, PAIRS, G, 2, SL])
        nT_lo = sb("nT_lo", [HALF, 2, GT])
        n0 = sb("n0", [SL, G, D])
        filler = sb("filler", [128, 4 * KP + KP // 128 * D + 2 * KP + 4 * D - PAIRS * G * 2 * SL - 2 * GT - G * D])

        text_scope = ctx.enter_context(ExitStack())
        scope[0] = text_scope
        img_add = sb("img_add", [N_PATCH + 1, D])
        img_sel = sb("img_sel", [N_PATCH + 1, 128])
        tok_i = sb("tok_i", [NT, 4, TT], I32)
        tok_f = sb("tok_f", [NT, 7, TT])
        tok = sb("tok", [TT, 7, NT])
        ids = sb("ids", [TT, NT], I32)
        keep = sb("keep", [TT, NT, 2])
        segm = sb("segm", [TT, N_SEG, NT])
        vco_i = sb("vco_i", [B, S_TXT], I32)
        vco = sb("vco", [B, S_TXT])
        vmin = sb("vmin", [B, 1])
        order = sb("order", [B, S_TXT])
        frow = sb("frow", [TT, 3, T_EMB])
        prow = sb("prow", [TT, 3, T_EMB])
        qrow = sb("qrow", [TT, 3, T_EMB])
        arg = sb("arg", [TT, NT, 3 * T_EMB])
        turns = sb("turns", [TT, NT, 3 * T_EMB])
        f1all = sb("f1all", [TT, NT, F1W])
        f1 = sb("f1", [TT, 2, F1W])
        f1T = sb("f1T", [C1, 2, 2, TT])
        f2 = sb("f2", [TT, 2, F2W])
        f2T = sb("f2T", [C2, 2, 2, TT])
        blend = sb("blend", [TT, 2, D])
        gelu = sb("gelu", [TT, 2, D])
        txt_h = sb("txt_h", [TT, 2, D])
        w_merge = sb("w_merge", [C1, 2, D])
        w_feat = sb("w_feat", [C2, 2, D])
        seg_rows = sb("seg_rows", [TT, N_SEG, D])
        text_scope.close()

        attn_scope = ctx.enter_context(ExitStack())
        scope[0] = attn_scope
        h_res = sb("h_res", [SL, G, D])
        n1 = sb("n1", [SL, G, D])
        y0 = sb("y0", [SL, G, D])
        n1_pb = sb("n1_pb", [SL, G, D])
        h_keep = sb("h_keep", [SL, G, D])
        x2 = sb("x2", [SL, G, D])
        yT = sb("yT", [HALF, 2, GT])
        h2T = sb("h2T", [HALF, 2, GT])
        qT = sb("qT", [128, PAIRS, GT])
        q2T = sb("q2T", [HALF, SIXES, GT])
        score = sb("score", [SL, 4, UH, SL])
        smax = sb("smax", [SL, 4, UH])
        eT = sb("eT", [SL, 2, UH * SL])
        zinv = sb("zinv", [SL, 2, UH])
        z1 = sb("z1", [SL, 2, HEADS * DH1])
        z2 = sb("z2", [SL, 2, D])
        z1T = sb("z1T", [128, PAIRS, SL])
        z2T = sb("z2T", [HALF, 2, SL])
        rt = {n: sb(f"rt_{n}", [SL, G, E]) for n in ("logit", "eq", "mark", "pick1", "rest", "pick2", "sel", "before", "pos", "at")}
        rc = {n: sb(f"rc_{n}", [SL, G]) for n in ("m1", "i1", "m2", "i2", "gap", "ex", "den", "w1", "w2")}
        posf = sb("posf", [SL, TOPK, G])
        q_flat = qT[0:1].rearrange("p a b -> p (a b)")
        past, jumps = (q_flat[:, k * NTILE * E:(k + 1) * NTILE * E].rearrange("p (t e) -> p t e", e=E) for k in range(2))
        attn_scope.close()
        weights_scope.close()

        moe_scope = ctx.enter_context(ExitStack())
        scope[0] = moe_scope
        xt = sb("xt", [128, 4, ROW])
        xT = sb("xT", [HALF + 1, 2, 2, 128])
        w1_now = sb("w1_now", [HALF + 1, 2, 2, FF])
        hidT = sb("hidT", [128, 2, FF])
        y_raw = sb("y_raw", [128, 2, D])
        y_row = sb("y_row", [128, 2, D])
        last_r, last_ya = sb("last_r", [LP, NP_, CJ, D]), sb("last_ya", [LP, NP_, CJ, D])
        last_yb = sb("last_yb", [LP, 2, CJ, D])
        experts_w = sb("experts_w", [128, E, W_COLS])
        moe_scope.close()
        s = {n: sem(n) for n in """vco_loaded tokens_loaded sine_rows_loaded text_w_loaded img_loaded
            order_chain order_stored order_loaded img_w_loaded img_sel_ready tok_staged tokT_done tok_ready ids_ready masks_ready arg_chain arg_ready sines_ready
            f1_cols_ready gathered_first gathered_rest ident_ready pool_chain pool_consts attn_pool_consts
            patchT_done patchT_out img_done img_ready img_stored
            f1_ready f1T_done f1T_ready merge_done blend_half merged sines_copied f2T_done f2T_ready feat_done gelu_done seg_chain text_ready
            text_stored0 text_stored1 attn_w_loaded attn_vec_ready qkv_w_loaded weights_split nT_hi
            h_loaded res_ready keep_ready n1pb_ready
            fill_done fill_free0 fill_free1 score_done score_out smax_done shifted exp_done et_done et_out pv_done zinv_done z_out
            r_ready r_stored route gap_ready ex_ready pos_ready rows_copied scattered runsum_ready counts_done tables
            tables_ready tails_stored0 tails_stored1 spare_stored zero_rows_ready attn_end moe_ones
            xt_loaded0 xt_loaded1 xt_loaded2 xt_loaded3 xT_done xT_ready up_done0 up_done1 w1_copied0 w1_copied1 hid_ready0 hid_ready1
            down_done y_biased y_ready y_stored0 y_stored1
            r_loaded0 r_loaded1 r_loaded2 r_loaded3 ya_loaded0 ya_loaded1 ya_loaded2 ya_loaded3 yb_loaded0 yb_loaded1
            last_chain last_out out_stored apart""".split()}
        for e in range(E):
            s[f"expert_loaded{e}"] = sem(f"expert_loaded{e}")
        for k in range(4):
            for n in ("stats", "mv", "var", "rstd", "norm"):
                s[f"ln{k}_{n}"] = sem(f"ln{k}_{n}")

        g_bank, s_bank, t_bank, z_bank = banks[0:2], banks[2:4], banks[4:6], banks[6:8]


        def patch_source(k):
            return t["x"][8 * k:8 * k + 8].rearrange("b (ph i) (pw j) c -> (b ph) pw i (j c)", i=PATCH, j=PATCH)

        def img_loads():
            return [(w_img[:], t["L0_tok_W"].rearrange("(c p) d -> p c d", p=128)),
                    (img_add[0:N_PATCH, :], t["L0_tok_pos_emb"]),
                    (img_add[N_PATCH:N_PATCH + 1, :], t["L0_tok_b"].unsqueeze(0))]

        def text_loads():
            pairs = [(w_merge[:, 0, :], t["L0_txt_merge_w"][0:C1, :]),
                     (w_merge[0:C1 - 1, 1, :], t["L0_txt_merge_w"][C1:D + 1, :]),
                     (w_merge[C1 - 1:C1, 1, :], t["L0_txt_merge_b"].unsqueeze(0)),
                     (w_feat[:, 0, :], t["L0_txt_proj_w"][0:C2, :]),
                     (w_feat[0:C2 - 2, 1, :], t["L0_txt_proj_w"][C2:, :]),
                     (w_feat[C2 - 2:C2 - 1, 1, :], t["L0_txt_proj_b"].unsqueeze(0)),
                     (w_feat[C2 - 1:C2, 1, :], t["L0_txt_proj_b"].unsqueeze(0))]
            pairs += [(seg_rows[:, k, :], t["L0_txt_segment_emb"][k:k + 1, :].broadcast_to([TT, D])) for k in range(N_SEG)]
            return pairs

        def attn_loads():
            pairs = []
            for c in range(2):
                rows_c = slice(c * HALF, (c + 1) * HALF)
                pairs += [(wqkv2[:, c, :], t["L0_ffn_qkv_w"][rows_c, :]), (wp2[:, c, :], t["L0_ffn_proj_w"][rows_c, :]),
                          (wgate[:, c, :], t["L0_ffn_gate_w"][rows_c, :])]
            pairs += [(wo[:], t["L0_attn_W_O"].rearrange("h e d -> (h e) d").rearrange("(c p) d -> p c d", p=128)),
                      (bq[:], t["L0_attn_b_Q"].rearrange("h e -> (h e)").rearrange("(c p) -> p c", p=128)),
                      (bk[:], t["L0_attn_b_K"].rearrange("h e -> (h e)").rearrange("(c p) -> p c", p=128)),
                      (g1col[:], t["L0_ffn_ln1_g"].rearrange("(c p) -> p c", p=HALF)),
                      (b1col[:], t["L0_ffn_ln1_b"].rearrange("(c p) -> p c", p=HALF)),
                      (bo_row[:], t["L0_attn_b_O"].unsqueeze(0).broadcast_to([SL, D])),
                      (pb_row[:], t["L0_ffn_proj_b"].unsqueeze(0).broadcast_to([SL, D])),
                      (gb_row[:], t["L0_ffn_gate_b"].unsqueeze(0).broadcast_to([SL, E])),
                      (g2col[:], t["L0_ffn_ln2_g"].rearrange("(c p) -> p c", p=HALF)),
                      (b2col[:], t["L0_ffn_ln2_b"].rearrange("(c p) -> p c", p=HALF))]
            return pairs

        def qkv_loads():
            pairs = [(wv[HALF:HALF + 1, 1, :], t["L0_attn_b_V"].rearrange("h e -> (h e)").unsqueeze(0))]
            for c in range(2):
                for to, name in ((wq, "L0_attn_W_Q"), (wk_, "L0_attn_W_K"), (wv, "L0_attn_W_V")):
                    pairs.append((to[0:HALF, c, :].rearrange("p (h e) -> p h e", h=HEADS), t[name][:, c * HALF:(c + 1) * HALF, :].rearrange("h d e -> d h e")))
            return pairs

        def expert_loads(e):
            cols = experts_w[:, e]
            return [(cols[0:HALF, 0:2 * FF].rearrange("p (c f) -> p c f", c=2), t["L0_ffn_w1"][e].rearrange("(c p) f -> p c f", p=HALF)),
                    (cols[HALF:HALF + 1, 0:2 * FF].rearrange("p (c f) -> p c f", c=2), t["L0_ffn_b1"][e:e + 1, :].unsqueeze(1).broadcast_to([1, 2, FF])),
                    (cols[:, 2 * FF:2 * FF + FF // 128 * D].rearrange("p (c d) -> p c d", d=D), t["L0_ffn_w2"][e].rearrange("(c p) d -> p c d", p=128)),
                    (cols[:, W_COLS - D:], t["L0_ffn_b2"][e:e + 1, :].broadcast_to([128, D]))]

        def expert_cols(e, first, count):
            return experts_w[:, bass.ds(e, 1), first:first + count].rearrange("p a b -> p (a b)")

        def text_steps(eng, step, before_drain=None):
            for k in range(PEEL):
                step(k // 2, k % 2)
            with eng.Fori(PEEL // 2, NT // 2) as i:
                for p in range(2):
                    step(i, p)
            for k in range(NT, NT + 6):
                if k == NT + 1 and before_drain:
                    before_drain()
                step(k // 2, k % 2)

        def tile_at(i, p, lag):
            if isinstance(i, int) and not 0 <= 2 * i + p - lag < NT:
                return None
            return i * 2 + (p - lag), (p - lag) % 2

        def attn_bodies(eng, body):
            for n in range(FIRST_FULL + 1):
                body(Body(n, n))
            with eng.Fori(FIRST_FULL + 1, LAST_FULL + 1) as i:
                body(Body(FIRST_FULL, i))
            for n in range(LAST_FULL + 1, NG + 2):
                body(Body(n, n))

        def expert_steps(eng, step):
            for p in range(4):
                step(0, p)
            with eng.Fori(1, NTILE // 4) as i:
                for p in range(4):
                    step(i, p)
            for k in range(NTILE // 4 * 4, NTILE + 2):
                step(k // 4, k % 4)

        def xtile_at(i, p, lag):
            if isinstance(i, int) and not 0 <= 4 * i + p - lag < NTILE:
                return None
            return i * 4 + (p - lag), (p - lag) % 4

        def store_tails(eng, k):
            eng.wait_ge(s["tables_ready"], 1)
            eng.wait_ge(s["zero_rows_ready"], 1)
            for e in range(k, E, 2):
                row = eng.value_load(tail_row[0:1, e:e + 1], min_val=0, max_val=E * REGION - 128)
                eng.dma_start(xs_d[bass.ds(row, 128), :], zero_rows[:, e, :]).then_inc(s[f"tails_stored{k}"], 16)

        def copy_w1(eng, copy, h, i, p):
            if (at := xtile_at(i, p, -1)) is None:
                return
            tile, place = at
            if isinstance(tile, int) and tile <= 4:
                for e in range(tile, tile + 1 if tile < 4 else E):
                    eng.wait_ge(s[f"expert_loaded{e}"], 16 * len(expert_loads(e)))
            now = eng.value_load(tile_expert[0:1, bass.ds(tile, 1)], min_val=0, max_val=E - 1)
            at_least(eng, s[f"up_done{h}"], tile - 1)
            half = slice(h * (FF // 2), (h + 1) * (FF // 2))
            copy(w1_now[:, place % 2, :, half], expert_cols(now, 0, 2 * FF)[0:HALF + 1].rearrange("p (c f) -> p c f", c=2)[:, :, half]).then_inc(s[f"w1_copied{h}"], 1)

        def half_count(i, p, lag):
            return i * 2 + (p - lag) // 2

        def evacuated(eng, b, *label):
            bank, _, before = b.fill(*label)
            eng.wait_ge(s[f"fill_free{bank}"], before + 1)

        def filled(eng, b, *label):
            bank, before, _ = b.fill(*label)
            eng.wait_ge(s["fill_done"], before + 1)
            return g_bank[bank], s[f"fill_free{bank}"]

        def wait_apart(eng, sem, value):
            at_least(eng, sem, value)
            if not isinstance(value, int):
                eng.sem_inc(s["apart"], 1)

        block = ctx.enter_context(nc.Block())

        @block.sync
        def _(sp):
            def flat_tokens(a):
                return a.rearrange("b s -> (b s)").rearrange("(n k) -> n k", k=TT)

            sp.dma_start(vco_i[:], t["itok_BS_0_2047"]).then_inc(s["vco_loaded"], 16)
            for slot, name in enumerate(("x_txt", "itok_BS_1_36498", "itok_BS_0_99", "mask_BS_i2_0")):
                sp.dma_start(tok_i[:, slot, :], flat_tokens(t[name])).then_inc(s["tokens_loaded"], 16)
            sp.dma_start(tok_f[:, 4, :], flat_tokens(t["fside_BS_concept_values"])).then_inc(s["tokens_loaded"], 16)
            sp.dma_start(tok_f[:, 5, :], flat_tokens(t["mask_BS_f1_0"])).then_inc(s["tokens_loaded"], 16)
            sp.wait_ge(s["order_chain"], 4)
            sp.dma_start(ord_d, order[:]).then_inc(s["order_stored"], 16)
            for k in range(2):
                sp.dma_start(frow[:, k, :], t["L0_txt_w_age"].broadcast_to([TT, T_EMB])).then_inc(s["sine_rows_loaded"], 16)
                sp.dma_start(prow[:, k, :], t["L0_txt_phi_age"].broadcast_to([TT, T_EMB])).then_inc(s["sine_rows_loaded"], 16)
            sp.dma_start(frow[:, 2, :], t["pos_freq"].broadcast_to([TT, T_EMB])).then_inc(s["sine_rows_loaded"], 16)
            sp.dma_start(qrow[:].rearrange("p a b -> p (a b)"), t["quarter"].broadcast_to([TT, 3 * T_EMB])).then_inc(s["sine_rows_loaded"], 16)
            sp.wait_ge(s["order_stored"], 16)
            sp.dma_start(tok_f[:, 3, :], flat_tokens(ord_d)).then_inc(s["order_loaded"], 16)
            for to, of in attn_loads():
                sp.dma_start(to, of, allow_slow_non_contiguous=True).then_inc(s["attn_w_loaded"], 16)

            for k in range(4):
                sp.wait_ge(s["img_ready"], k + 1)
                sp.dma_start(img_d[k * 128:(k + 1) * 128, :], img_h[:, k, :]).then_inc(s["img_stored"], 16)

            sp.wait_ge(s["img_stored"], 64)
            for to, of in qkv_loads():
                sp.dma_start(to, of).then_inc(s["qkv_w_loaded"], 16)

            def load_h(g):
                at_least(sp, s["ln0_norm"], g * G)
                at_least(sp, s["res_ready"], g)
                sp.dma_start(h_in[0:N_PATCH, :, :], img_d.rearrange("(b s) d -> s b d", s=N_PATCH)[:, bass.ds(g * G, G), :]).then_inc(s["h_loaded"], 16)
                sp.dma_start(h_in[N_PATCH:S, :, :], txt_d.rearrange("(b s) d -> s b d", s=S_TXT)[:, bass.ds(g * G, G), :]).then_inc(s["h_loaded"], 16)
            def store_text(i, p):
                if (at := tile_at(i, p, 5)) is not None:
                    tile, par = at
                    sp.wait_ge(s["text_ready"], tile + 1)
                    sp.dma_start(txt_d[bass.ds(tile * TT, TT), :], txt_h[:, par, :]).then_inc(s[f"text_stored{par}"], 16)

            def load_first_group():
                sp.wait_ge(s["img_stored"], 64)
                for par in range(2):
                    sp.wait_ge(s[f"text_stored{par}"], 16 * (NT // 2 - 3))
                sp.wait_ge(s["attn_pool_consts"], 1)
                load_h(0)
            text_steps(sp, store_text, load_first_group)

            for par in range(2):
                sp.wait_ge(s[f"text_stored{par}"], 16 * (NT // 2))

            def body(b):
                if b.has_n:
                    load_h(b.i + 1)
                if b.has_b:
                    g = b.i - 1
                    sp.wait_ge(s["r_ready"], (g + 1) * G)
                    sp.dma_start(r_d.rearrange("(b s) d -> s b d", s=S)[:, bass.ds(g * G, G), :], h_keep[0:S, :, :]).then_inc(s["r_stored"], 16)
            attn_bodies(sp, body)

            store_tails(sp, 0)
            sp.wait_ge(s["attn_end"], 1)
            sp.wait_ge(s["r_stored"], 16 * NG)

            def load_expert(e):
                for to, of in expert_loads(e):
                    sp.dma_start(to, of).then_inc(s[f"expert_loaded{e}"], 16)
            load_expert(0)
            load_expert(1)

            def pieces(a, k):
                return a.rearrange("(p j) d -> p j d", p=LP)[:, k * CJ:(k + 1) * CJ, :]
            sp.wait_ge(s["scattered"], 16 * TOPK * B)
            for k in range(2):
                sp.wait_ge(s[f"tails_stored{k}"], 16 * (E // 2))
            sp.wait_ge(s["spare_stored"], 16)

            def load_tile(tile, place):
                row = sp.value_load(tile_row[0:1, bass.ds(tile, 1)], min_val=0, max_val=XS_ROWS - 128)
                sp.dma_start(xt[:, place, :], xs_d[bass.ds(row, 128), :]).then_inc(s[f"xt_loaded{place}"], 16)
            for k in range(2):
                load_tile(k, k)


            def load_ahead(i, p):
                if (at := xtile_at(i, p, -2)) is not None:
                    at_least(sp, s[f"y_stored{p % 2}"], half_count(i, p, 0) * 16)
                    load_tile(*at)
                if isinstance(i, int) and i == 0:
                    for e in ((2, 3), (4, 5), (6,), (7,))[p]:
                        load_expert(e)
            expert_steps(sp, load_ahead)
            for k in range(NP_):
                sp.dma_start(last_r[:, k], pieces(r_d, k)).then_inc(s[f"r_loaded{k}"], 16)

            sp.wait_ge(s["y_stored0"], 16 * (NTILE // 2))
            sp.wait_ge(s["y_stored1"], 16 * (NTILE // 2))
            for k in range(NP_):
                sp.dma_start(last_ya[:, k], pieces(y_d[0:B * S, :], k)).then_inc(s[f"ya_loaded{k}"], 16)
                at_least(sp, s["last_out"], k - 1)
                sp.dma_start(last_yb[:, k % 2], pieces(y_d[B * S:SLOTS, :], k)).then_inc(s[f"yb_loaded{k % 2}"], 16)
            for k in range(NP_):
                sp.wait_ge(s["last_out"], k + 1)
                sp.dma_start(pieces(out.rearrange("b s d -> (b s) d"), k), last_ya[:, k]).then_inc(s["out_stored"], 16)
            sp.wait_ge(s["out_stored"], 16 * NP_)

        @block.gpsimd
        def _(pool):
            links = [0]

            def link(ins):
                links[0] += 1
                ins.then_inc(s["pool_chain"], 1)
                pool.wait_ge(s["pool_chain"], links[0])

            link(pool.memset(ident[:], 0.0))
            pool.affine_select(out=ident[:], in_=ident[:], compare_op=ALU.not_equal, fill=1.0, base=0,
                               pattern=[[-1, 128]], channel_multiplier=1).then_inc(s["ident_ready"], 1)
            pool.wait_ge(s["ident_ready"], 1)
            pool.memset(f2[:, :, F2W - 2:F2W - 1], 1.0).then_inc(s["pool_consts"], 1)
            pool.memset(f2[:, :, F2W - 1:F2W], 0.0).then_inc(s["pool_consts"], 1)
            pool.memset(f1all[:, :, F1W - 1:F1W], 1.0).then_inc(s["pool_consts"], 1)
            link(pool.memset(img_sel[:], 1.0))
            pool.tensor_copy(img_sel[0:N_PATCH, :].rearrange("p (a b) -> p a b", b=N_PATCH),
                             ident[0:N_PATCH, 0:N_PATCH].unsqueeze(1).broadcast_to([N_PATCH, 128 // N_PATCH, N_PATCH])).then_inc(s["img_sel_ready"], 1)
            link(pool.memset(zero_rows[:], 0.0))
            link(pool.iota(zero_rows[:, :, D:D + 1].bitcast(I32), pattern=[[128, max(E, SPARE)], [0, 1]], base=SLOTS + E * 128, channel_multiplier=1))
            pool.dma_start(xs_d[E * REGION:XS_ROWS, :].rearrange("(j p) w -> p j w", p=128), zero_rows[:, 0:SPARE, :]).then_inc(s["spare_stored"], 16)
            link(pool.memset(ones_first[:], 1.0))
            link(pool.affine_select(out=ones_first[:], in_=ones_first[:], compare_op=ALU.is_ge, fill=0.0, base=S - 1,
                                    pattern=[[0, 128]], channel_multiplier=-1))
            link(pool.iota(part_id[:], pattern=[[0, 1]], base=0, channel_multiplier=1, allow_small_or_imprecise_dtypes=True))
            link(pool.iota(base_row[:], pattern=[[REGION, E]], base=0, channel_multiplier=0, allow_small_or_imprecise_dtypes=True))
            pool.wait_ge(s["ids_ready"], 1)
            for tile in range(NT):
                name = "gathered_first" if tile < PEEL else "gathered_rest"
                pool.indirect_dma_start(out=f1all[:, tile, 0:D], out_offset=None, in_=t["L0_txt_concept_emb"],
                                        in_offset=bass.IndirectOffsetOnAxis(ap=ids[:, tile:tile + 1], axis=0)).then_inc(s[name], 16)

            pool.wait_ge(s["spare_stored"], 16)
            pool.iota(zero_rows[:, :, D:D + 1].bitcast(I32), pattern=[[128, max(E, SPARE)], [0, 1]], base=SLOTS, channel_multiplier=1).then_inc(s["zero_rows_ready"], 1)

            pool.wait_ge(s["qkv_w_loaded"], 16 * len(qkv_loads()))
            for whole, high, low in ((wq, wq_hi, wq_lo), (wk_, wk_hi, wk_lo), (wv, wv_hi, wv_lo)):
                link(pool.tensor_copy(high[0:HALF].bitcast(F32R), whole[0:HALF]))
                link(pool.tensor_tensor(low[0:HALF].bitcast(F32R), whole[0:HALF], high[0:HALF], ALU.subtract))
            pool.wait_ge(s["gathered_first"], 16 * PEEL)
            pool.wait_ge(s["gathered_rest"], 16 * (NT - PEEL))
            bias, high, low = (w[HALF:HALF + 1, 1, :] for w in (wv, wv_hi, wv_lo))
            link(pool.tensor_copy(high.bitcast(F32R), bias))
            pool.tensor_tensor(low.bitcast(F32R), bias, high, ALU.subtract).then_inc(s["weights_split"], 1)
            pool.wait_ge(s["weights_split"], 1)
            link(pool.memset(h_in[:], 0.0))
            link(pool.memset(kbd[:], 0.0))
            link(pool.memset(head_rows[:], 1.0))
            link(pool.affine_select(out=head_rows[:], in_=head_rows[:], compare_op=ALU.is_ge, fill=0.0, base=0,
                                    pattern=[[-DH2, HEADS // SIXES]], channel_multiplier=1))
            link(pool.affine_select(out=head_rows[:], in_=head_rows[:], compare_op=ALU.is_ge, fill=0.0, base=DH2 - 1,
                                    pattern=[[DH2, HEADS // SIXES]], channel_multiplier=-1))
            link(pool.memset(causal[:], 0.0))
            link(pool.affine_select(out=causal[:], in_=causal[:], compare_op=ALU.is_ge, fill=NEG, base=0,
                                    pattern=[[0, UH], [-1, SL]], channel_multiplier=1))
            link(pool.memset(padded[:], 0.0))
            link(pool.affine_select(out=padded[:], in_=padded[:], compare_op=ALU.is_ge, fill=NEG, base=S - 1,
                                    pattern=[[0, UH], [-1, SL]], channel_multiplier=0))
            link(pool.memset(earlier[:], 1.0))
            link(pool.affine_select(out=earlier[:], in_=earlier[:], compare_op=ALU.is_gt, fill=0.0, base=0,
                                    pattern=[[1, SL]], channel_multiplier=-1))
            link(pool.affine_select(out=earlier[:], in_=earlier[:], compare_op=ALU.is_ge, fill=0.0, base=S - 1,
                                    pattern=[[0, SL]], channel_multiplier=-1))
            link(pool.memset(neg_half[:], -0.5))
            link(pool.iota(from_end[:], pattern=[[-1, E]], base=E, channel_multiplier=0, allow_small_or_imprecise_dtypes=True))
            link(pool.iota(dest0[:], pattern=[[B * S, TOPK], [S, G]], base=0, channel_multiplier=1, allow_small_or_imprecise_dtypes=True))
            link(pool.iota(tt_["t"][:], pattern=[[1, NTILE]], base=0, channel_multiplier=0, allow_small_or_imprecise_dtypes=True))
            link(pool.memset(runsum[:], 0.0))
            link(pool.tensor_copy(nT[HALF:HALF + 1, 1, :].bitcast(F32R).rearrange("p (a b) -> p a b", b=128),
                                  ones_first[0:1, :].unsqueeze(1).broadcast_to([1, GT // 128, 128])))
            link(pool.memset(v1[:, :, :, DH1:DH1 + 1], 1.0))
            pool.memset(v2[:, :, :, DH2:DH2 + 1], 1.0).then_inc(s["attn_pool_consts"], 1)

            def power(k, g):
                pool.wait_ge(s[f"ln{k}_var"], g + 1)
                pool.tensor_tensor(lns[k]["rstd"][:], lns[k]["var"][:], neg_half[:], ALU.pow).then_inc(s[f"ln{k}_rstd"], 1)

            def next_residual(g):
                at_least(pool, s["ln1_norm"], g * G)
                at_least(pool, s["keep_ready"], g)
                pool.wait_ge(s["h_loaded"], (g + 1) * 32)
                pool.tensor_tensor(h_res[:], h_in[:], bo_row[:].unsqueeze(1).broadcast_to([SL, G, D]), ALU.add).then_inc(s["res_ready"], 1)

            power(0, 0)
            pool.wait_ge(s["attn_w_loaded"], 16 * len(attn_loads()))
            for par in range(2):
                pool.wait_ge(s[f"text_stored{par}"], 16 * (NT // 2))
            pool.wait_ge(s["img_stored"], 64)
            next_residual(0)

            def shift(b, k):
                if 0 <= k < len(b.units):
                    at = k % 4
                    pool.wait_ge(s["smax_done"], b.units_before + k + 1)
                    pool.tensor_tensor(score[:, at], score[:, at], smax[:, at].unsqueeze(2).broadcast_to([SL, UH, SL]),
                                       ALU.subtract).then_inc(s["shifted"], 1)

            def scatter(b, k):
                if b.has_c and k < TOPK * G:
                    g, choice = k // TOPK, k % TOPK
                    if k == 0:
                        pool.wait_ge(s["pos_ready"], b.i - 1)
                        wait_apart(pool, s["rows_copied"], b.i - 1)
                    pool.indirect_dma_start(out=xs_d, out_offset=bass.IndirectOffsetOnAxis(ap=posi[0:S, choice, g:g + 1], axis=0),
                                            in_=rows[0:S, choice, g, :], in_offset=None).then_inc(s["scattered"], 16)

            def residual_row(b, step):
                for label in posts_of(b.n, step):
                    if label[0] == "pj":
                        g = label[1]
                        evacuated(pool, b, "pj", g)
                        pool.tensor_tensor(h_keep[:, g], x2[:, g], h_keep[:, g], ALU.add).then_inc(s["r_ready"], 1)

            def body(b):
                if b.has_n:
                    power(0, b.i + 1)
                for step in range(b.steps + 1):
                    shift(b, step)
                    scatter(b, step)
                    residual_row(b, step - 1)
                if b.has_a:
                    power(1, b.i)
                if b.has_b:
                    power(3, b.i - 1)
                if b.has_a:
                    power(2, b.i)
                    evacuated(pool, b, "wo", G - 1)
                    if b.has_b:
                        wait_apart(pool, s["r_stored"], b.i * 16)
                    pool.tensor_copy(h_keep[:], h_res[:]).then_inc(s["keep_ready"], 1)
                    pool.tensor_tensor(n1_pb[:], n1[:], pb_row[:].unsqueeze(1).broadcast_to([SL, G, D]), ALU.add).then_inc(s["n1pb_ready"], 1)
                if b.has_b:
                    pool.wait_ge(s["ln3_norm"], b.i * G)
                    wait_apart(pool, s["scattered"], (b.i - 1) * (16 * TOPK * G))
                    pool.tensor_copy(rows[:, 1, :, 0:D], rows[:, 0, :, 0:D]).then_inc(s["rows_copied"], 1)
                if b.has_n:
                    next_residual(b.i + 1)
            attn_bodies(pool, body)

            def scatter_rows(i, p):
                if (at := xtile_at(i, p, 1)) is not None:
                    tile, place = at
                    wait_apart(pool, s["y_ready"], tile + 1)
                    pool.indirect_dma_start(out=y_d, out_offset=bass.IndirectOffsetOnAxis(ap=xt[:, place, D:D + 1].bitcast(I32), axis=0),
                                            in_=y_row[:, place % 2, :], in_offset=None).then_inc(s[f"y_stored{place % 2}"], 16)
            expert_steps(pool, scatter_rows)

        @block.scalar
        def _(act):
            for to, of in img_loads():
                act.dma_start(to, of).then_inc(s["img_w_loaded"], 16)
            for k in range(4):
                for w in range(IMG // PATCH):
                    act.dma_start(xpatch[w::IMG // PATCH, k, :].rearrange("q (i c) -> q i c", i=PATCH), patch_source(k)[:, w]).then_inc(s["img_loaded"], 16)
            for to, of in text_loads():
                act.dma_start(to, of, allow_slow_non_contiguous=True).then_inc(s["text_w_loaded"], 16)

            for k in range(4):
                for h in range(2):
                    act.wait_ge(s["patchT_done"], 2 * k + h + 1)
                    at_least(act, s["img_done"], k - 1)
                    act.copy(patchT[:, k % 2, 3 * h:3 * h + 3, :].rearrange("p a b -> p (a b)"), t_bank[h][:, 0:384]).then_inc(s["patchT_out"], 1)
                act.wait_ge(s["img_done"], k + 1)
                act.copy(img_h[:, k, :], banks[2 + k % 2][:, 0:D]).then_inc(s["img_ready"], 1)

            act.wait_ge(s["arg_ready"], 1)
            act.activation(turns[:], arg[:], ACT.Sin).then_inc(s["sines_ready"], 1)
            act.wait_ge(s["sines_ready"], 1)

            def text(i, p):
                if (at := tile_at(i, p, 0)) is not None:
                    tile, par = at
                    if isinstance(i, int):
                        act.wait_ge(s["gathered_first"], 16 * PEEL)
                        act.wait_ge(s["f1_cols_ready"], 1)
                        act.wait_ge(s["pool_consts"], 3)
                    else:
                        act.wait_ge(s["gathered_rest"], 16 * (NT - PEEL))
                    at_least(act, s["f1T_done"], tile - 1)
                    at_least(act, s["merged"], tile - 1)
                    act.copy(f1[:, par, :], f1all[:, bass.ds(tile, 1), :].rearrange("p a b -> p (a b)")).then_inc(s["f1_ready"], 1)
                    at_least(act, s["f2T_done"], tile - 1)
                    act.copy(f2[:, par, D:F2W - 2], turns[:, bass.ds(tile, 1), :].rearrange("p a b -> p (a b)")).then_inc(s["sines_copied"], 1)
                if (at := tile_at(i, p, 4)) is not None:
                    tile, par = at
                    act.wait_ge(s["feat_done"], tile + 1)
                    at_least(act, s["text_ready"], tile - 1)
                    act.activation(gelu[:, par, :], banks[6 + par][0:TT, 0:D], ACT.Gelu).then_inc(s["gelu_done"], 1)

            def copy_nT(bank, pair):
                return act.copy(nT[0:HALF].bitcast(F32R)[:, :, pair * 2 * SL:(pair + 1) * 2 * SL].rearrange("p c (g t) -> p c g t", g=2),
                                bank[0:HALF, 0:4 * SL].rearrange("p (g c t) -> p c g t", g=2, c=2))

            def first_nT():
                act.wait_ge(s["attn_pool_consts"], 1)
                for pair in range(2):
                    act.wait_ge(s["fill_done"], pair + 1)
                    copy_nT(g_bank[pair], pair).then_inc(s["nT_hi"], 1)
            text_steps(act, text, first_nT)

            act.wait_ge(s["attn_vec_ready"], 1)
            for par in range(2):
                act.wait_ge(s[f"text_stored{par}"], 16 * (NT // 2))

            def body(b):
                if b.has_a:
                    for k in range(PAIRS):
                        bank, free = filled(act, b, "q", k)
                        act.activation(qT[:, k, :], bank[:, 0:GT], ACT.Identity, bias=bq[:, k:k + 1], scale=DH1 ** -0.5).then_inc(free, 1)
                        bank, free = filled(act, b, "k", k)
                        for j in range(2):
                            ins = act.activation(kbd[64 * j:64 * j + 64, k, :, j, :], bank[64 * j:64 * j + 64, 0:GT].rearrange("p (g t) -> p g t", g=G),
                                                 ACT.Identity, bias=bk[64 * j:64 * j + 64, k:k + 1])
                        ins.then_inc(free, 1)
                    for g in range(G):
                        for h in range(2):
                            bank, free = filled(act, b, "v", g, h)
                            act.copy(v1[:, g, 6 * h:6 * h + 6, 0:DH1], bank[0:SL, 0:6 * DH1].rearrange("p (h e) -> p h e", h=6)).then_inc(free, 1)
                if b.has_b:
                    for k in range(SIXES):
                        bank, free = filled(act, b, "q2", k)
                        act.mul(q2T[:, k, :], bank[0:HALF, 0:GT], DH2 ** -0.5).then_inc(free, 1)
                        bank, free = filled(act, b, "k2", k)
                        for j in range(HEADS // SIXES):
                            ins = act.mul(k2bd[:, k * (HEADS // SIXES) + j].rearrange("p g t -> p (g t)"), bank[0:HALF, 0:GT], head_rows[:, j:j + 1])
                        ins.then_inc(free, 1)
                    for pair in range(2):
                        bank, free = filled(act, b, "v2", pair)
                        act.copy(v2[:, 2 * pair:2 * pair + 2, :, 0:DH2].rearrange("p g h e -> p (g h) e"),
                                 bank[0:SL, 0:2 * D].rearrange("p (h e) -> p h e", e=DH2)).then_inc(free, 1)
                if b.has_c:
                    act.wait_ge(s["gap_ready"], b.i - 1)
                    act.activation(rc["ex"][:], rc["gap"][:], ACT.Exp).then_inc(s["ex_ready"], 1)
                for step in range(b.steps):
                    k = step - LAG_T
                    if 0 <= k < len(b.units):
                        act.wait_ge(s["et_done"], b.units_before + k + 1)
                        at_least(act, s["pv_done"], b.units_before + k - 1)
                        act.copy(eT[:, k % 2, :], t_bank[k % 2][0:SL, 0:UH * SL]).then_inc(s["et_out"], 1)
                    k = step - LAG_T + 1
                    if 0 <= k < len(b.units):
                        act.wait_ge(s["shifted"], b.units_before + k + 1)
                        act.activation(score[:, k % 4], score[:, k % 4], ACT.Exp).then_inc(s["exp_done"], 1)
                    for label in posts_of(b.n, step):
                        if label[0] == "zT":
                            bank, free = filled(act, b, *label)
                            act.copy(z1T[:, 3 * label[2]:3 * label[2] + 3, :].rearrange("p a b -> p (a b)"), bank[:, 0:3 * SL]).then_inc(free, 1)
                        if label[0] == "z2T":
                            bank, free = filled(act, b, *label)
                            act.copy(z2T[:].rearrange("p a b -> p (a b)"), bank[0:HALF, 0:2 * SL]).then_inc(free, 1)
                        if label[0] == "nT":
                            bank, free = filled(act, b, *label)
                            copy_nT(bank, label[1]).then_inc(s["nT_hi"], 1)
            attn_bodies(act, body)

            store_tails(act, 1)
            act.wait_ge(s["attn_end"], 1)
            act.wait_ge(s["r_stored"], 16 * NG)

            def expert(i, p):
                tile = i * 4 + p
                copy_w1(act, act.copy, 1, i, p)
                if xtile_at(i, p, 0) is not None:
                    for h in range(2):
                        act.wait_ge(s[f"up_done{h}"], tile + 1)
                        at_least(act, s["down_done"], tile - 1)
                        act.activation(hidT[:, p % 2, h * (FF // 2):(h + 1) * (FF // 2)], banks[2 + h][:, 0:FF // 2], ACT.Gelu).then_inc(s[f"hid_ready{h}"], 1)
            copy_w1(act, act.copy, 1, -1, 3)
            expert_steps(act, expert)

        @block.vector
        def _(dve):
            dve.wait_ge(s["vco_loaded"], 16)
            dve.tensor_copy(vco[:], vco_i[:]).then_inc(s["order_chain"], 1)
            dve.wait_ge(s["order_chain"], 1)
            dve.tensor_reduce(vmin[:], vco[:], AX.X, ALU.min).then_inc(s["order_chain"], 1)
            dve.wait_ge(s["order_chain"], 2)
            dve.tensor_scalar(order[:], vco[:], vmin[:, 0:1], 0.0, ALU.subtract, ALU.max).then_inc(s["order_chain"], 1)
            dve.wait_ge(s["order_chain"], 3)
            dve.tensor_scalar(order[:], order[:], float(MAX_POS - 1), None, ALU.min).then_inc(s["order_chain"], 1)
            dve.wait_ge(s["tokens_loaded"], 16 * 6)
            dve.tensor_copy(tok_f[:, 0:3, :], tok_i[:, 0:3, :]).then_inc(s["tok_staged"], 1)
            dve.tensor_copy(tok_f[:, 6, :], tok_i[:, 3, :]).then_inc(s["tok_staged"], 1)
            dve.wait_ge(s["tokT_done"], 1)
            dve.tensor_copy(tok[:].rearrange("p a b -> p (a b)"), banks[0][0:TT, 0:7 * NT]).then_inc(s["tok_ready"], 1)
            dve.wait_ge(s["tok_ready"], 1)
            dve.tensor_copy(ids[:], tok[:, 0, :]).then_inc(s["ids_ready"], 1)
            dve.tensor_copy(f1all[:, :, D:D + 1].rearrange("p a b -> p (a b)"), tok[:, 4, :]).then_inc(s["f1_cols_ready"], 1)
            dve.tensor_scalar(keep[:, :, 0], tok[:, 5, :], 0.0, None, ALU.not_equal).then_inc(s["masks_ready"], 1)
            dve.tensor_scalar(keep[:, :, 1], tok[:, 5, :], 0.0, None, ALU.is_equal).then_inc(s["masks_ready"], 1)
            for k in range(N_SEG):
                dve.tensor_scalar(segm[:, k, :], tok[:, 6, :], float(k), None, ALU.is_equal).then_inc(s["masks_ready"], 1)

            dve.wait_ge(s["sine_rows_loaded"], 16 * 6)
            chain = [0]

            def link(ins):
                chain[0] += 1
                ins.then_inc(s["arg_chain"], 1)
                dve.wait_ge(s["arg_chain"], chain[0])
            wide = [TT, NT, 3, T_EMB]
            a4 = arg[:].rearrange("p n (k c) -> p n k c", k=3)
            a3, u3 = arg[:], turns[:]
            link(dve.memset(prow[:, 2, :], 0.0))
            link(dve.tensor_tensor(a4, tok[:, 1:4, :].rearrange("p k n -> p n k").unsqueeze(3).broadcast_to(wide), frow[:].unsqueeze(1).broadcast_to(wide), ALU.mult))
            rows3 = [TT, NT, 3 * T_EMB]
            phases = prow[:].rearrange("p k c -> p (k c)").unsqueeze(1).broadcast_to(rows3)
            quarters = qrow[:].rearrange("p k c -> p (k c)").unsqueeze(1).broadcast_to(rows3)
            link(dve.tensor_tensor(a3, a3, phases, ALU.add))
            link(dve.tensor_scalar(u3, a3, 1 / (2 * math.pi), None, ALU.mult))
            link(dve.scalar_tensor_tensor(u3, quarters, 0.25, u3, ALU.mult, ALU.add))
            link(dve.tensor_scalar(u3, u3, MAGIC, None, ALU.add))
            link(dve.tensor_scalar(u3, u3, -MAGIC, None, ALU.add))
            for part in (TP1, TP2, TP3):
                link(dve.scalar_tensor_tensor(a3, u3, -part, a3, ALU.mult, ALU.add))
            link(dve.scalar_tensor_tensor(a3, quarters, math.pi / 2, a3, ALU.mult, ALU.add))
            dve.tensor_scalar(a3, a3, 3.1415925, -3.1415925, ALU.min, ALU.max).then_inc(s["arg_ready"], 1)

            dve.wait_ge(s["text_w_loaded"], 16 * len(text_loads()))

            def text(i, p):
                if (at := tile_at(i, p, 1)) is not None:
                    tile, par = at
                    dve.wait_ge(s["merge_done"], tile + 1)
                    if isinstance(i, int):
                        dve.wait_ge(s["masks_ready"], 2 + N_SEG)
                    dve.tensor_scalar(blend[:, par, :], banks[2 + par][0:TT, 0:D], keep[:, bass.ds(tile, 1), 0], None, ALU.mult).then_inc(s["blend_half"], 1)
                    dve.wait_ge(s["blend_half"], tile + 1)
                    at_least(dve, s["f2T_done"], tile - 1)
                    dve.scalar_tensor_tensor(f2[:, par, 0:D], f1[:, par, 0:D], keep[:, bass.ds(tile, 1), 1], blend[:, par, :], ALU.mult, ALU.add).then_inc(s["merged"], 1)
                if (at := tile_at(i, p, 0)) is not None:
                    tile, par = at
                    dve.wait_ge(s["f1T_done"], tile + 1)
                    at_least(dve, s["merge_done"], tile - 1)
                    dve.tensor_copy(f1T[:, par].rearrange("p c t -> p (c t)"), banks[par][0:C1, 0:2 * TT]).then_inc(s["f1T_ready"], 1)
                if (at := tile_at(i, p, 2)) is not None:
                    tile, par = at
                    dve.wait_ge(s["f2T_done"], tile + 1)
                    at_least(dve, s["feat_done"], tile - 1)
                    dve.tensor_copy(f2T[:, par].rearrange("p c t -> p (c t)"), banks[4 + par][0:C2, 0:2 * TT]).then_inc(s["f2T_ready"], 1)
                if (at := tile_at(i, p, 5)) is not None:
                    tile, par = at
                    dve.wait_ge(s["gelu_done"], tile + 1)
                    at_least(dve, s[f"text_stored{par}"], 16 * (i + (p - 5 - par) // 2))
                    for k in range(N_SEG):
                        ins = dve.scalar_tensor_tensor(txt_h[:, par, :], seg_rows[:, k, :], segm[:, k, bass.ds(tile, 1)], (gelu if k == 0 else txt_h)[:, par, :], ALU.mult, ALU.add)
                        if k < N_SEG - 1:
                            ins.then_inc(s["seg_chain"], 1)
                            dve.wait_ge(s["seg_chain"], tile * (N_SEG - 1) + k + 1)
                        else:
                            ins.then_inc(s["text_ready"], 1)
            def stats_of(k, g, src):
                ln = lns[k]
                for j in range(G):
                    dve.bn_stats(ln["stats"][:, j], src[:, j]).then_inc(s[f"ln{k}_stats"], 1)
                wait_apart(dve, s[f"ln{k}_stats"], (g + 1) * G)
                for j in range(G):
                    dve.bn_aggr(ln["mv"][:, j], ln["stats"][:, j]).then_inc(s[f"ln{k}_mv"], 1)
                dve.wait_ge(s[f"ln{k}_mv"], (g + 1) * G)
                dve.tensor_scalar(ln["var"][:], ln["mv"][:, :, 1], EPS, None, ALU.add).then_inc(s[f"ln{k}_var"], 1)

            def normalise(k, g, dst, src):
                ln = lns[k]
                dve.wait_ge(s[f"ln{k}_rstd"], g + 1)
                for j in range(G):
                    dve.tensor_scalar(dst[:, j], src[:, j], ln["mv"][:, j, 0:1], ln["rstd"][:, j:j + 1], ALU.subtract, ALU.mult).then_inc(s[f"ln{k}_norm"], 1)

            def rest_nT(bank, pair, copies):
                dve.wait_ge(s["nT_hi"], copies)
                at = slice(pair * 2 * SL, (pair + 1) * 2 * SL)
                return dve.tensor_tensor(nT_lo[:].bitcast(F32R)[:, :, at].rearrange("p c (g t) -> p c g t", g=2),
                                         bank[0:HALF, 0:4 * SL].rearrange("p (g c t) -> p c g t", g=2, c=2),
                                         nT[0:HALF, :, at].rearrange("p c (g t) -> p c g t", g=2), ALU.subtract)

            def first_norm():
                dve.wait_ge(s["attn_w_loaded"], 16 * len(attn_loads()))
                dve.tensor_scalar(bq[:], bq[:], DH1 ** -0.5, None, ALU.mult).then_inc(s["attn_vec_ready"], 1)
                dve.wait_ge(s["attn_pool_consts"], 1)
                dve.wait_ge(s["h_loaded"], 32)
                stats_of(0, 0, h_in)
                normalise(0, 0, n0, h_in)
                for pair in range(2):
                    rest_nT(g_bank[pair], pair, pair + 1).then_inc(s[f"fill_free{pair}"], 1)
            text_steps(dve, text, first_norm)

            for par in range(2):
                dve.wait_ge(s[f"text_stored{par}"], 16 * (NT // 2))

            def affine_copy(bank, free, pair, dst, scale, shift):
                for c in range(2):
                    ins = dve.tensor_scalar(dst[:, c, pair * 2 * SL:(pair + 1) * 2 * SL].rearrange("p (g t) -> p g t", g=2),
                                            bank[0:HALF, 0:4 * SL].rearrange("p (g c t) -> p c g t", g=2, c=2)[:, c],
                                            scale[:, c:c + 1], shift[:, c:c + 1], ALU.mult, ALU.add)
                ins.then_inc(free, 1)

            wide3 = [SL, G, E]

            def bc(a):
                return a.unsqueeze(2).broadcast_to(wide3)

            def route(b):
                g, n = b.i - 2, [0]

                def link(ins):
                    n[0] += 1
                    ins.then_inc(s["route"], 1)
                    dve.wait_ge(s["route"], g * ROUTE + n[0])
                bank, free = filled(dve, b, "gate")
                ends = from_end[:].unsqueeze(1).broadcast_to(wide3)
                dve.tensor_tensor(rt["logit"][:], bank[0:SL, 0:G * E].rearrange("p (g e) -> p g e", g=G), gb_row[:].unsqueeze(1).broadcast_to(wide3), ALU.add).then_inc(free, 1)
                evacuated(dve, b, "gate")
                link(dve.tensor_reduce(rc["m1"][:], rt["logit"][:], AX.X, ALU.max))
                link(dve.tensor_tensor(rt["eq"][:], rt["logit"][:], bc(rc["m1"][:]), ALU.is_equal))
                link(dve.tensor_tensor(rt["mark"][:], rt["eq"][:], ends, ALU.mult))
                link(dve.tensor_reduce(rc["i1"][:], rt["mark"][:], AX.X, ALU.max))
                link(dve.tensor_tensor(rt["pick1"][:], bc(rc["i1"][:]), ends, ALU.is_equal))
                link(dve.scalar_tensor_tensor(rt["rest"][:], rt["pick1"][:], NEG, rt["logit"][:], ALU.mult, ALU.add))
                link(dve.tensor_reduce(rc["m2"][:], rt["rest"][:], AX.X, ALU.max))
                dve.tensor_tensor(rc["gap"][:], rc["m2"][:], rc["m1"][:], ALU.subtract).then_inc(s["gap_ready"], 1)
                link(dve.tensor_tensor(rt["eq"][:], rt["rest"][:], bc(rc["m2"][:]), ALU.is_equal))
                link(dve.tensor_tensor(rt["mark"][:], rt["eq"][:], ends, ALU.mult))
                link(dve.tensor_reduce(rc["i2"][:], rt["mark"][:], AX.X, ALU.max))
                link(dve.tensor_tensor(rt["pick2"][:], bc(rc["i2"][:]), ends, ALU.is_equal))
                link(dve.tensor_tensor(rt["sel"][:], rt["pick1"][:], rt["pick2"][:], ALU.add))
                link(dve.tensor_copy(rt["before"][:, 0], runsum[:]))
                for j in range(1, G):
                    link(dve.tensor_tensor(rt["before"][:, j], rt["before"][:, j - 1], rt["sel"][:, j - 1], ALU.add))
                link(dve.tensor_tensor(runsum[:], rt["before"][:, G - 1], rt["sel"][:, G - 1], ALU.add))
                dve.wait_ge(s["ex_ready"], g + 1)
                link(dve.tensor_scalar(rc["den"][:], rc["ex"][:], 1.0, None, ALU.add))
                link(dve.reciprocal(rc["w1"][:], rc["den"][:]))
                link(dve.tensor_tensor(rc["w2"][:], rc["ex"][:], rc["w1"][:], ALU.mult))
                at_least(dve, s["scattered"], g * (16 * TOPK * G))
                link(dve.tensor_copy(rows[:, 0, :, D + 1], rc["w1"][:]))
                link(dve.tensor_copy(rows[:, 1, :, D + 1], rc["w2"][:]))
                link(dve.tensor_copy(rows[:, :, :, D].bitcast(I32), dest0[:]))
                link(dve.tensor_scalar(dest0[:], dest0[:], float(G * S), None, ALU.add))
                bank, free = filled(dve, b, "rank")
                dve.tensor_tensor(rt["pos"][:], bank[0:SL, 0:G * E].rearrange("p (g e) -> p g e", g=G), base_row[0:SL].unsqueeze(1).broadcast_to(wide3), ALU.add).then_inc(free, 1)
                evacuated(dve, b, "rank")
                for k, pick in enumerate(("pick1", "pick2")):
                    link(dve.tensor_tensor(rt["at"][:], rt["pos"][:], rt[pick][:], ALU.mult))
                    link(dve.tensor_reduce(posf[:, k], rt["at"][:], AX.X, ALU.add))
                dve.tensor_copy(posi[:], posf[:]).then_inc(s["pos_ready"], 1)
                assert n[0] == ROUTE, n[0]

            def body(b):
                if b.has_c:
                    for pair in range(2):
                        affine_copy(*filled(dve, b, "h2T", pair), pair, h2T, g2col, b2col)
                if b.has_b:
                    for pair in range(2):
                        affine_copy(*filled(dve, b, "yT", pair), pair, yT, g1col, b1col)
                if b.has_n:
                    dve.wait_ge(s["h_loaded"], (b.i + 2) * 32)
                    stats_of(0, b.i + 1, h_in)
                    dve.wait_ge(s["fill_done"], b.fills_before)
                    normalise(0, b.i + 1, n0, h_in)
                if b.has_c:
                    route(b)
                for step in range(b.steps):
                    k = step
                    if 0 <= k < len(b.units):
                        kind, g, u = b.units[k]
                        dve.wait_ge(s["score_done"], b.units_before + k + 1)
                        at_least(dve, s["et_done"], b.units_before + k - 3)
                        dve.tensor_tensor(score[:, k % 4].rearrange("p a b -> p (a b)"), s_bank[k % 2][0:SL, 0:UH * SL],
                                          (causal if kind == "a" else padded)[:].rearrange("p a b -> p (a b)"), ALU.add).then_inc(s["score_out"], 1)
                        dve.wait_ge(s["score_out"], b.units_before + k + 1)
                        dve.tensor_reduce(smax[:, k % 4], score[:, k % 4], AX.X, ALU.max).then_inc(s["smax_done"], 1)
                    k = step - LAG_PV
                    if 0 <= k < len(b.units):
                        kind, g, u = b.units[k]
                        w = DH1 if kind == "a" else DH2
                        z = z_bank[k % 2][0:SL, 0:UH * (w + 1)].rearrange("p (h e) -> p h e", h=UH)
                        dve.wait_ge(s["pv_done"], b.units_before + k + 1)
                        dve.reciprocal(zinv[:, k % 2], z[:, :, w]).then_inc(s["zinv_done"], 1)
                        dve.wait_ge(s["zinv_done"], b.units_before + k + 1)
                        dst = (z1 if kind == "a" else z2)[:, g % 2, u * UH * w:(u + 1) * UH * w].rearrange("p (h e) -> p h e", h=UH)
                        dve.tensor_tensor(dst, z[:, :, 0:w], zinv[:, k % 2].unsqueeze(2).broadcast_to([SL, UH, w]), ALU.mult).then_inc(s["z_out"], 1)
                    for label in posts_of(b.n, step):
                        if label[0] == "wo":
                            g = label[1]
                            bank, free = filled(dve, b, *label)
                            if g == 0:
                                dve.wait_ge(s["res_ready"], b.i + 1)
                            dve.tensor_tensor(h_res[:, g], bank[0:SL, 0:D], h_res[:, g], ALU.add).then_inc(free, 1)
                        if label[0] == "pj":
                            g = label[1]
                            bank, free = filled(dve, b, *label)
                            if g == 0:
                                dve.wait_ge(s["n1pb_ready"], b.i)
                                at_least(dve, s["r_ready"], (b.i - 1) * G)
                            dve.tensor_tensor(x2[:, g], bank[0:SL, 0:D], n1_pb[:, g], ALU.add).then_inc(free, 1)
                        if label[0] == "nT":
                            bank, free = filled(dve, b, *label)
                            rest_nT(bank, label[1], (b.i + 1) * 2 + label[1] + 1).then_inc(free, 1)
                if b.has_a:
                    evacuated(dve, b, "wo", G - 1)
                    stats_of(1, b.i, h_res)
                if b.has_b:
                    evacuated(dve, b, "pj", G - 1)
                    stats_of(3, b.i - 1, x2)
                if b.has_a:
                    at_least(dve, s["n1pb_ready"], b.i)
                    normalise(1, b.i, n1, h_res)
                    dve.wait_ge(s["ln1_norm"], (b.i + 1) * G)
                    stats_of(2, b.i, n1)
                if b.has_b:
                    at_least(dve, s["scattered"], (b.i - 1) * (16 * TOPK * G))
                    at_least(dve, s["rows_copied"], b.i - 1)
                    normalise(3, b.i - 1, rows[:, 0, :, 0:D], x2)
                if b.has_a:
                    normalise(2, b.i, y0, n1)
            attn_bodies(dve, body)

            links = [0]

            def link(ins):
                links[0] += 1
                ins.then_inc(s["tables"], 1)
                dve.wait_ge(s["tables"], links[0])
            link(dve.memset(tb["one"][:], 1.0))
            dve.wait_ge(s["counts_done"], 1)
            link(dve.tensor_copy(counts[:], s_bank[0][:, 0:E]))
            link(dve.tensor_tensor(tail_row[:], counts[0:1, :], base_row[0:1, :], ALU.add))
            link(dve.tensor_scalar(tb["x"][:], counts[0:1, :], 1 / 128, 127 / 256, ALU.mult, ALU.add))
            link(dve.tensor_scalar(tb["up"][:], tb["x"][:], MAGIC, None, ALU.add))
            link(dve.tensor_scalar(tb["whole"][:], tb["up"][:], -MAGIC, None, ALU.add))
            link(dve.tensor_scalar(tb["nt"][:], tb["whole"][:], 1.0, None, ALU.max))
            link(dve.tensor_tensor_scan(tb["end"][:], tb["one"][:], tb["nt"][:], 0.0, ALU.mult, ALU.add))
            link(dve.tensor_scalar(tb["jump"][:], tb["nt"][:], -128.0, float(REGION), ALU.mult, ALU.add))
            w54 = [1, NTILE, E]
            link(dve.tensor_tensor(past, tt_["t"][:].unsqueeze(2).broadcast_to(w54), tb["end"][:].unsqueeze(1).broadcast_to(w54), ALU.is_ge))
            link(dve.tensor_reduce(tt_["e"][:], past, AX.X, ALU.add))
            link(dve.tensor_scalar(tile_expert[:], tt_["e"][:], float(E - 1), None, ALU.min))
            link(dve.tensor_tensor(jumps, past, tb["jump"][:].unsqueeze(1).broadcast_to(w54), ALU.mult))
            link(dve.tensor_reduce(tt_["s"][:], jumps, AX.X, ALU.add))
            link(dve.scalar_tensor_tensor(tile_row[:], tt_["t"][:], 128.0, tt_["s"][:], ALU.mult, ALU.add))
            dve.memset(tb["x"][:], 0.0).then_inc(s["tables_ready"], 1)
            dve.wait_ge(s["tables_ready"], 1)
            dve.memset(tb["up"][:], 0.0).then_inc(s["attn_end"], 1)

            dve.wait_ge(s["attn_end"], 1)
            dve.wait_ge(s["r_stored"], 16 * NG)
            for k in range(2):
                dve.memset(xT[HALF:HALF + 1, k, 1, :], 1.0).then_inc(s["moe_ones"], 1)

            def features(tile, par):
                dve.wait_ge(s["xT_done"], tile + 1)
                at_least(dve, s["up_done1"], tile - 1)
                for c in range(2):
                    ins = dve.tensor_scalar(xT[0:HALF, par, c, :], banks[par][0:HALF, c * 128:(c + 1) * 128], g2col[:, c:c + 1], b2col[:, c:c + 1], ALU.mult, ALU.add)
                ins.then_inc(s["xT_ready"], 1)

            features(0, 0)
            copy_w1(dve, dve.tensor_copy, 0, -1, 3)

            def expert(i, p):
                if (at := xtile_at(i, p, -1)) is not None:
                    features(at[0], at[1] % 2)
                copy_w1(dve, dve.tensor_copy, 0, i, p)
                if (at := xtile_at(i, p, 1)) is not None:
                    tile, place = at
                    e = dve.value_load(tile_expert[0:1, bass.ds(tile, 1)], min_val=0, max_val=E - 1)
                    dve.wait_ge(s["down_done"], tile + 1)
                    dve.tensor_tensor(y_raw[:, place % 2, :], banks[6 + place % 2][:, 0:D], expert_cols(e, W_COLS - D, D), ALU.add).then_inc(s["y_biased"], 1)
                    dve.wait_ge(s["y_biased"], tile + 1)
                    at_least(dve, s[f"y_stored{place % 2}"], half_count(i, p, 1) * 16)
                    dve.tensor_scalar(y_row[:, place % 2, :], y_raw[:, place % 2, :], xt[:, place, D + 1:D + 2], None, ALU.mult).then_inc(s["y_ready"], 1)
            expert_steps(dve, expert)

            for k in range(NP_):
                dve.wait_ge(s[f"r_loaded{k}"], 16)
                dve.wait_ge(s[f"ya_loaded{k}"], 16)
                dve.tensor_tensor(last_ya[:, k], last_ya[:, k], last_r[:, k], ALU.add).then_inc(s["last_chain"], 1)
                dve.wait_ge(s["last_chain"], k + 1)
                dve.wait_ge(s[f"yb_loaded{k % 2}"], 16 * (k // 2 + 1))
                dve.tensor_tensor(last_ya[:, k], last_ya[:, k], last_yb[:, k % 2], ALU.add).then_inc(s["last_out"], 1)

        @block.tensor
        def _(pe):
            pe.wait_ge(s["ident_ready"], 1)
            pe.wait_ge(s["tok_staged"], 2)
            pe.wait_ge(s["order_loaded"], 16)
            for k in range(7):
                ins = pe.transpose(banks[0][0:TT, k * NT:(k + 1) * NT], tok_f[:, k, :], ident[0:NT, 0:NT])
            ins.then_inc(s["tokT_done"], 1)

            pe.wait_ge(s["img_loaded"], 16 * 4 * (IMG // PATCH))
            pe.wait_ge(s["img_w_loaded"], 16 * len(img_loads()))
            pe.wait_ge(s["img_sel_ready"], 1)
            for k in range(4):
                for h in range(2):
                    at_least(pe, s["patchT_out"], 2 * k + h - 1)
                    for c in range(3):
                        ins = pe.transpose(t_bank[h][:, c * 128:(c + 1) * 128], xpatch[:, k, (3 * h + c) * 128:(3 * h + c + 1) * 128], ident[:])
                    ins.then_inc(s["patchT_done"], 1)
                pe.wait_ge(s["patchT_out"], 2 * k + 2)
                at_least(pe, s["img_ready"], k - 1)
                for c in range(KP // 128):
                    pe.matmul(banks[2 + k % 2][:, 0:D], patchT[:, k % 2, c, :], w_img[:, c, :], start=c == 0, stop=False)
                ins = pe.matmul(banks[2 + k % 2][:, 0:D], img_sel[:], img_add[:], start=False, stop=True)
                ins.then_inc(s["img_done"], 1)
            pe.wait_ge(s["img_ready"], 4)
            pe.wait_ge(s["tok_ready"], 1)
            pe.wait_ge(s["text_w_loaded"], 16 * len(text_loads()))

            def text(i, p):
                if (at := tile_at(i, p, 1)) is not None:
                    tile, par = at
                    pe.wait_ge(s["f1T_ready"], tile + 1)
                    at_least(pe, s["merged"], tile - 1)
                    for c in range(2):
                        ins = pe.matmul(banks[2 + par][0:TT, 0:D], f1T[:, par, c, :], w_merge[:, c, :], start=c == 0, stop=c == 1)
                    ins.then_inc(s["merge_done"], 1)
                if (at := tile_at(i, p, 0)) is not None:
                    tile, par = at
                    pe.wait_ge(s["f1_ready"], tile + 1)
                    at_least(pe, s["f1T_ready"], tile - 1)
                    for c in range(2):
                        ins = pe.transpose(banks[par][0:C1, c * TT:(c + 1) * TT], f1[:, par, c * C1:(c + 1) * C1], ident[0:TT, 0:TT])
                    ins.then_inc(s["f1T_done"], 1)
                if (at := tile_at(i, p, 2)) is not None:
                    tile, par = at
                    pe.wait_ge(s["merged"], tile + 1)
                    pe.wait_ge(s["sines_copied"], tile + 1)
                    at_least(pe, s["f2T_ready"], tile - 1)
                    for c in range(2):
                        ins = pe.transpose(banks[4 + par][0:C2, c * TT:(c + 1) * TT], f2[:, par, c * C2:(c + 1) * C2], ident[0:TT, 0:TT])
                    ins.then_inc(s["f2T_done"], 1)
                if (at := tile_at(i, p, 3)) is not None:
                    tile, par = at
                    pe.wait_ge(s["f2T_ready"], tile + 1)
                    at_least(pe, s["gelu_done"], tile - 1)
                    for c in range(2):
                        ins = pe.matmul(banks[6 + par][0:TT, 0:D], f2T[:, par, c, :], w_feat[:, c, :], start=c == 0, stop=c == 1)
                    ins.then_inc(s["feat_done"], 1)

            def turn_pair(bank, src, pair):
                for j in range(2):
                    for c in range(2):
                        ins = pe.transpose(bank[0:HALF, (2 * j + c) * SL:(2 * j + c + 1) * SL], src[:, 2 * pair + j, c * HALF:(c + 1) * HALF], ident[0:SL, 0:SL])
                return ins

            def in_parts(to, products, first, last):
                for k, (a, b) in enumerate(products):
                    ins = pe.matmul(to, a.bitcast(F32R), b.bitcast(F32R), start=first and k == 0, stop=last and k == len(products) - 1)
                return ins

            def first_turns():
                pe.wait_ge(s["f1T_ready"], NT)
                pe.wait_ge(s["ln0_norm"], G)
                for pair in range(2):
                    turn_pair(g_bank[pair], n0, pair).then_inc(s["fill_done"], 1)
            text_steps(pe, text, first_turns)

            pe.wait_ge(s["gelu_done"], NT)
            pe.wait_ge(s["attn_w_loaded"], 16 * len(attn_loads()))
            pe.wait_ge(s["attn_pool_consts"], 1)
            pe.wait_ge(s["attn_vec_ready"], 1)
            pe.wait_ge(s["weights_split"], 1)

            def open_fill(b, *label, reads=()):
                bank, _, before = b.fill(*label)
                pe.wait_ge(s[f"fill_free{bank}"], before)
                for other in reads:
                    if b.fill(*other)[0] != bank:
                        evacuated(pe, b, *other)
                return g_bank[bank]

            def body(b):
                if b.has_a:
                    for bank in range(2):
                        pe.wait_ge(s[f"fill_free{bank}"], b.bank_fills_before)
                    for k in range(PAIRS):
                        cols = slice(k * 128, (k + 1) * 128)
                        for w, high, low in (("q", wq_hi, wq_lo), ("k", wk_hi, wk_lo)):
                            bank = open_fill(b, w, k)
                            for c in range(2):
                                ins = in_parts(bank[:, 0:GT], [(high[:, c, cols], nT[0:HALF, c, :]), (low[:, c, cols], nT[0:HALF, c, :]),
                                                               (high[:, c, cols], nT_lo[:, c, :])], c == 0, c == 1)
                            ins.then_inc(s["fill_done"], 1)
                if b.has_c:
                    pe.wait_ge(s["ln3_norm"], (b.i - 1) * G)
                    for pair in range(2):
                        turn_pair(open_fill(b, "h2T", pair), rows[:, 0], pair).then_inc(s["fill_done"], 1)
                if b.has_b:
                    pe.wait_ge(s["ln2_norm"], b.i * G)
                    for pair in range(2):
                        turn_pair(open_fill(b, "yT", pair), y0, pair).then_inc(s["fill_done"], 1)
                if b.has_a:
                    for g in range(G):
                        for h in range(2):
                            bank = open_fill(b, "v", g, h)
                            own, cols = slice(g * SL, (g + 1) * SL), slice(h * 6 * DH1, (h + 1) * 6 * DH1)
                            for c in range(2):
                                rows_c = slice(0, HALF + c)
                                ins = in_parts(bank[0:SL, 0:6 * DH1], [(nT[rows_c, c, own], wv_hi[rows_c, c, cols]), (nT[rows_c, c, own], wv_lo[rows_c, c, cols]),
                                                                       (nT_lo[:, c, own], wv_hi[0:HALF, c, cols])], c == 0, c == 1)
                            ins.then_inc(s["fill_done"], 1)
                if b.has_c:
                    bank = open_fill(b, "gate", reads=[("h2T", 0), ("h2T", 1)])
                    for g in range(G):
                        for c in range(2):
                            ins = pe.matmul(bank[0:SL, g * E:(g + 1) * E], h2T[:, c, g * SL:(g + 1) * SL], wgate[:, c, :], start=c == 0, stop=c == 1)
                    ins.then_inc(s["fill_done"], 1)
                if b.has_b:
                    for k in range(SIXES):
                        for j, w in enumerate(("q2", "k2")):
                            bank = open_fill(b, w, k, reads=[("yT", 0), ("yT", 1)] if (w, k) == ("q2", 0) else [])
                            for c in range(2):
                                ins = pe.matmul(bank[0:HALF, 0:GT], wqkv2[:, c, j * D + k * HALF:j * D + (k + 1) * HALF], yT[:, c, :], start=c == 0, stop=c == 1)
                            ins.then_inc(s["fill_done"], 1)
                    for pair in range(2):
                        bank = open_fill(b, "v2", pair)
                        for j in range(2):
                            g = 2 * pair + j
                            for c in range(2):
                                ins = pe.matmul(bank[0:SL, j * D:(j + 1) * D], yT[:, c, g * SL:(g + 1) * SL], wqkv2[:, c, 2 * D:], start=c == 0, stop=c == 1)
                        ins.then_inc(s["fill_done"], 1)
                if b.has_c:
                    pe.wait_ge(s["route"], (b.i - 2) * ROUTE + ROUTE_SEL)
                    bank = open_fill(b, "rank")
                    pe.matmul(bank[0:SL, 0:G * E], earlier[:], rt["sel"][:].rearrange("p a b -> p (a b)"), start=True, stop=False)
                    pe.matmul(bank[0:SL, 0:G * E], ones_first[:, 0:SL], rt["before"][:].rearrange("p a b -> p (a b)"), start=False, stop=True).then_inc(s["fill_done"], 1)

                for step in range(b.steps):
                    k = step
                    if k < len(b.units):
                        kind, g, u = b.units[k]
                        if k == 0:
                            for last in range(2):
                                evacuated(pe, b, *(("v2", last) if b.has_b else ("v", G - 1, last)))
                        at_least(pe, s["score_out"], b.units_before + k - 1)
                        bank = s_bank[k % 2]
                        if kind == "a":
                            for j in range(2):
                                c = 2 * u + j
                                ins = pe.matmul(bank[0:SL, j * 2 * SL:(j + 1) * 2 * SL], qT[:, c, g * SL:(g + 1) * SL],
                                                kbd[:, c, g].rearrange("p a b -> p (a b)"), start=True, stop=True)
                        else:
                            for c in range(SIXES):
                                first, end = max(u * UH, c * 6), min((u + 1) * UH, (c + 1) * 6)
                                if first < end:
                                    ins = pe.matmul(bank[0:SL, (first - u * UH) * SL:(end - u * UH) * SL], q2T[:, c, g * SL:(g + 1) * SL],
                                                    k2bd[:, first:end, g, :], start=True, stop=True)
                        ins.then_inc(s["score_done"], 1)
                    k = step - LAG_T
                    if 0 <= k < len(b.units):
                        pe.wait_ge(s["exp_done"], b.units_before + k + 1)
                        at_least(pe, s["et_out"], b.units_before + k - 1)
                        for h in range(UH):
                            ins = pe.transpose(t_bank[k % 2][0:SL, h * SL:(h + 1) * SL], score[:, k % 4, h, :], ident[0:SL, 0:SL])
                        ins.then_inc(s["et_done"], 1)
                    k = step - LAG_PV
                    if 0 <= k < len(b.units):
                        kind, g, u = b.units[k]
                        v, w = (v1, DH1 + 1) if kind == "a" else (v2, DH2 + 1)
                        pe.wait_ge(s["et_out"], b.units_before + k + 1)
                        at_least(pe, s["z_out"], b.units_before + k - 1)
                        for h in range(UH):
                            ins = pe.matmul(z_bank[k % 2][0:SL, h * w:(h + 1) * w], eT[:, k % 2, h * SL:(h + 1) * SL], v[:, g, u * UH + h, :], start=True, stop=True)
                        ins.then_inc(s["pv_done"], 1)
                    for label in posts_of(b.n, step):
                        what, g = label[0], label[1]
                        bank = open_fill(b, *label, reads={"wo": [("zT", g, 0), ("zT", g, 1)], "pj": [("z2T", g)]}.get(what, []))
                        if what == "zT":
                            pe.wait_ge(s["z_out"], b.units_before + b.units.index(("a", g, UN - 1)) + 1)
                            for j in range(3):
                                c = 3 * label[2] + j
                                ins = pe.transpose(bank[:, j * SL:(j + 1) * SL], z1[:, g % 2, c * 128:(c + 1) * 128], ident[0:SL, 0:SL])
                        elif what == "z2T":
                            pe.wait_ge(s["z_out"], b.units_before + b.units.index(("b", g, UN - 1)) + 1)
                            for c in range(2):
                                ins = pe.transpose(bank[0:HALF, c * SL:(c + 1) * SL], z2[:, g % 2, c * HALF:(c + 1) * HALF], ident[0:SL, 0:SL])
                        elif what == "nT":
                            pe.wait_ge(s["ln0_norm"], (b.i + 2) * G)
                            ins = turn_pair(bank, n0, g)
                        elif what == "wo":
                            for c in range(PAIRS):
                                ins = pe.matmul(bank[0:SL, 0:D], z1T[:, c, :], wo[:, c, :], start=c == 0, stop=c == PAIRS - 1)
                        else:
                            for c in range(2):
                                ins = pe.matmul(bank[0:SL, 0:D], z2T[:, c, :], wp2[:, c, :], start=c == 0, stop=c == 1)
                        ins.then_inc(s["fill_done"], 1)
            attn_bodies(pe, body)

            pe.wait_ge(s["route"], NG * ROUTE)
            pe.matmul(s_bank[0][:, 0:E], ones_first[:], runsum[:], start=True, stop=True).then_inc(s["counts_done"], 1)

            pe.wait_ge(s["moe_ones"], 2)

            def turn_rows(tile, place, loads):
                pe.wait_ge(s[f"xt_loaded{place}"], loads * 16)
                at_least(pe, s["xT_ready"], tile - 1)
                for c in range(2):
                    ins = pe.transpose(banks[place % 2][0:HALF, c * 128:(c + 1) * 128], xt[:, place, c * HALF:(c + 1) * HALF], ident[:])
                ins.then_inc(s["xT_done"], 1)
            turn_rows(0, 0, 1)

            def expert(i, p):
                tile = i * 4 + p
                if xtile_at(i, p, 0) is not None:
                    pe.wait_ge(s["xT_ready"], tile + 1)
                    for h in range(2):
                        pe.wait_ge(s[f"w1_copied{h}"], tile + 1)
                        at_least(pe, s[f"hid_ready{h}"], tile)
                        for j in range(3):
                            first = (3 * h + j) * 128
                            for c in range(2):
                                ins = pe.matmul(banks[2 + h][:, j * 128:(j + 1) * 128], w1_now[0:HALF + c, p % 2, c, first:first + 128],
                                                xT[0:HALF + c, p % 2, c, :], start=c == 0, stop=c == 1)
                        ins.then_inc(s[f"up_done{h}"], 1)
                if (at := xtile_at(i, p, -1)) is not None:
                    turn_rows(*at, i + (1 if p < 3 else 2))
                if xtile_at(i, p, 1) is not None:
                    par = (p - 1) % 2
                    e = pe.value_load(tile_expert[0:1, bass.ds(tile - 1, 1)], min_val=0, max_val=E - 1)
                    for h in range(2):
                        pe.wait_ge(s[f"hid_ready{h}"], tile)
                    at_least(pe, s["y_biased"], tile - 2)
                    for c in range(FF // 128):
                        ins = pe.matmul(banks[6 + par][:, 0:D], hidT[:, par, c * 128:(c + 1) * 128],
                                        expert_cols(e, 2 * FF + c * D, D), start=c == 0, stop=c == FF // 128 - 1)
                    ins.then_inc(s["down_done"], 1)
            expert_steps(pe, expert)


_INS = """x x_txt itok_BS_0_99 itok_BS_1_36498 itok_BS_0_2047 fside_BS_concept_values mask_BS_f1_0 mask_BS_i2_0 L0_tok_W L0_tok_b
L0_tok_pos_emb L0_txt_concept_emb L0_txt_segment_emb L0_txt_w_age L0_txt_phi_age L0_txt_merge_w L0_txt_merge_b L0_txt_proj_w
L0_txt_proj_b L0_attn_W_Q L0_attn_b_Q L0_attn_W_K L0_attn_b_K L0_attn_W_V L0_attn_b_V L0_attn_W_O L0_attn_b_O L0_ffn_ln1_g
L0_ffn_ln1_b L0_ffn_qkv_w L0_ffn_proj_w L0_ffn_proj_b L0_ffn_ln2_g L0_ffn_ln2_b L0_ffn_gate_w L0_ffn_gate_b L0_ffn_w1 L0_ffn_b1
L0_ffn_w2 L0_ffn_b2""".split()


def kernel(**inputs):
    import numpy as _np
    import concourse.bacc as _bacc
    from concourse import mybir as _mybir
    from concourse.bass_utils import run_bass_kernel_spmd as _run

    nc = _bacc.Bacc("TRN2", target_bir_lowering=False, num_devices=1)
    arrays, args = {}, {}

    def give(name, a):
        arrays[f"in_{name}"] = a
        args[name] = nc.dram_tensor(f"in_{name}", a.shape, _mybir.dt.from_np(a.dtype), kind="ExternalInput").ap()
    for name in _INS:
        give(name, _np.ascontiguousarray(inputs[name]))
    freq = _np.exp(_np.arange(0, T_EMB, 2, dtype=_np.float32) * (-math.log(10000.0) / T_EMB)).astype(_np.float32)
    give("pos_freq", _np.repeat(freq, 2)[None, :])
    quarter = _np.zeros((1, 3 * T_EMB), _np.float32)
    quarter[0, 2 * T_EMB + 1::2] = 1.0
    give("quarter", quarter)
    out = nc.dram_tensor("out_0", (B, S, D), _mybir.dt.float32, kind="ExternalOutput").ap()
    program(nc, args, out)
    r = _run(nc, [arrays], core_ids=[0])
    return r.results[0]["out_0"]
```

```python
import math
from contextlib import ExitStack

import numpy as np

import concourse.bass as bass
from concourse import mybir

ALU = mybir.AluOpType
ACT = mybir.ActivationFunctionType
AX = mybir.AxisListType
F32 = mybir.dt.float32
I32 = mybir.dt.int32
F32R = mybir.dt.float32r

B, S_TXT, N_PATCH = 32, 77, 16
S = S_TXT + N_PATCH
D = 192
HALF = D // 2
N_SEG, T_EMB, MAX_POS = 3, 16, 512
HEADS, DH1, DH2 = 12, 64, 16
E, FF = 8, 768
EPS = 1e-5
NEG = -1e30

TT = 112
NT = B * S_TXT // TT
assert NT * TT == B * S_TXT
PEEL = 8
PATCH, IMG = 16, 64
KP = PATCH * PATCH * 3
F1W = D + 2
F2W = D + 3 * T_EMB + 2
C1, C2 = F1W // 2, F2W // 2

G = 4
NG = B // G
SL = 96
GT = G * SL
UH = 4
UN = HEADS // UH
PAIRS = HEADS * DH1 // 128
SIXES = 2

TOPK = 2
ROW = D + 2
REGION = -(-(B * S + 128) // 128) * 128
SLOTS = TOPK * B * S
NTILE = -(-SLOTS // 128) + E - 1 + (-(-SLOTS // 128) + E - 1) % 2
W_COLS = 2 * FF + FF // 128 * D + D
SPARE = NTILE - SLOTS // 128 + 1
XS_ROWS = E * REGION + SPARE * 128
Y_ROWS = SLOTS + (E + SPARE) * 128

LP, CJ = 124, 6
NP_ = B * S // (LP * CJ)

ROUTE = 28
ROUTE_SEL = 17

MAGIC = 1.5 * 2.0 ** 23
TP1 = 6.28125
TP2 = math.floor((2 * math.pi - TP1) * 2 ** 18) / 2 ** 18
TP3 = 2 * math.pi - TP1 - TP2


def at_least(eng, sem, value):
    if not isinstance(value, int) or value > 0:
        eng.wait_ge(sem, value)


class Body:

    def __init__(self, n, i):
        self.n, self.i = n, i
        self.has_a, self.has_b, self.has_c, self.has_n = parts_of(n)
        self.front, self.posts, self.units = front_of(n), all_posts_of(n), units_of(n)
        assert len(self.front) % RING == 0 and len(self.posts) % 2 == 0
        self.steps = len(self.units) + LAG_PROJ + 2
        self.units_before = count_before(n, i, units_of, 1)
        fronts, posts = count_before(n, i, front_of, RING), count_before(n, i, all_posts_of, 2)
        self.fills_before = fronts * RING + posts * 2 + 2
        self.bank_fills_before = [fronts + (posts + 1 if bank < 2 else 0) for bank in range(RING)]

    def fill(self, *label):
        if label in self.front:
            k = self.front.index(label)
            return k % RING, self.fills_before + k, self.bank_fills_before[k % RING] + k // RING
        k = self.posts.index(label)
        return k % 2, self.fills_before + len(self.front) + k, self.bank_fills_before[k % 2] + len(self.front) // RING + k // 2


RING = 4
FIRST_FULL, LAST_FULL = 2, NG - 2
LAG_T, LAG_PV, LAG_PROJ = 3, 4, 6


def parts_of(n):
    return n < NG, 1 <= n <= NG, n >= 2, n < NG - 1


def count_before(n, i, of, per):
    first = sum(len(of(m)) for m in range(n)) // per
    if isinstance(i, int):
        return first
    each = len(of(n)) // per
    return i * each + (first - n * each)


def units_of(n):
    a, b, _, _ = parts_of(n)
    return [(kind, g, u) for g in range(G) for u in range(UN) for kind, on in (("a", a), ("b", b)) if on]


def posts_of(n, step):
    units, found = units_of(n), []
    for lag in (LAG_PROJ + 1, LAG_PROJ):
        k = step - lag
        if 0 <= k < len(units) and units[k][2] == UN - 1:
            kind, g, _ = units[k]
            if lag == LAG_PROJ:
                found += [("zT", g, 0), ("zT", g, 1)] if kind == "a" else [("z2T", g)]
            else:
                found += [("wo", g)] if kind == "a" else [("pj", g)]
    for k, after in enumerate((("zT", G - 1, 1), ("wo", G - 1))):
        if parts_of(n)[3] and after in found:
            found += [("nT", k)]
    return found


def front_of(n):
    a, b, c, _ = parts_of(n)
    part = {"q": a, "k": a, "v": a, "yT": b, "q2": b, "k2": b, "v2": b, "h2T": c, "gate": c, "rank": c}
    f = [(w, k) for k in range(PAIRS) for w in ("q", "k")]
    f += [("v", 0, 0), ("v", 0, 1), ("h2T", 0), ("v", 1, 0), ("h2T", 1), ("v", 1, 1), ("yT", 0), ("v", 2, 0), ("yT", 1), ("v", 2, 1),
          ("gate",), ("v", 3, 0), ("q2", 0), ("k2", 0), ("v", 3, 1), ("q2", 1), ("rank",), ("k2", 1), ("v2", 0), ("v2", 1)]
    return [label for label in f if part[label[0]]]


def all_posts_of(n):
    return [label for step in range(len(units_of(n)) + LAG_PROJ + 2) for label in posts_of(n, step)]


def program(nc, t, out):
    def dram(name, shape):
        return nc.dram_tensor(name, shape, F32, kind="Internal").ap()

    txt_d = dram("txt_d", [B * S_TXT, D])
    img_d = dram("img_d", [B * N_PATCH, D])
    ord_d = dram("ord_d", [B, S_TXT])
    r_d = dram("r_d", [B * S, D])
    xs_d = dram("xs_d", [XS_ROWS, ROW])
    y_d = dram("y_d", [Y_ROWS, D])

    ctx = ExitStack()
    with ctx:
        scope = [ctx]

        def sb(name, shape, dt=F32):
            return scope[0].enter_context(nc.sbuf_tensor(name, shape, dt))

        def sem(name):
            return ctx.enter_context(nc.semaphore(name))

        banks = [ctx.enter_context(nc.psum_tensor(f"bank{k}", [128, 512], F32)) for k in range(8)]

        ident = sb("ident", [128, 128])
        zero_rows = sb("zero_rows", [128, max(E, SPARE), ROW])
        tail_row = sb("tail_row", [1, E], I32)
        rows = sb("rows", [SL, TOPK, G, ROW])
        posi = sb("posi", [SL, TOPK, G], I32)
        counts = sb("counts", [128, E])
        tile_expert = sb("tile_expert", [1, NTILE], I32)
        tile_row = sb("tile_row", [1, NTILE], I32)
        ones_first = sb("ones_first", [SL, 128])
        g2col = sb("g2col", [HALF, 2])
        b2col = sb("b2col", [HALF, 2])
        base_row = sb("base_row", [128, E])

        weights_scope = ctx.enter_context(ExitStack())
        scope[0] = weights_scope
        (wq_hi, wq_lo), (wk_hi, wk_lo), (wv_hi, wv_lo) = (
            [sb(f"{n}_{part}", [HALF + more, 2, HEADS * DH1]) for part in ("hi", "lo")] for n, more in (("wq", 0), ("wk", 0), ("wv", 1)))
        wo = sb("wo", [128, PAIRS, D])
        bq, bk = sb("bq", [128, PAIRS]), sb("bk", [128, PAIRS])
        wqkv2, wp2 = sb("wqkv2", [HALF, 2, 3 * D]), sb("wp2", [HALF, 2, D])
        wgate = sb("wgate", [HALF, 2, E])
        g1col, b1col = sb("g1col", [HALF, 2]), sb("b1col", [HALF, 2])
        bo_row, pb_row = sb("bo_row", [SL, D]), sb("pb_row", [SL, D])
        gb_row = sb("gb_row", [SL, E])
        causal, padded = sb("causal", [SL, UH, SL]), sb("padded", [SL, UH, SL])
        earlier = sb("earlier", [SL, SL])
        head_rows = sb("head_rows", [HALF, HEADS // SIXES])
        neg_half = sb("neg_half", [SL, G])
        from_end = sb("from_end", [SL, E])
        dest0 = sb("dest0", [SL, G, TOPK])
        h_in = sb("h_in", [SL, G, D])
        nT = sb("nT", [HALF + 1, 2, GT])
        v1 = sb("v1", [SL, G, HEADS, DH1 + 1])
        k2bd = sb("k2bd", [HALF, HEADS, G, SL])
        v2 = sb("v2", [SL, G, HEADS, DH2 + 1])
        runsum = sb("runsum", [SL, E])
        lns = [{"stats": sb(f"ln{k}_stats", [SL, G, 6]), "mv": sb(f"ln{k}_mv", [SL, G, 2]),
                "var": sb(f"ln{k}_var", [SL, G]), "rstd": sb(f"ln{k}_rstd", [SL, G])} for k in range(4)]
        tb = {n: sb(f"tb_{n}", [1, E]) for n in ("x", "up", "whole", "nt", "end", "jump", "one")}
        tt_ = {n: sb(f"tt_{n}", [1, NTILE]) for n in ("t", "e", "s")}

        image_scope = ctx.enter_context(ExitStack())
        scope[0] = image_scope
        xpatch = sb("xpatch", [128, 4, KP])
        w_img = sb("w_img", [128, KP // 128, D])
        patchT = sb("patchT", [128, 2, KP // 128, 128])
        img_h = sb("img_h", [128, 4, D])
        image_scope.close()
        whole_scope = ctx.enter_context(ExitStack())
        scope[0] = whole_scope
        wq, wk_, wv = sb("wq", [HALF, 2, HEADS * DH1]), sb("wk", [HALF, 2, HEADS * DH1]), sb("wv", [HALF + 1, 2, HEADS * DH1])
        whole_scope.close()
        scope[0] = weights_scope
        kbd = sb("kbd", [128, PAIRS, G, 2, SL])
        nT_lo = sb("nT_lo", [HALF, 2, GT])
        n0 = sb("n0", [SL, G, D])
        filler = sb("filler", [128, 4 * KP + KP // 128 * D + 2 * KP + 4 * D - PAIRS * G * 2 * SL - 2 * GT - G * D])

        text_scope = ctx.enter_context(ExitStack())
        scope[0] = text_scope
        img_add = sb("img_add", [N_PATCH + 1, D])
        img_sel = sb("img_sel", [N_PATCH + 1, 128])
        tok_i = sb("tok_i", [NT, 4, TT], I32)
        tok_f = sb("tok_f", [NT, 7, TT])
        tok = sb("tok", [TT, 7, NT])
        ids = sb("ids", [TT, NT], I32)
        keep = sb("keep", [TT, NT, 2])
        segm = sb("segm", [TT, N_SEG, NT])
        vco_i = sb("vco_i", [B, S_TXT], I32)
        vco = sb("vco", [B, S_TXT])
        vmin = sb("vmin", [B, 1])
        order = sb("order", [B, S_TXT])
        frow = sb("frow", [TT, 3, T_EMB])
        prow = sb("prow", [TT, 3, T_EMB])
        qrow = sb("qrow", [TT, 3, T_EMB])
        arg = sb("arg", [TT, NT, 3 * T_EMB])
        turns = sb("turns", [TT, NT, 3 * T_EMB])
        f1all = sb("f1all", [TT, NT, F1W])
        f1 = sb("f1", [TT, 2, F1W])
        f1T = sb("f1T", [C1, 2, 2, TT])
        f2 = sb("f2", [TT, 2, F2W])
        f2T = sb("f2T", [C2, 2, 2, TT])
        blend = sb("blend", [TT, 2, D])
        gelu = sb("gelu", [TT, 2, D])
        txt_h = sb("txt_h", [TT, 2, D])
        w_merge = sb("w_merge", [C1, 2, D])
        w_feat = sb("w_feat", [C2, 2, D])
        seg_rows = sb("seg_rows", [TT, N_SEG, D])
        text_scope.close()

        attn_scope = ctx.enter_context(ExitStack())
        scope[0] = attn_scope
        h_res = sb("h_res", [SL, G, D])
        n1 = sb("n1", [SL, G, D])
        y0 = sb("y0", [SL, G, D])
        n1_pb = sb("n1_pb", [SL, G, D])
        h_keep = sb("h_keep", [SL, G, D])
        x2 = sb("x2", [SL, G, D])
        yT = sb("yT", [HALF, 2, GT])
        h2T = sb("h2T", [HALF, 2, GT])
        qT = sb("qT", [128, PAIRS, GT])
        q2T = sb("q2T", [HALF, SIXES, GT])
        score = sb("score", [SL, 4, UH, SL])
        smax = sb("smax", [SL, 4, UH])
        eT = sb("eT", [SL, 2, UH * SL])
        zinv = sb("zinv", [SL, 2, UH])
        z1 = sb("z1", [SL, 2, HEADS * DH1])
        z2 = sb("z2", [SL, 2, D])
        z1T = sb("z1T", [128, PAIRS, SL])
        z2T = sb("z2T", [HALF, 2, SL])
        rt = {n: sb(f"rt_{n}", [SL, G, E]) for n in ("logit", "eq", "mark", "pick1", "rest", "pick2", "sel", "before", "pos", "at")}
        rc = {n: sb(f"rc_{n}", [SL, G]) for n in ("m1", "i1", "m2", "i2", "gap", "ex", "den", "w1", "w2")}
        posf = sb("posf", [SL, TOPK, G])
        q_flat = qT[0:1].rearrange("p a b -> p (a b)")
        past, jumps = (q_flat[:, k * NTILE * E:(k + 1) * NTILE * E].rearrange("p (t e) -> p t e", e=E) for k in range(2))
        attn_scope.close()
        weights_scope.close()

        moe_scope = ctx.enter_context(ExitStack())
        scope[0] = moe_scope
        xt = sb("xt", [128, 4, ROW])
        xT = sb("xT", [HALF + 1, 2, 2, 128])
        w1_now = sb("w1_now", [HALF + 1, 2, 2, FF])
        w2_now = sb("w2_now", [128, 2, FF // 128 * D])
        hidT = sb("hidT", [128, 2, FF])
        y_raw = sb("y_raw", [128, 2, D])
        y_row = sb("y_row", [128, 2, D])
        last_r, last_ya = sb("last_r", [LP, NP_, CJ, D]), sb("last_ya", [LP, NP_, CJ, D])
        last_yb = sb("last_yb", [LP, 2, CJ, D])
        experts_w = sb("experts_w", [128, E, W_COLS])
        moe_scope.close()

        s = {n: sem(n) for n in """vco_loaded tokens_loaded sine_rows_loaded text_w_loaded img_loaded
            order_chain order_stored order_loaded img_w_loaded img_sel_ready tok_staged tokT_done tok_ready ids_ready masks_ready arg_chain arg_ready sines_ready
            f1_cols_ready gathered_first gathered_rest ident_ready pool_chain pool_consts attn_pool_consts
            patchT_done patchT_out img_done img_ready img_stored
            f1_ready f1T_done f1T_ready merge_done blend_half merged sines_copied f2T_done f2T_ready feat_done gelu_done seg_chain text_ready
            text_stored0 text_stored1 attn_w_loaded attn_vec_ready qkv_w_loaded weights_split nT_hi
            h_loaded res_ready keep_ready n1pb_ready
            fill_done fill_free0 fill_free1 fill_free2 fill_free3 score_done score_out smax_done shifted exp_done et_done et_out pv_done zinv_done z_out
            r_ready r_stored route gap_ready ex_ready k2_placed0 k2_placed1 k2_placed2 pos_ready rows_copied scattered counts_done tables
            tables_ready tails_stored0 tails_stored1 spare_stored zero_rows_ready attn_end moe_ones
            xt_loaded0 xt_loaded1 xt_loaded2 xt_loaded3 xT_done xT_ready up_done0 up_done1 w1_copied0 w1_copied1 w2_copied hid_ready0 hid_ready1
            down_done y_biased y_ready y_stored0 y_stored1
            r_loaded0 r_loaded1 r_loaded2 r_loaded3 ya_loaded0 ya_loaded1 ya_loaded2 ya_loaded3 yb_loaded0 yb_loaded1
            last_chain last_out out_stored apart""".split()}
        for e in range(E):
            s[f"expert_loaded{e}"] = sem(f"expert_loaded{e}")
        for k in range(4):
            for n in ("stats", "mv", "var", "rstd", "norm"):
                s[f"ln{k}_{n}"] = sem(f"ln{k}_{n}")

        s_bank, t_bank, z_bank = banks[2:4], banks[4:6], banks[6:8]
        g_bank = banks[0:2] + z_bank

        def patch_source(k):
            return t["x"][8 * k:8 * k + 8].rearrange("b (ph i) (pw j) c -> (b ph) pw i (j c)", i=PATCH, j=PATCH)

        def img_loads():
            return [(w_img[:], t["L0_tok_W"].rearrange("(c p) d -> p c d", p=128)),
                    (img_add[0:N_PATCH, :], t["L0_tok_pos_emb"]),
                    (img_add[N_PATCH:N_PATCH + 1, :], t["L0_tok_b"].unsqueeze(0))]

        def text_loads():
            pairs = [(w_merge[:, 0, :], t["L0_txt_merge_w"][0:C1, :]),
                     (w_merge[0:C1 - 1, 1, :], t["L0_txt_merge_w"][C1:D + 1, :]),
                     (w_merge[C1 - 1:C1, 1, :], t["L0_txt_merge_b"].unsqueeze(0)),
                     (w_feat[:, 0, :], t["L0_txt_proj_w"][0:C2, :]),
                     (w_feat[0:C2 - 2, 1, :], t["L0_txt_proj_w"][C2:, :]),
                     (w_feat[C2 - 2:C2 - 1, 1, :], t["L0_txt_proj_b"].unsqueeze(0)),
                     (w_feat[C2 - 1:C2, 1, :], t["L0_txt_proj_b"].unsqueeze(0))]
            pairs += [(seg_rows[:, k, :], t["L0_txt_segment_emb"][k:k + 1, :].broadcast_to([TT, D])) for k in range(N_SEG)]
            return pairs

        def attn_loads():
            pairs = []
            for c in range(2):
                rows_c = slice(c * HALF, (c + 1) * HALF)
                pairs += [(wqkv2[:, c, :], t["L0_ffn_qkv_w"][rows_c, :]), (wp2[:, c, :], t["L0_ffn_proj_w"][rows_c, :]),
                          (wgate[:, c, :], t["L0_ffn_gate_w"][rows_c, :])]
            pairs += [(wo[:], t["L0_attn_W_O"].rearrange("h e d -> (h e) d").rearrange("(c p) d -> p c d", p=128)),
                      (bq[:], t["L0_attn_b_Q"].rearrange("h e -> (h e)").rearrange("(c p) -> p c", p=128)),
                      (bk[:], t["L0_attn_b_K"].rearrange("h e -> (h e)").rearrange("(c p) -> p c", p=128)),
                      (g1col[:], t["L0_ffn_ln1_g"].rearrange("(c p) -> p c", p=HALF)),
                      (b1col[:], t["L0_ffn_ln1_b"].rearrange("(c p) -> p c", p=HALF)),
                      (bo_row[:], t["L0_attn_b_O"].unsqueeze(0).broadcast_to([SL, D])),
                      (pb_row[:], t["L0_ffn_proj_b"].unsqueeze(0).broadcast_to([SL, D])),
                      (gb_row[:], t["L0_ffn_gate_b"].unsqueeze(0).broadcast_to([SL, E])),
                      (g2col[:], t["L0_ffn_ln2_g"].rearrange("(c p) -> p c", p=HALF)),
                      (b2col[:], t["L0_ffn_ln2_b"].rearrange("(c p) -> p c", p=HALF))]
            return pairs

        def qkv_loads():
            pairs = [(wv[HALF:HALF + 1, 1, :], t["L0_attn_b_V"].rearrange("h e -> (h e)").unsqueeze(0))]
            for c in range(2):
                for to, name in ((wq, "L0_attn_W_Q"), (wk_, "L0_attn_W_K"), (wv, "L0_attn_W_V")):
                    pairs.append((to[0:HALF, c, :].rearrange("p (h e) -> p h e", h=HEADS), t[name][:, c * HALF:(c + 1) * HALF, :].rearrange("h d e -> d h e")))
            return pairs

        def expert_loads(e):
            cols = experts_w[:, e]
            return [(cols[0:HALF, 0:2 * FF].rearrange("p (c f) -> p c f", c=2), t["L0_ffn_w1"][e].rearrange("(c p) f -> p c f", p=HALF)),
                    (cols[HALF:HALF + 1, 0:2 * FF].rearrange("p (c f) -> p c f", c=2), t["L0_ffn_b1"][e:e + 1, :].unsqueeze(1).broadcast_to([1, 2, FF])),
                    (cols[:, 2 * FF:2 * FF + FF // 128 * D].rearrange("p (c d) -> p c d", d=D), t["L0_ffn_w2"][e].rearrange("(c p) d -> p c d", p=128)),
                    (cols[:, W_COLS - D:], t["L0_ffn_b2"][e:e + 1, :].broadcast_to([128, D]))]

        def expert_cols(e, first, count):
            return experts_w[:, bass.ds(e, 1), first:first + count].rearrange("p a b -> p (a b)")

        def text_steps(eng, step, first_group={}):
            for k in range(PEEL):
                step(k // 2, k % 2)
            with eng.Fori(PEEL // 2, NT // 2 - 1) as i:
                for p in range(2):
                    step(i, p)
            for k in range(NT - 2, NT + 6):
                if k in first_group:
                    first_group[k]()
                step(k // 2, k % 2)

        def tile_at(i, p, lag):
            if isinstance(i, int) and not 0 <= 2 * i + p - lag < NT:
                return None
            return i * 2 + (p - lag), (p - lag) % 2

        def attn_bodies(eng, body):
            for n in range(FIRST_FULL + 1):
                body(Body(n, n))
            with eng.Fori(FIRST_FULL + 1, LAST_FULL + 1) as i:
                body(Body(FIRST_FULL, i))
            for n in range(LAST_FULL + 1, NG + 2):
                body(Body(n, n))

        def expert_steps(eng, step):
            for k in range(E):
                step(k // 4, k % 4)
            with eng.Fori(E // 4, NTILE // 4) as i:
                for p in range(4):
                    step(i, p)
            for k in range(NTILE // 4 * 4, NTILE + 2):
                step(k // 4, k % 4)

        def xtile_at(i, p, lag):
            if isinstance(i, int) and not 0 <= 4 * i + p - lag < NTILE:
                return None
            return i * 4 + (p - lag), (p - lag) % 4

        def store_tails(eng, k):
            eng.wait_ge(s["tables_ready"], 1)
            eng.wait_ge(s["zero_rows_ready"], 1)
            for e in range(k, E, 2):
                row = eng.value_load(tail_row[0:1, e:e + 1], min_val=0, max_val=E * REGION - 128)
                eng.dma_start(xs_d[bass.ds(row, 128), :], zero_rows[:, e, :]).then_inc(s[f"tails_stored{k}"], 16)

        def copy_w1(eng, copy, h, i, p):
            if (at := xtile_at(i, p, -1)) is None:
                return
            tile, place = at
            if isinstance(tile, int) and tile < E:
                eng.wait_ge(s[f"expert_loaded{tile}"], 16 * len(expert_loads(tile)))
            now = eng.value_load(tile_expert[0:1, bass.ds(tile, 1)], min_val=0, max_val=E - 1)
            at_least(eng, s[f"up_done{h}"], tile - 1)
            half = slice(h * (FF // 2), (h + 1) * (FF // 2))
            copy(w1_now[:, place % 2, :, half], expert_cols(now, 0, 2 * FF)[0:HALF + 1].rearrange("p (c f) -> p c f", c=2)[:, :, half]).then_inc(s[f"w1_copied{h}"], 1)

        def half_count(i, p, lag):
            return i * 2 + (p - lag) // 2

        def evacuated(eng, b, *label):
            bank, _, before = b.fill(*label)
            eng.wait_ge(s[f"fill_free{bank}"], before + 1)

        def filled(eng, b, *label):
            bank, before, _ = b.fill(*label)
            eng.wait_ge(s["fill_done"], before + 1)
            return g_bank[bank], s[f"fill_free{bank}"]

        def wait_apart(eng, sem, value):
            at_least(eng, sem, value)
            if not isinstance(value, int):
                eng.sem_inc(s["apart"], 1)

        block = ctx.enter_context(nc.Block())

        @block.sync
        def _(sp):
            def flat_tokens(a):
                return a.rearrange("b s -> (b s)").rearrange("(n k) -> n k", k=TT)

            sp.dma_start(vco_i[:], t["itok_BS_0_2047"]).then_inc(s["vco_loaded"], 16)
            for slot, name in enumerate(("x_txt", "itok_BS_1_36498", "itok_BS_0_99", "mask_BS_i2_0")):
                sp.dma_start(tok_i[:, slot, :], flat_tokens(t[name])).then_inc(s["tokens_loaded"], 16)
            sp.dma_start(tok_f[:, 4, :], flat_tokens(t["fside_BS_concept_values"])).then_inc(s["tokens_loaded"], 16)
            sp.dma_start(tok_f[:, 5, :], flat_tokens(t["mask_BS_f1_0"])).then_inc(s["tokens_loaded"], 16)
            sp.wait_ge(s["order_chain"], 4)
            sp.dma_start(ord_d, order[:]).then_inc(s["order_stored"], 16)
            for k in range(2):
                sp.dma_start(frow[:, k, :], t["L0_txt_w_age"].broadcast_to([TT, T_EMB])).then_inc(s["sine_rows_loaded"], 16)
                sp.dma_start(prow[:, k, :], t["L0_txt_phi_age"].broadcast_to([TT, T_EMB])).then_inc(s["sine_rows_loaded"], 16)
            sp.dma_start(frow[:, 2, :], t["pos_freq"].broadcast_to([TT, T_EMB])).then_inc(s["sine_rows_loaded"], 16)
            sp.dma_start(qrow[:].rearrange("p a b -> p (a b)"), t["quarter"].broadcast_to([TT, 3 * T_EMB])).then_inc(s["sine_rows_loaded"], 16)
            sp.wait_ge(s["order_stored"], 16)
            sp.dma_start(tok_f[:, 3, :], flat_tokens(ord_d)).then_inc(s["order_loaded"], 16)
            for to, of in text_loads():
                sp.dma_start(to, of, allow_slow_non_contiguous=True).then_inc(s["text_w_loaded"], 16)
            for to, of in attn_loads():
                sp.dma_start(to, of, allow_slow_non_contiguous=True).then_inc(s["attn_w_loaded"], 16)

            for k in range(4):
                sp.wait_ge(s["img_ready"], k + 1)
                sp.dma_start(img_d[k * 128:(k + 1) * 128, :], img_h[:, k, :]).then_inc(s["img_stored"], 16)

            sp.wait_ge(s["img_stored"], 64)
            for to, of in qkv_loads():
                sp.dma_start(to, of).then_inc(s["qkv_w_loaded"], 16)

            def load_h(g):
                at_least(sp, s["ln0_norm"], g * G)
                at_least(sp, s["res_ready"], g)
                sp.dma_start(h_in[0:N_PATCH, :, :], img_d.rearrange("(b s) d -> s b d", s=N_PATCH)[:, bass.ds(g * G, G), :]).then_inc(s["h_loaded"], 16)
                sp.dma_start(h_in[N_PATCH:S, :, :], txt_d.rearrange("(b s) d -> s b d", s=S_TXT)[:, bass.ds(g * G, G), :]).then_inc(s["h_loaded"], 16)

            def store_text(i, p):
                if (at := tile_at(i, p, 5)) is not None:
                    tile, par = at
                    sp.wait_ge(s["text_ready"], tile + 1)
                    sp.dma_start(txt_d[bass.ds(tile * TT, TT), :], txt_h[:, par, :]).then_inc(s[f"text_stored{par}"], 16)

            def load_first_group():
                sp.wait_ge(s["img_stored"], 64)
                for par in range(2):
                    sp.wait_ge(s[f"text_stored{par}"], 16 * (NT // 2 - 4))
                sp.wait_ge(s["attn_pool_consts"], 1)
                load_h(0)
            text_steps(sp, store_text, {NT - 2: load_first_group})

            for par in range(2):
                sp.wait_ge(s[f"text_stored{par}"], 16 * (NT // 2))

            def body(b):
                if b.has_n:
                    load_h(b.i + 1)
                if b.has_b:
                    g = b.i - 1
                    sp.wait_ge(s["r_ready"], (g + 1) * G)
                    sp.dma_start(r_d.rearrange("(b s) d -> s b d", s=S)[:, bass.ds(g * G, G), :], h_keep[0:S, :, :]).then_inc(s["r_stored"], 16)
            attn_bodies(sp, body)

            store_tails(sp, 0)
            sp.wait_ge(s["attn_end"], 1)
            sp.wait_ge(s["r_stored"], 16 * NG)

            def load_expert(e):
                for to, of in expert_loads(e):
                    sp.dma_start(to, of).then_inc(s[f"expert_loaded{e}"], 16)
            for e in range(2):
                load_expert(e)

            def pieces(a, k):
                return a.rearrange("(p j) d -> p j d", p=LP)[:, k * CJ:(k + 1) * CJ, :]
            sp.wait_ge(s["scattered"], 16 * TOPK * B)
            for k in range(2):
                sp.wait_ge(s[f"tails_stored{k}"], 16 * (E // 2))
            sp.wait_ge(s["spare_stored"], 16)

            def load_tile(tile, place):
                row = sp.value_load(tile_row[0:1, bass.ds(tile, 1)], min_val=0, max_val=XS_ROWS - 128)
                sp.dma_start(xt[:, place, :], xs_d[bass.ds(row, 128), :]).then_inc(s[f"xt_loaded{place}"], 16)
            for k in range(2):
                load_tile(k, k)
            load_expert(2)

            def load_ahead(i, p):
                if (at := xtile_at(i, p, -2)) is not None:
                    at_least(sp, s[f"y_stored{p % 2}"], half_count(i, p, 0) * 16)
                    load_tile(*at)
                if isinstance(i, int) and 3 + 4 * i + p < E:
                    load_expert(3 + 4 * i + p)
            expert_steps(sp, load_ahead)
            for k in range(NP_):
                sp.dma_start(last_r[:, k], pieces(r_d, k)).then_inc(s[f"r_loaded{k}"], 16)

            sp.wait_ge(s["y_stored0"], 16 * (NTILE // 2))
            sp.wait_ge(s["y_stored1"], 16 * (NTILE // 2))
            for k in range(NP_):
                sp.dma_start(last_ya[:, k], pieces(y_d[0:B * S, :], k)).then_inc(s[f"ya_loaded{k}"], 16)
                at_least(sp, s["last_out"], k - 1)
                sp.dma_start(last_yb[:, k % 2], pieces(y_d[B * S:SLOTS, :], k)).then_inc(s[f"yb_loaded{k % 2}"], 16)
            for k in range(NP_):
                sp.wait_ge(s["last_out"], k + 1)
                sp.dma_start(pieces(out.rearrange("b s d -> (b s) d"), k), last_ya[:, k]).then_inc(s["out_stored"], 16)
            sp.wait_ge(s["out_stored"], 16 * NP_)

        @block.gpsimd
        def _(pool):
            links = [0]

            def link(ins):
                links[0] += 1
                ins.then_inc(s["pool_chain"], 1)
                pool.wait_ge(s["pool_chain"], links[0])

            link(pool.memset(ident[:], 0.0))
            pool.affine_select(out=ident[:], in_=ident[:], compare_op=ALU.not_equal, fill=1.0, base=0,
                               pattern=[[-1, 128]], channel_multiplier=1).then_inc(s["ident_ready"], 1)
            pool.wait_ge(s["ident_ready"], 1)
            pool.memset(f2[:, :, F2W - 2:F2W - 1], 1.0).then_inc(s["pool_consts"], 1)
            pool.memset(f2[:, :, F2W - 1:F2W], 0.0).then_inc(s["pool_consts"], 1)
            pool.memset(f1all[:, :, F1W - 1:F1W], 1.0).then_inc(s["pool_consts"], 1)
            link(pool.memset(img_sel[:], 1.0))
            pool.tensor_copy(img_sel[0:N_PATCH, :].rearrange("p (a b) -> p a b", b=N_PATCH),
                             ident[0:N_PATCH, 0:N_PATCH].unsqueeze(1).broadcast_to([N_PATCH, 128 // N_PATCH, N_PATCH])).then_inc(s["img_sel_ready"], 1)
            link(pool.memset(zero_rows[:], 0.0))
            link(pool.iota(zero_rows[:, :, D:D + 1].bitcast(I32), pattern=[[128, max(E, SPARE)], [0, 1]], base=SLOTS + E * 128, channel_multiplier=1))
            pool.dma_start(xs_d[E * REGION:XS_ROWS, :].rearrange("(j p) w -> p j w", p=128), zero_rows[:, 0:SPARE, :]).then_inc(s["spare_stored"], 16)
            link(pool.memset(ones_first[:], 1.0))
            link(pool.affine_select(out=ones_first[:], in_=ones_first[:], compare_op=ALU.is_ge, fill=0.0, base=S - 1,
                                    pattern=[[0, 128]], channel_multiplier=-1))
            link(pool.iota(base_row[:], pattern=[[REGION, E]], base=0, channel_multiplier=0, allow_small_or_imprecise_dtypes=True))
            pool.wait_ge(s["ids_ready"], 1)
            for tile in range(NT):
                name = "gathered_first" if tile < PEEL else "gathered_rest"
                pool.indirect_dma_start(out=f1all[:, tile, 0:D], out_offset=None, in_=t["L0_txt_concept_emb"],
                                        in_offset=bass.IndirectOffsetOnAxis(ap=ids[:, tile:tile + 1], axis=0)).then_inc(s[name], 16)

            pool.wait_ge(s["spare_stored"], 16)
            pool.iota(zero_rows[:, :, D:D + 1].bitcast(I32), pattern=[[128, max(E, SPARE)], [0, 1]], base=SLOTS, channel_multiplier=1).then_inc(s["zero_rows_ready"], 1)

            pool.wait_ge(s["qkv_w_loaded"], 16 * len(qkv_loads()))
            for whole, high, low in ((wq, wq_hi, wq_lo), (wk_, wk_hi, wk_lo), (wv, wv_hi, wv_lo)):
                link(pool.tensor_copy(high[0:HALF].bitcast(F32R), whole[0:HALF]))
                link(pool.tensor_tensor(low[0:HALF].bitcast(F32R), whole[0:HALF], high[0:HALF], ALU.subtract))
            pool.wait_ge(s["gathered_first"], 16 * PEEL)
            pool.wait_ge(s["gathered_rest"], 16 * (NT - PEEL))
            bias, high, low = (w[HALF:HALF + 1, 1, :] for w in (wv, wv_hi, wv_lo))
            link(pool.tensor_copy(high.bitcast(F32R), bias))
            pool.tensor_tensor(low.bitcast(F32R), bias, high, ALU.subtract).then_inc(s["weights_split"], 1)
            pool.wait_ge(s["weights_split"], 1)
            link(pool.memset(h_in[:], 0.0))
            link(pool.memset(kbd[:], 0.0))
            link(pool.memset(head_rows[:], 1.0))
            link(pool.affine_select(out=head_rows[:], in_=head_rows[:], compare_op=ALU.is_ge, fill=0.0, base=0,
                                    pattern=[[-DH2, HEADS // SIXES]], channel_multiplier=1))
            link(pool.affine_select(out=head_rows[:], in_=head_rows[:], compare_op=ALU.is_ge, fill=0.0, base=DH2 - 1,
                                    pattern=[[DH2, HEADS // SIXES]], channel_multiplier=-1))
            link(pool.memset(causal[:], 0.0))
            link(pool.affine_select(out=causal[:], in_=causal[:], compare_op=ALU.is_ge, fill=NEG, base=0,
                                    pattern=[[0, UH], [-1, SL]], channel_multiplier=1))
            link(pool.memset(padded[:], 0.0))
            link(pool.affine_select(out=padded[:], in_=padded[:], compare_op=ALU.is_ge, fill=NEG, base=S - 1,
                                    pattern=[[0, UH], [-1, SL]], channel_multiplier=0))
            link(pool.memset(earlier[:], 1.0))
            link(pool.affine_select(out=earlier[:], in_=earlier[:], compare_op=ALU.is_gt, fill=0.0, base=0,
                                    pattern=[[1, SL]], channel_multiplier=-1))
            link(pool.affine_select(out=earlier[:], in_=earlier[:], compare_op=ALU.is_ge, fill=0.0, base=S - 1,
                                    pattern=[[0, SL]], channel_multiplier=-1))
            link(pool.memset(neg_half[:], -0.5))
            link(pool.iota(from_end[:], pattern=[[-1, E]], base=E, channel_multiplier=0, allow_small_or_imprecise_dtypes=True))
            link(pool.iota(dest0[:], pattern=[[B * S, TOPK], [S, G]], base=0, channel_multiplier=1, allow_small_or_imprecise_dtypes=True))
            link(pool.iota(tt_["t"][:], pattern=[[1, NTILE]], base=0, channel_multiplier=0, allow_small_or_imprecise_dtypes=True))
            link(pool.memset(runsum[:], 0.0))
            link(pool.tensor_copy(nT[HALF:HALF + 1, 1, :].bitcast(F32R).rearrange("p (a b) -> p a b", b=128),
                                  ones_first[0:1, :].unsqueeze(1).broadcast_to([1, GT // 128, 128])))
            link(pool.memset(v1[:, :, :, DH1:DH1 + 1], 1.0))
            pool.memset(v2[:, :, :, DH2:DH2 + 1], 1.0).then_inc(s["attn_pool_consts"], 1)

            def power(k, g):
                pool.wait_ge(s[f"ln{k}_var"], g + 1)
                pool.tensor_tensor(lns[k]["rstd"][:], lns[k]["var"][:], neg_half[:], ALU.pow).then_inc(s[f"ln{k}_rstd"], 1)

            def next_residual(g):
                at_least(pool, s["ln1_norm"], g * G)
                at_least(pool, s["keep_ready"], g)
                pool.wait_ge(s["h_loaded"], (g + 1) * 32)
                pool.tensor_tensor(h_res[:], h_in[:], bo_row[:].unsqueeze(1).broadcast_to([SL, G, D]), ALU.add).then_inc(s["res_ready"], 1)

            power(0, 0)
            pool.wait_ge(s["attn_w_loaded"], 16 * len(attn_loads()))
            for par in range(2):
                pool.wait_ge(s[f"text_stored{par}"], 16 * (NT // 2))
            pool.wait_ge(s["img_stored"], 64)
            next_residual(0)

            def shift(b, k):
                if 0 <= k < len(b.units):
                    at = k % 4
                    pool.wait_ge(s["smax_done"], b.units_before + k + 1)
                    pool.tensor_tensor(score[:, at], score[:, at], smax[:, at].unsqueeze(2).broadcast_to([SL, UH, SL]),
                                       ALU.subtract).then_inc(s["shifted"], 1)

            def scatter(b, k):
                if b.has_c and k < TOPK * G:
                    g, choice = k // TOPK, k % TOPK
                    if k == 0:
                        pool.wait_ge(s["pos_ready"], b.i - 1)
                        wait_apart(pool, s["rows_copied"], b.i - 1)
                    pool.indirect_dma_start(out=xs_d, out_offset=bass.IndirectOffsetOnAxis(ap=posi[0:S, choice, g:g + 1], axis=0),
                                            in_=rows[0:S, choice, g, :], in_offset=None).then_inc(s["scattered"], 16)

            def residual_row(b, step):
                for label in posts_of(b.n, step):
                    if label[0] == "pj":
                        g = label[1]
                        evacuated(pool, b, "pj", g)
                        pool.tensor_tensor(h_keep[:, g], x2[:, g], h_keep[:, g], ALU.add).then_inc(s["r_ready"], 1)

            def body(b):
                if b.has_b:
                    evacuated(pool, b, "k2", 0)
                    wide_k = [HALF, HEADS // SIXES, GT]
                    pool.tensor_tensor(k2bd[:, 0:HEADS // SIXES].rearrange("p h g t -> p h (g t)"), eT[:, 0, :].unsqueeze(1).broadcast_to(wide_k),
                                       head_rows[:].unsqueeze(2).broadcast_to(wide_k), ALU.mult).then_inc(s["k2_placed0"], 1)
                if b.has_n:
                    power(0, b.i + 1)
                for step in range(b.steps + 1):
                    shift(b, step)
                    scatter(b, step)
                    residual_row(b, step - 1)
                if b.has_a:
                    power(1, b.i)
                if b.has_b:
                    power(3, b.i - 1)
                if b.has_a:
                    power(2, b.i)
                    evacuated(pool, b, "wo", G - 1)
                    if b.has_b:
                        wait_apart(pool, s["r_stored"], b.i * 16)
                    pool.tensor_copy(h_keep[:], h_res[:]).then_inc(s["keep_ready"], 1)
                    pool.tensor_tensor(n1_pb[:], n1[:], pb_row[:].unsqueeze(1).broadcast_to([SL, G, D]), ALU.add).then_inc(s["n1pb_ready"], 1)
                if b.has_b:
                    pool.wait_ge(s["ln3_norm"], b.i * G)
                    wait_apart(pool, s["scattered"], (b.i - 1) * (16 * TOPK * G))
                    pool.tensor_copy(rows[:, 1, :, 0:D], rows[:, 0, :, 0:D]).then_inc(s["rows_copied"], 1)
                if b.has_n:
                    next_residual(b.i + 1)
            attn_bodies(pool, body)

            def scatter_rows(i, p):
                if (at := xtile_at(i, p, 1)) is not None:
                    tile, place = at
                    wait_apart(pool, s["y_ready"], tile + 1)
                    pool.indirect_dma_start(out=y_d, out_offset=bass.IndirectOffsetOnAxis(ap=xt[:, place, D:D + 1].bitcast(I32), axis=0),
                                            in_=y_row[:, place % 2, :], in_offset=None).then_inc(s[f"y_stored{place % 2}"], 16)
            expert_steps(pool, scatter_rows)

        @block.scalar
        def _(act):
            for to, of in img_loads():
                act.dma_start(to, of).then_inc(s["img_w_loaded"], 16)
            for k in range(4):
                for w in range(IMG // PATCH):
                    act.dma_start(xpatch[w::IMG // PATCH, k, :].rearrange("q (i c) -> q i c", i=PATCH), patch_source(k)[:, w]).then_inc(s["img_loaded"], 16)

            for k in range(4):
                for h in range(2):
                    act.wait_ge(s["patchT_done"], 2 * k + h + 1)
                    at_least(act, s["img_done"], k - 1)
                    act.copy(patchT[:, k % 2, 3 * h:3 * h + 3, :].rearrange("p a b -> p (a b)"), t_bank[h][:, 0:384]).then_inc(s["patchT_out"], 1)
                act.wait_ge(s["img_done"], k + 1)
                act.copy(img_h[:, k, :], banks[2 + k % 2][:, 0:D]).then_inc(s["img_ready"], 1)

            act.wait_ge(s["arg_ready"], 1)
            act.activation(turns[:], arg[:], ACT.Sin).then_inc(s["sines_ready"], 1)
            act.wait_ge(s["sines_ready"], 1)

            def text(i, p):
                if (at := tile_at(i, p, 4)) is not None:
                    tile, par = at
                    act.wait_ge(s["feat_done"], tile + 1)
                    at_least(act, s["text_ready"], tile - 1)
                    act.activation(gelu[:, par, :], banks[6 + par][0:TT, 0:D], ACT.Gelu).then_inc(s["gelu_done"], 1)
                if (at := tile_at(i, p, 0)) is not None:
                    tile, par = at
                    act.wait_ge(s["f1T_done"], tile + 1)
                    at_least(act, s["merge_done"], tile - 1)
                    act.copy(f1T[:, par].rearrange("p c t -> p (c t)"), banks[par][0:C1, 0:2 * TT]).then_inc(s["f1T_ready"], 1)
                if (at := tile_at(i, p, 2)) is not None:
                    tile, par = at
                    act.wait_ge(s["f2T_done"], tile + 1)
                    at_least(act, s["feat_done"], tile - 1)
                    act.copy(f2T[:, par].rearrange("p c t -> p (c t)"), banks[4 + par][0:C2, 0:2 * TT]).then_inc(s["f2T_ready"], 1)
                if (at := tile_at(i, p, 0)) is not None:
                    tile, par = at
                    at_least(act, s["f2T_done"], tile - 1)
                    act.copy(f2[:, par, D:F2W - 2], turns[:, bass.ds(tile, 1), :].rearrange("p a b -> p (a b)")).then_inc(s["sines_copied"], 1)
                if (at := tile_at(i, p, -1)) is not None:
                    tile, par = at
                    if isinstance(tile, int) and tile < PEEL:
                        act.wait_ge(s["gathered_first"], 16 * PEEL)
                        act.wait_ge(s["f1_cols_ready"], 1)
                        act.wait_ge(s["pool_consts"], 3)
                    else:
                        act.wait_ge(s["gathered_rest"], 16 * (NT - PEEL))
                    at_least(act, s["f1T_done"], tile - 1)
                    at_least(act, s["merged"], tile - 1)
                    act.copy(f1[:, par, :], f1all[:, bass.ds(tile, 1), :].rearrange("p a b -> p (a b)")).then_inc(s["f1_ready"], 1)
            text(-1, 1)

            def copy_nT(bank, pair):
                return act.copy(nT[0:HALF].bitcast(F32R)[:, :, pair * 2 * SL:(pair + 1) * 2 * SL].rearrange("p c (g t) -> p c g t", g=2),
                                bank[0:HALF, 0:4 * SL].rearrange("p (g c t) -> p c g t", g=2, c=2))

            def first_nT():
                act.wait_ge(s["attn_pool_consts"], 1)
                for pair in range(2):
                    act.wait_ge(s["fill_done"], pair + 1)
                    copy_nT(g_bank[pair], pair).then_inc(s["nT_hi"], 1)
            text_steps(act, text, {NT + 3: first_nT})

            act.wait_ge(s["attn_vec_ready"], 1)
            for par in range(2):
                act.wait_ge(s[f"text_stored{par}"], 16 * (NT // 2))

            def body(b):
                for label in b.front:
                    what, k = label[0], label[-1]
                    if label == (("q2", 1) if b.has_b else ("rank",)) and b.has_c:
                        act.wait_ge(s["gap_ready"], b.i - 1)
                        act.activation(rc["ex"][:], rc["gap"][:], ACT.Exp).then_inc(s["ex_ready"], 1)
                    if what == "q":
                        bank, free = filled(act, b, *label)
                        act.activation(qT[:, k, :], bank[:, 0:GT], ACT.Identity, bias=bq[:, k:k + 1], scale=DH1 ** -0.5).then_inc(free, 1)
                    elif what == "k":
                        bank, free = filled(act, b, *label)
                        for j in range(2):
                            ins = act.activation(kbd[64 * j:64 * j + 64, k, :, j, :], bank[64 * j:64 * j + 64, 0:GT].rearrange("p (g t) -> p g t", g=G),
                                                 ACT.Identity, bias=bk[64 * j:64 * j + 64, k:k + 1])
                        ins.then_inc(free, 1)
                    elif what == "v":
                        bank, free = filled(act, b, *label)
                        act.copy(v1[:, label[1], 6 * k:6 * k + 6, 0:DH1], bank[0:SL, 0:6 * DH1].rearrange("p (h e) -> p h e", h=6)).then_inc(free, 1)
                    elif what == "q2":
                        bank, free = filled(act, b, *label)
                        act.mul(q2T[:, k, :], bank[0:HALF, 0:GT], DH2 ** -0.5).then_inc(free, 1)
                    elif what == "k2":
                        bank, free = filled(act, b, *label)
                        act.copy(eT[:, k, :], bank[0:HALF, 0:GT]).then_inc(free, 1)
                    elif what == "v2":
                        bank, free = filled(act, b, *label)
                        act.copy(v2[:, 2 * k:2 * k + 2, :, 0:DH2].rearrange("p g h e -> p (g h) e"),
                                 bank[0:SL, 0:2 * D].rearrange("p (h e) -> p h e", e=DH2)).then_inc(free, 1)
                for step in range(b.steps):
                    if b.has_b and step < 3:
                        if step == 0:
                            evacuated(act, b, "k2", 1)
                        for j in range(2 * step, 2 * step + 2):
                            ins = act.mul(k2bd[:, HEADS // SIXES + j].rearrange("p g t -> p (g t)"), eT[:, 1, :], head_rows[:, j:j + 1])
                        if step != 1:
                            ins.then_inc(s[f"k2_placed{1 + step // 2}"], 1)
                    k = step - LAG_T
                    if k == 0 and b.has_b:
                        act.wait_ge(s["k2_placed0"], b.i)
                    if 0 <= k < len(b.units):
                        act.wait_ge(s["et_done"], b.units_before + k + 1)
                        at_least(act, s["pv_done"], b.units_before + k - 1)
                        act.copy(eT[:, k % 2, :], t_bank[k % 2][0:SL, 0:UH * SL]).then_inc(s["et_out"], 1)
                    k = step - LAG_T + 1
                    if 0 <= k < len(b.units):
                        act.wait_ge(s["shifted"], b.units_before + k + 1)
                        act.activation(score[:, k % 4], score[:, k % 4], ACT.Exp).then_inc(s["exp_done"], 1)
                    for label in posts_of(b.n, step):
                        if label[0] == "zT":
                            bank, free = filled(act, b, *label)
                            act.copy(z1T[:, 3 * label[2]:3 * label[2] + 3, :].rearrange("p a b -> p (a b)"), bank[:, 0:3 * SL]).then_inc(free, 1)
                        if label[0] == "z2T":
                            bank, free = filled(act, b, *label)
                            act.copy(z2T[:].rearrange("p a b -> p (a b)"), bank[0:HALF, 0:2 * SL]).then_inc(free, 1)
                        if label[0] == "nT":
                            bank, free = filled(act, b, *label)
                            copy_nT(bank, label[1]).then_inc(s["nT_hi"], 1)
            attn_bodies(act, body)

            store_tails(act, 1)
            act.wait_ge(s["attn_end"], 1)
            act.wait_ge(s["r_stored"], 16 * NG)

            def expert(i, p):
                tile = i * 4 + p
                copy_w1(act, act.copy, 1, i, p)
                if xtile_at(i, p, 0) is not None:
                    for h in range(2):
                        act.wait_ge(s[f"up_done{h}"], tile + 1)
                        at_least(act, s["down_done"], tile - 1)
                        act.activation(hidT[:, p % 2, h * (FF // 2):(h + 1) * (FF // 2)], banks[2 + h][:, 0:FF // 2], ACT.Gelu).then_inc(s[f"hid_ready{h}"], 1)
            copy_w1(act, act.copy, 1, -1, 3)
            expert_steps(act, expert)

        @block.vector
        def _(dve):
            dve.wait_ge(s["vco_loaded"], 16)
            dve.tensor_copy(vco[:], vco_i[:]).then_inc(s["order_chain"], 1)
            dve.wait_ge(s["order_chain"], 1)
            dve.tensor_reduce(vmin[:], vco[:], AX.X, ALU.min).then_inc(s["order_chain"], 1)
            dve.wait_ge(s["order_chain"], 2)
            dve.tensor_scalar(order[:], vco[:], vmin[:, 0:1], 0.0, ALU.subtract, ALU.max).then_inc(s["order_chain"], 1)
            dve.wait_ge(s["order_chain"], 3)
            dve.tensor_scalar(order[:], order[:], float(MAX_POS - 1), None, ALU.min).then_inc(s["order_chain"], 1)
            dve.wait_ge(s["tokens_loaded"], 16 * 6)
            dve.tensor_copy(tok_f[:, 0:3, :], tok_i[:, 0:3, :]).then_inc(s["tok_staged"], 1)
            dve.tensor_copy(tok_f[:, 6, :], tok_i[:, 3, :]).then_inc(s["tok_staged"], 1)
            dve.wait_ge(s["tokT_done"], 1)
            dve.tensor_copy(tok[:].rearrange("p a b -> p (a b)"), banks[0][0:TT, 0:7 * NT]).then_inc(s["tok_ready"], 1)
            dve.wait_ge(s["tok_ready"], 1)
            dve.tensor_copy(ids[:], tok[:, 0, :]).then_inc(s["ids_ready"], 1)
            dve.tensor_copy(f1all[:, :, D:D + 1].rearrange("p a b -> p (a b)"), tok[:, 4, :]).then_inc(s["f1_cols_ready"], 1)
            dve.tensor_scalar(keep[:, :, 0], tok[:, 5, :], 0.0, None, ALU.not_equal).then_inc(s["masks_ready"], 1)
            dve.tensor_scalar(keep[:, :, 1], tok[:, 5, :], 0.0, None, ALU.is_equal).then_inc(s["masks_ready"], 1)
            for k in range(N_SEG):
                dve.tensor_scalar(segm[:, k, :], tok[:, 6, :], float(k), None, ALU.is_equal).then_inc(s["masks_ready"], 1)

            dve.wait_ge(s["sine_rows_loaded"], 16 * 6)
            chain = [0]

            def link(ins):
                chain[0] += 1
                ins.then_inc(s["arg_chain"], 1)
                dve.wait_ge(s["arg_chain"], chain[0])
            wide = [TT, NT, 3, T_EMB]
            a4 = arg[:].rearrange("p n (k c) -> p n k c", k=3)
            a3, u3 = arg[:], turns[:]
            link(dve.memset(prow[:, 2, :], 0.0))
            link(dve.tensor_tensor(a4, tok[:, 1:4, :].rearrange("p k n -> p n k").unsqueeze(3).broadcast_to(wide), frow[:].unsqueeze(1).broadcast_to(wide), ALU.mult))
            rows3 = [TT, NT, 3 * T_EMB]
            phases = prow[:].rearrange("p k c -> p (k c)").unsqueeze(1).broadcast_to(rows3)
            quarters = qrow[:].rearrange("p k c -> p (k c)").unsqueeze(1).broadcast_to(rows3)
            link(dve.tensor_tensor(a3, a3, phases, ALU.add))
            link(dve.tensor_scalar(u3, a3, 1 / (2 * math.pi), None, ALU.mult))
            link(dve.scalar_tensor_tensor(u3, quarters, 0.25, u3, ALU.mult, ALU.add))
            link(dve.tensor_scalar(u3, u3, MAGIC, None, ALU.add))
            link(dve.tensor_scalar(u3, u3, -MAGIC, None, ALU.add))
            for part in (TP1, TP2, TP3):
                link(dve.scalar_tensor_tensor(a3, u3, -part, a3, ALU.mult, ALU.add))
            link(dve.scalar_tensor_tensor(a3, quarters, math.pi / 2, a3, ALU.mult, ALU.add))
            dve.tensor_scalar(a3, a3, 3.1415925, -3.1415925, ALU.min, ALU.max).then_inc(s["arg_ready"], 1)

            dve.wait_ge(s["text_w_loaded"], 16 * len(text_loads()))

            def text(i, p):
                if (at := tile_at(i, p, 1)) is not None:
                    tile, par = at
                    dve.wait_ge(s["merge_done"], tile + 1)
                    if isinstance(i, int):
                        dve.wait_ge(s["masks_ready"], 2 + N_SEG)
                    dve.tensor_scalar(blend[:, par, :], banks[2 + par][0:TT, 0:D], keep[:, bass.ds(tile, 1), 0], None, ALU.mult).then_inc(s["blend_half"], 1)
                    dve.wait_ge(s["blend_half"], tile + 1)
                    at_least(dve, s["f2T_done"], tile - 1)
                    dve.scalar_tensor_tensor(f2[:, par, 0:D], f1[:, par, 0:D], keep[:, bass.ds(tile, 1), 1], blend[:, par, :], ALU.mult, ALU.add).then_inc(s["merged"], 1)
                if (at := tile_at(i, p, 5)) is not None:
                    tile, par = at
                    dve.wait_ge(s["gelu_done"], tile + 1)
                    at_least(dve, s[f"text_stored{par}"], 16 * (i + (p - 5 - par) // 2))
                    for k in range(N_SEG):
                        ins = dve.scalar_tensor_tensor(txt_h[:, par, :], seg_rows[:, k, :], segm[:, k, bass.ds(tile, 1)], (gelu if k == 0 else txt_h)[:, par, :], ALU.mult, ALU.add)
                        if k < N_SEG - 1:
                            ins.then_inc(s["seg_chain"], 1)
                            dve.wait_ge(s["seg_chain"], tile * (N_SEG - 1) + k + 1)
                        else:
                            ins.then_inc(s["text_ready"], 1)

            def stats_of(k, g, src):
                ln = lns[k]
                for j in range(G):
                    dve.bn_stats(ln["stats"][:, j], src[:, j]).then_inc(s[f"ln{k}_stats"], 1)
                wait_apart(dve, s[f"ln{k}_stats"], (g + 1) * G)
                for j in range(G):
                    dve.bn_aggr(ln["mv"][:, j], ln["stats"][:, j]).then_inc(s[f"ln{k}_mv"], 1)
                dve.wait_ge(s[f"ln{k}_mv"], (g + 1) * G)
                dve.tensor_scalar(ln["var"][:], ln["mv"][:, :, 1], EPS, None, ALU.add).then_inc(s[f"ln{k}_var"], 1)

            def normalise(k, g, dst, src):
                ln = lns[k]
                dve.wait_ge(s[f"ln{k}_rstd"], g + 1)
                for j in range(G):
                    dve.tensor_scalar(dst[:, j], src[:, j], ln["mv"][:, j, 0:1], ln["rstd"][:, j:j + 1], ALU.subtract, ALU.mult).then_inc(s[f"ln{k}_norm"], 1)

            def rest_nT(bank, pair, copies):
                dve.wait_ge(s["nT_hi"], copies)
                at = slice(pair * 2 * SL, (pair + 1) * 2 * SL)
                return dve.tensor_tensor(nT_lo[:].bitcast(F32R)[:, :, at].rearrange("p c (g t) -> p c g t", g=2),
                                         bank[0:HALF, 0:4 * SL].rearrange("p (g c t) -> p c g t", g=2, c=2),
                                         nT[0:HALF, :, at].rearrange("p c (g t) -> p c g t", g=2), ALU.subtract)

            def first_stats():
                dve.wait_ge(s["attn_w_loaded"], 16 * len(attn_loads()))
                dve.tensor_scalar(bq[:], bq[:], DH1 ** -0.5, None, ALU.mult).then_inc(s["attn_vec_ready"], 1)
                dve.wait_ge(s["attn_pool_consts"], 1)
                dve.wait_ge(s["h_loaded"], 32)
                stats_of(0, 0, h_in)

            def first_rest():
                for pair in range(2):
                    rest_nT(g_bank[pair], pair, pair + 1).then_inc(s[f"fill_free{pair}"], 1)
            text_steps(dve, text, {NT: first_stats, NT + 1: lambda: normalise(0, 0, n0, h_in), NT + 4: first_rest})

            for par in range(2):
                dve.wait_ge(s[f"text_stored{par}"], 16 * (NT // 2))

            def affine_copy(bank, free, pair, dst, scale, shift):
                for c in range(2):
                    ins = dve.tensor_scalar(dst[:, c, pair * 2 * SL:(pair + 1) * 2 * SL].rearrange("p (g t) -> p g t", g=2),
                                            bank[0:HALF, 0:4 * SL].rearrange("p (g c t) -> p c g t", g=2, c=2)[:, c],
                                            scale[:, c:c + 1], shift[:, c:c + 1], ALU.mult, ALU.add)
                ins.then_inc(free, 1)

            wide3 = [SL, G, E]

            def bc(a):
                return a.unsqueeze(2).broadcast_to(wide3)

            def next_stats(b):
                dve.wait_ge(s["h_loaded"], (b.i + 2) * 32)
                stats_of(0, b.i + 1, h_in)

            def route(b):
                g, n = b.i - 2, [0]

                def link(ins):
                    n[0] += 1
                    ins.then_inc(s["route"], 1)
                    dve.wait_ge(s["route"], g * ROUTE + n[0])
                bank, free = filled(dve, b, "gate")
                ends = from_end[:].unsqueeze(1).broadcast_to(wide3)
                dve.tensor_tensor(rt["logit"][:], bank[0:SL, 0:G * E].rearrange("p (g e) -> p g e", g=G), gb_row[:].unsqueeze(1).broadcast_to(wide3), ALU.add).then_inc(free, 1)
                evacuated(dve, b, "gate")
                link(dve.tensor_reduce(rc["m1"][:], rt["logit"][:], AX.X, ALU.max))
                link(dve.tensor_tensor(rt["eq"][:], rt["logit"][:], bc(rc["m1"][:]), ALU.is_equal))
                link(dve.tensor_tensor(rt["mark"][:], rt["eq"][:], ends, ALU.mult))
                link(dve.tensor_reduce(rc["i1"][:], rt["mark"][:], AX.X, ALU.max))
                link(dve.tensor_tensor(rt["pick1"][:], bc(rc["i1"][:]), ends, ALU.is_equal))
                link(dve.scalar_tensor_tensor(rt["rest"][:], rt["pick1"][:], NEG, rt["logit"][:], ALU.mult, ALU.add))
                link(dve.tensor_reduce(rc["m2"][:], rt["rest"][:], AX.X, ALU.max))
                dve.tensor_tensor(rc["gap"][:], rc["m2"][:], rc["m1"][:], ALU.subtract).then_inc(s["gap_ready"], 1)
                link(dve.tensor_tensor(rt["eq"][:], rt["rest"][:], bc(rc["m2"][:]), ALU.is_equal))
                link(dve.tensor_tensor(rt["mark"][:], rt["eq"][:], ends, ALU.mult))
                link(dve.tensor_reduce(rc["i2"][:], rt["mark"][:], AX.X, ALU.max))
                link(dve.tensor_tensor(rt["pick2"][:], bc(rc["i2"][:]), ends, ALU.is_equal))
                link(dve.tensor_tensor(rt["sel"][:], rt["pick1"][:], rt["pick2"][:], ALU.add))
                link(dve.tensor_copy(rt["before"][:, 0], runsum[:]))
                for j in range(1, G):
                    link(dve.tensor_tensor(rt["before"][:, j], rt["before"][:, j - 1], rt["sel"][:, j - 1], ALU.add))
                link(dve.tensor_tensor(runsum[:], rt["before"][:, G - 1], rt["sel"][:, G - 1], ALU.add))
                assert n[0] == ROUTE_SEL, n[0]
                if b.has_n:
                    next_stats(b)
                dve.wait_ge(s["ex_ready"], g + 1)
                link(dve.tensor_scalar(rc["den"][:], rc["ex"][:], 1.0, None, ALU.add))
                link(dve.reciprocal(rc["w1"][:], rc["den"][:]))
                link(dve.tensor_tensor(rc["w2"][:], rc["ex"][:], rc["w1"][:], ALU.mult))
                at_least(dve, s["scattered"], g * (16 * TOPK * G))
                link(dve.tensor_copy(rows[:, 0, :, D + 1], rc["w1"][:]))
                link(dve.tensor_copy(rows[:, 1, :, D + 1], rc["w2"][:]))
                link(dve.tensor_copy(rows[:, :, :, D].bitcast(I32), dest0[:]))
                link(dve.tensor_scalar(dest0[:], dest0[:], float(G * S), None, ALU.add))
                bank, free = filled(dve, b, "rank")
                dve.tensor_tensor(rt["pos"][:], bank[0:SL, 0:G * E].rearrange("p (g e) -> p g e", g=G), base_row[0:SL].unsqueeze(1).broadcast_to(wide3), ALU.add).then_inc(free, 1)
                evacuated(dve, b, "rank")
                for k, pick in enumerate(("pick1", "pick2")):
                    link(dve.tensor_tensor(rt["at"][:], rt["pos"][:], rt[pick][:], ALU.mult))
                    link(dve.tensor_reduce(posf[:, k], rt["at"][:], AX.X, ALU.add))
                dve.tensor_copy(posi[:], posf[:]).then_inc(s["pos_ready"], 1)
                assert n[0] == ROUTE, n[0]

            def body(b):
                if b.has_c:
                    for pair in range(2):
                        affine_copy(*filled(dve, b, "h2T", pair), pair, h2T, g2col, b2col)
                if b.has_b:
                    for pair in range(2):
                        affine_copy(*filled(dve, b, "yT", pair), pair, yT, g1col, b1col)
                if b.has_c:
                    route(b)
                elif b.has_n:
                    next_stats(b)
                for step in range(b.steps):
                    if b.has_n and step == 6:
                        normalise(0, b.i + 1, n0, h_in)
                    k = step
                    if 0 <= k < len(b.units):
                        kind, g, u = b.units[k]
                        dve.wait_ge(s["score_done"], b.units_before + k + 1)
                        at_least(dve, s["et_done"], b.units_before + k - 3)
                        dve.tensor_tensor(score[:, k % 4].rearrange("p a b -> p (a b)"), s_bank[k % 2][0:SL, 0:UH * SL],
                                          (causal if kind == "a" else padded)[:].rearrange("p a b -> p (a b)"), ALU.add).then_inc(s["score_out"], 1)
                        dve.wait_ge(s["score_out"], b.units_before + k + 1)
                        dve.tensor_reduce(smax[:, k % 4], score[:, k % 4], AX.X, ALU.max).then_inc(s["smax_done"], 1)
                    k = step - LAG_PV
                    if 0 <= k < len(b.units):
                        kind, g, u = b.units[k]
                        w = DH1 if kind == "a" else DH2
                        z = z_bank[k % 2][0:SL, 0:UH * (w + 1)].rearrange("p (h e) -> p h e", h=UH)
                        dve.wait_ge(s["pv_done"], b.units_before + k + 1)
                        dve.reciprocal(zinv[:, k % 2], z[:, :, w]).then_inc(s["zinv_done"], 1)
                        dve.wait_ge(s["zinv_done"], b.units_before + k + 1)
                        dst = (z1 if kind == "a" else z2)[:, g % 2, u * UH * w:(u + 1) * UH * w].rearrange("p (h e) -> p h e", h=UH)
                        dve.tensor_tensor(dst, z[:, :, 0:w], zinv[:, k % 2].unsqueeze(2).broadcast_to([SL, UH, w]), ALU.mult).then_inc(s["z_out"], 1)
                    for label in posts_of(b.n, step):
                        if label[0] == "wo":
                            g = label[1]
                            bank, free = filled(dve, b, *label)
                            if g == 0:
                                dve.wait_ge(s["res_ready"], b.i + 1)
                            dve.tensor_tensor(h_res[:, g], bank[0:SL, 0:D], h_res[:, g], ALU.add).then_inc(free, 1)
                        if label[0] == "pj":
                            g = label[1]
                            bank, free = filled(dve, b, *label)
                            if g == 0:
                                dve.wait_ge(s["n1pb_ready"], b.i)
                                at_least(dve, s["r_ready"], (b.i - 1) * G)
                            dve.tensor_tensor(x2[:, g], bank[0:SL, 0:D], n1_pb[:, g], ALU.add).then_inc(free, 1)
                        if label[0] == "nT":
                            bank, free = filled(dve, b, *label)
                            rest_nT(bank, label[1], (b.i + 1) * 2 + label[1] + 1).then_inc(free, 1)
                if b.has_a:
                    evacuated(dve, b, "wo", G - 1)
                    stats_of(1, b.i, h_res)
                if b.has_b:
                    evacuated(dve, b, "pj", G - 1)
                    stats_of(3, b.i - 1, x2)
                if b.has_a:
                    at_least(dve, s["n1pb_ready"], b.i)
                    normalise(1, b.i, n1, h_res)
                    dve.wait_ge(s["ln1_norm"], (b.i + 1) * G)
                    stats_of(2, b.i, n1)
                if b.has_b:
                    at_least(dve, s["scattered"], (b.i - 1) * (16 * TOPK * G))
                    at_least(dve, s["rows_copied"], b.i - 1)
                    normalise(3, b.i - 1, rows[:, 0, :, 0:D], x2)
                if b.has_a:
                    normalise(2, b.i, y0, n1)
            attn_bodies(dve, body)

            links = [0]

            def link(ins):
                links[0] += 1
                ins.then_inc(s["tables"], 1)
                dve.wait_ge(s["tables"], links[0])
            link(dve.memset(tb["one"][:], 1.0))
            dve.wait_ge(s["counts_done"], 1)
            link(dve.tensor_copy(counts[:], s_bank[0][:, 0:E]))
            link(dve.tensor_tensor(tail_row[:], counts[0:1, :], base_row[0:1, :], ALU.add))
            link(dve.tensor_scalar(tb["x"][:], counts[0:1, :], 1 / 128, 127 / 256, ALU.mult, ALU.add))
            link(dve.tensor_scalar(tb["up"][:], tb["x"][:], MAGIC, None, ALU.add))
            link(dve.tensor_scalar(tb["whole"][:], tb["up"][:], -MAGIC, None, ALU.add))
            link(dve.tensor_scalar(tb["nt"][:], tb["whole"][:], 1.0, None, ALU.max))
            link(dve.tensor_tensor_scan(tb["end"][:], tb["one"][:], tb["nt"][:], 0.0, ALU.mult, ALU.add))
            link(dve.tensor_scalar(tb["jump"][:], tb["nt"][:], -128.0, float(REGION), ALU.mult, ALU.add))
            w54 = [1, NTILE, E]
            link(dve.tensor_tensor(past, tt_["t"][:].unsqueeze(2).broadcast_to(w54), tb["end"][:].unsqueeze(1).broadcast_to(w54), ALU.is_ge))
            link(dve.tensor_reduce(tt_["e"][:], past, AX.X, ALU.add))
            link(dve.tensor_scalar(tile_expert[:], tt_["e"][:], float(E - 1), None, ALU.min))
            link(dve.tensor_tensor(jumps, past, tb["jump"][:].unsqueeze(1).broadcast_to(w54), ALU.mult))
            link(dve.tensor_reduce(tt_["s"][:], jumps, AX.X, ALU.add))
            link(dve.scalar_tensor_tensor(tile_row[:], tt_["t"][:], 128.0, tt_["s"][:], ALU.mult, ALU.add))
            dve.memset(tb["x"][:], 0.0).then_inc(s["tables_ready"], 1)
            dve.wait_ge(s["tables_ready"], 1)
            dve.memset(tb["up"][:], 0.0).then_inc(s["attn_end"], 1)

            dve.wait_ge(s["attn_end"], 1)
            dve.wait_ge(s["r_stored"], 16 * NG)
            for k in range(2):
                dve.memset(xT[HALF:HALF + 1, k, 1, :], 1.0).then_inc(s["moe_ones"], 1)

            def features(tile, par):
                dve.wait_ge(s["xT_done"], tile + 1)
                at_least(dve, s["up_done1"], tile - 1)
                for c in range(2):
                    ins = dve.tensor_scalar(xT[0:HALF, par, c, :], banks[par][0:HALF, c * 128:(c + 1) * 128], g2col[:, c:c + 1], b2col[:, c:c + 1], ALU.mult, ALU.add)
                ins.then_inc(s["xT_ready"], 1)

            features(0, 0)
            copy_w1(dve, dve.tensor_copy, 0, -1, 3)

            def expert(i, p):
                if (at := xtile_at(i, p, -1)) is not None:
                    features(at[0], at[1] % 2)
                copy_w1(dve, dve.tensor_copy, 0, i, p)
                if xtile_at(i, p, 0) is not None:
                    tile = i * 4 + p
                    now = dve.value_load(tile_expert[0:1, bass.ds(tile, 1)], min_val=0, max_val=E - 1)
                    at_least(dve, s["down_done"], tile - 1)
                    dve.tensor_copy(w2_now[:, p % 2, :], expert_cols(now, 2 * FF, FF // 128 * D)).then_inc(s["w2_copied"], 1)
                if (at := xtile_at(i, p, 1)) is not None:
                    tile, place = at
                    e = dve.value_load(tile_expert[0:1, bass.ds(tile, 1)], min_val=0, max_val=E - 1)
                    dve.wait_ge(s["down_done"], tile + 1)
                    dve.tensor_tensor(y_raw[:, place % 2, :], banks[6 + place % 2][:, 0:D], expert_cols(e, W_COLS - D, D), ALU.add).then_inc(s["y_biased"], 1)
                    dve.wait_ge(s["y_biased"], tile + 1)
                    at_least(dve, s[f"y_stored{place % 2}"], half_count(i, p, 1) * 16)
                    dve.tensor_scalar(y_row[:, place % 2, :], y_raw[:, place % 2, :], xt[:, place, D + 1:D + 2], None, ALU.mult).then_inc(s["y_ready"], 1)
            expert_steps(dve, expert)

            for k in range(NP_):
                dve.wait_ge(s[f"r_loaded{k}"], 16)
                dve.wait_ge(s[f"ya_loaded{k}"], 16)
                dve.tensor_tensor(last_ya[:, k], last_ya[:, k], last_r[:, k], ALU.add).then_inc(s["last_chain"], 1)
                dve.wait_ge(s["last_chain"], k + 1)
                dve.wait_ge(s[f"yb_loaded{k % 2}"], 16 * (k // 2 + 1))
                dve.tensor_tensor(last_ya[:, k], last_ya[:, k], last_yb[:, k % 2], ALU.add).then_inc(s["last_out"], 1)

        @block.tensor
        def _(pe):
            pe.wait_ge(s["ident_ready"], 1)
            pe.wait_ge(s["tok_staged"], 2)
            pe.wait_ge(s["order_loaded"], 16)
            for k in range(7):
                ins = pe.transpose(banks[0][0:TT, k * NT:(k + 1) * NT], tok_f[:, k, :], ident[0:NT, 0:NT])
            ins.then_inc(s["tokT_done"], 1)

            pe.wait_ge(s["img_loaded"], 16 * 4 * (IMG // PATCH))
            pe.wait_ge(s["img_w_loaded"], 16 * len(img_loads()))
            pe.wait_ge(s["img_sel_ready"], 1)
            for k in range(4):
                for h in range(2):
                    at_least(pe, s["patchT_out"], 2 * k + h - 1)
                    for c in range(3):
                        ins = pe.transpose(t_bank[h][:, c * 128:(c + 1) * 128], xpatch[:, k, (3 * h + c) * 128:(3 * h + c + 1) * 128], ident[:])
                    ins.then_inc(s["patchT_done"], 1)
                pe.wait_ge(s["patchT_out"], 2 * k + 2)
                at_least(pe, s["img_ready"], k - 1)
                for c in range(KP // 128):
                    pe.matmul(banks[2 + k % 2][:, 0:D], patchT[:, k % 2, c, :], w_img[:, c, :], start=c == 0, stop=False)
                ins = pe.matmul(banks[2 + k % 2][:, 0:D], img_sel[:], img_add[:], start=False, stop=True)
                ins.then_inc(s["img_done"], 1)
            pe.wait_ge(s["img_ready"], 4)
            pe.wait_ge(s["tok_ready"], 1)
            pe.wait_ge(s["text_w_loaded"], 16 * len(text_loads()))

            def text(i, p):
                if (at := tile_at(i, p, 1)) is not None:
                    tile, par = at
                    pe.wait_ge(s["f1T_ready"], tile + 1)
                    at_least(pe, s["merged"], tile - 1)
                    for c in range(2):
                        ins = pe.matmul(banks[2 + par][0:TT, 0:D], f1T[:, par, c, :], w_merge[:, c, :], start=c == 0, stop=c == 1)
                    ins.then_inc(s["merge_done"], 1)
                if (at := tile_at(i, p, 0)) is not None:
                    tile, par = at
                    pe.wait_ge(s["f1_ready"], tile + 1)
                    at_least(pe, s["f1T_ready"], tile - 1)
                    for c in range(2):
                        ins = pe.transpose(banks[par][0:C1, c * TT:(c + 1) * TT], f1[:, par, c * C1:(c + 1) * C1], ident[0:TT, 0:TT])
                    ins.then_inc(s["f1T_done"], 1)
                if (at := tile_at(i, p, 2)) is not None:
                    tile, par = at
                    pe.wait_ge(s["merged"], tile + 1)
                    pe.wait_ge(s["sines_copied"], tile + 1)
                    at_least(pe, s["f2T_ready"], tile - 1)
                    for c in range(2):
                        ins = pe.transpose(banks[4 + par][0:C2, c * TT:(c + 1) * TT], f2[:, par, c * C2:(c + 1) * C2], ident[0:TT, 0:TT])
                    ins.then_inc(s["f2T_done"], 1)
                if (at := tile_at(i, p, 3)) is not None:
                    tile, par = at
                    pe.wait_ge(s["f2T_ready"], tile + 1)
                    at_least(pe, s["gelu_done"], tile - 1)
                    for c in range(2):
                        ins = pe.matmul(banks[6 + par][0:TT, 0:D], f2T[:, par, c, :], w_feat[:, c, :], start=c == 0, stop=c == 1)
                    ins.then_inc(s["feat_done"], 1)

            def turn_pair(bank, src, pair):
                for j in range(2):
                    for c in range(2):
                        ins = pe.transpose(bank[0:HALF, (2 * j + c) * SL:(2 * j + c + 1) * SL], src[:, 2 * pair + j, c * HALF:(c + 1) * HALF], ident[0:SL, 0:SL])
                return ins

            def in_parts(to, products, first, last):
                for k, (a, b) in enumerate(products):
                    ins = pe.matmul(to, a.bitcast(F32R), b.bitcast(F32R), start=first and k == 0, stop=last and k == len(products) - 1)
                return ins

            def first_turns():
                pe.wait_ge(s["f1T_ready"], NT)
                pe.wait_ge(s["ln0_norm"], G)
                for pair in range(2):
                    turn_pair(g_bank[pair], n0, pair).then_inc(s["fill_done"], 1)
            text_steps(pe, text, {NT + 3: first_turns})

            pe.wait_ge(s["gelu_done"], NT)
            pe.wait_ge(s["attn_w_loaded"], 16 * len(attn_loads()))
            pe.wait_ge(s["attn_pool_consts"], 1)
            pe.wait_ge(s["attn_vec_ready"], 1)
            pe.wait_ge(s["weights_split"], 1)

            def open_fill(b, *label, reads=()):
                bank, _, before = b.fill(*label)
                pe.wait_ge(s[f"fill_free{bank}"], before)
                for other in {b.fill(*other)[0]: other for other in reads}.values():
                    if b.fill(*other)[0] != bank:
                        evacuated(pe, b, *other)
                return g_bank[bank]

            def scores(b, k):
                kind, g, u = b.units[k]
                at_least(pe, s["score_out"], b.units_before + k - 1)
                bank = s_bank[k % 2]
                if kind == "a":
                    for j in range(2):
                        c = 2 * u + j
                        ins = pe.matmul(bank[0:SL, j * 2 * SL:(j + 1) * 2 * SL], qT[:, c, g * SL:(g + 1) * SL],
                                        kbd[:, c, g].rearrange("p a b -> p (a b)"), start=True, stop=True)
                else:
                    if g == 0:
                        pe.wait_ge(s[f"k2_placed{u}"], b.i)
                    for c in range(SIXES):
                        first, end = max(u * UH, c * 6), min((u + 1) * UH, (c + 1) * 6)
                        if first < end:
                            ins = pe.matmul(bank[0:SL, (first - u * UH) * SL:(end - u * UH) * SL], q2T[:, c, g * SL:(g + 1) * SL],
                                            k2bd[:, first:end, g, :], start=True, stop=True)
                ins.then_inc(s["score_done"], 1)

            def body(b):
                for label in b.front:
                    what = label[0]
                    if label == b.front[0]:
                        at_least(pe, s["z_out"], b.units_before)
                    if label == ("q", 0):
                        for bank in range(2):
                            pe.wait_ge(s[f"fill_free{bank}"], b.bank_fills_before[bank])
                    if what in ("q", "k"):
                        high, low = (wq_hi, wq_lo) if what == "q" else (wk_hi, wk_lo)
                        cols = slice(label[1] * 128, (label[1] + 1) * 128)
                        bank = open_fill(b, *label)
                        for c in range(2):
                            ins = in_parts(bank[:, 0:GT], [(high[:, c, cols], nT[0:HALF, c, :]), (low[:, c, cols], nT[0:HALF, c, :]),
                                                           (high[:, c, cols], nT_lo[:, c, :])], c == 0, c == 1)
                    elif what == "v":
                        g, h = label[1], label[2]
                        bank = open_fill(b, *label)
                        own, cols = slice(g * SL, (g + 1) * SL), slice(h * 6 * DH1, (h + 1) * 6 * DH1)
                        for c in range(2):
                            rows_c = slice(0, HALF + c)
                            ins = in_parts(bank[0:SL, 0:6 * DH1], [(nT[rows_c, c, own], wv_hi[rows_c, c, cols]), (nT[rows_c, c, own], wv_lo[rows_c, c, cols]),
                                                                   (nT_lo[:, c, own], wv_hi[0:HALF, c, cols])], c == 0, c == 1)
                    elif what == "h2T":
                        if label[1] == 0:
                            pe.wait_ge(s["ln3_norm"], (b.i - 1) * G)
                        ins = turn_pair(open_fill(b, *label), rows[:, 0], label[1])
                    elif what == "yT":
                        if label[1] == 0:
                            pe.wait_ge(s["ln2_norm"], b.i * G)
                        ins = turn_pair(open_fill(b, *label), y0, label[1])
                    elif what == "gate":
                        bank = open_fill(b, *label, reads=[("h2T", 0), ("h2T", 1)])
                        for g in range(G):
                            for c in range(2):
                                ins = pe.matmul(bank[0:SL, g * E:(g + 1) * E], h2T[:, c, g * SL:(g + 1) * SL], wgate[:, c, :], start=c == 0, stop=c == 1)
                    elif what in ("q2", "k2"):
                        first = (what == "k2") * D + label[1] * HALF
                        bank = open_fill(b, *label, reads=[("yT", 0), ("yT", 1)] if label == ("q2", 0) else [])
                        for c in range(2):
                            ins = pe.matmul(bank[0:HALF, 0:GT], wqkv2[:, c, first:first + HALF], yT[:, c, :], start=c == 0, stop=c == 1)
                    elif what == "v2":
                        bank = open_fill(b, *label)
                        for j in range(2):
                            g = 2 * label[1] + j
                            for c in range(2):
                                ins = pe.matmul(bank[0:SL, j * D:(j + 1) * D], yT[:, c, g * SL:(g + 1) * SL], wqkv2[:, c, 2 * D:], start=c == 0, stop=c == 1)
                    else:
                        pe.wait_ge(s["route"], (b.i - 2) * ROUTE + ROUTE_SEL)
                        bank = open_fill(b, *label)
                        pe.matmul(bank[0:SL, 0:G * E], earlier[:], rt["sel"][:].rearrange("p a b -> p (a b)"), start=True, stop=False)
                        ins = pe.matmul(bank[0:SL, 0:G * E], ones_first[:, 0:SL], rt["before"][:].rearrange("p a b -> p (a b)"), start=False, stop=True)
                    ins.then_inc(s["fill_done"], 1)

                for step in range(b.steps):
                    if step < len(b.units):
                        scores(b, step)
                    k = step - LAG_T
                    if 0 <= k < len(b.units):
                        pe.wait_ge(s["exp_done"], b.units_before + k + 1)
                        at_least(pe, s["et_out"], b.units_before + k - 1)
                        for h in range(UH):
                            ins = pe.transpose(t_bank[k % 2][0:SL, h * SL:(h + 1) * SL], score[:, k % 4, h, :], ident[0:SL, 0:SL])
                        ins.then_inc(s["et_done"], 1)
                    k = step - LAG_PV
                    if 0 <= k < len(b.units):
                        kind, g, u = b.units[k]
                        v, w = (v1, DH1 + 1) if kind == "a" else (v2, DH2 + 1)
                        if k == 0:
                            for bank in range(RING):
                                pe.wait_ge(s[f"fill_free{bank}"], b.bank_fills_before[bank] + len(b.front) // RING)
                        pe.wait_ge(s["et_out"], b.units_before + k + 1)
                        at_least(pe, s["z_out"], b.units_before + k - 1)
                        for h in range(UH):
                            ins = pe.matmul(z_bank[k % 2][0:SL, h * w:(h + 1) * w], eT[:, k % 2, h * SL:(h + 1) * SL], v[:, g, u * UH + h, :], start=True, stop=True)
                        ins.then_inc(s["pv_done"], 1)
                    for label in posts_of(b.n, step):
                        what, g = label[0], label[1]
                        bank = open_fill(b, *label, reads={"wo": [("zT", g, 0), ("zT", g, 1)], "pj": [("z2T", g)]}.get(what, []))
                        if what == "zT":
                            pe.wait_ge(s["z_out"], b.units_before + b.units.index(("a", g, UN - 1)) + 1)
                            for j in range(3):
                                c = 3 * label[2] + j
                                ins = pe.transpose(bank[:, j * SL:(j + 1) * SL], z1[:, g % 2, c * 128:(c + 1) * 128], ident[0:SL, 0:SL])
                        elif what == "z2T":
                            pe.wait_ge(s["z_out"], b.units_before + b.units.index(("b", g, UN - 1)) + 1)
                            for c in range(2):
                                ins = pe.transpose(bank[0:HALF, c * SL:(c + 1) * SL], z2[:, g % 2, c * HALF:(c + 1) * HALF], ident[0:SL, 0:SL])
                        elif what == "nT":
                            pe.wait_ge(s["ln0_norm"], (b.i + 2) * G)
                            ins = turn_pair(bank, n0, g)
                        elif what == "wo":
                            for c in range(PAIRS):
                                ins = pe.matmul(bank[0:SL, 0:D], z1T[:, c, :], wo[:, c, :], start=c == 0, stop=c == PAIRS - 1)
                        else:
                            for c in range(2):
                                ins = pe.matmul(bank[0:SL, 0:D], z2T[:, c, :], wp2[:, c, :], start=c == 0, stop=c == 1)
                        ins.then_inc(s["fill_done"], 1)
            attn_bodies(pe, body)

            pe.wait_ge(s["route"], NG * ROUTE)
            pe.matmul(s_bank[0][:, 0:E], ones_first[:], runsum[:], start=True, stop=True).then_inc(s["counts_done"], 1)

            pe.wait_ge(s["moe_ones"], 2)

            def turn_rows(tile, place, loads):
                pe.wait_ge(s[f"xt_loaded{place}"], loads * 16)
                at_least(pe, s["xT_ready"], tile - 1)
                for c in range(2):
                    ins = pe.transpose(banks[place % 2][0:HALF, c * 128:(c + 1) * 128], xt[:, place, c * HALF:(c + 1) * HALF], ident[:])
                ins.then_inc(s["xT_done"], 1)
            turn_rows(0, 0, 1)

            def expert(i, p):
                tile = i * 4 + p
                if xtile_at(i, p, 0) is not None:
                    pe.wait_ge(s["xT_ready"], tile + 1)
                    for h in range(2):
                        pe.wait_ge(s[f"w1_copied{h}"], tile + 1)
                        at_least(pe, s[f"hid_ready{h}"], tile)
                        for j in range(3):
                            first = (3 * h + j) * 128
                            for c in range(2):
                                ins = pe.matmul(banks[2 + h][:, j * 128:(j + 1) * 128], w1_now[0:HALF + c, p % 2, c, first:first + 128],
                                                xT[0:HALF + c, p % 2, c, :], start=c == 0, stop=c == 1)
                        ins.then_inc(s[f"up_done{h}"], 1)
                if (at := xtile_at(i, p, -1)) is not None:
                    turn_rows(*at, i + (1 if p < 3 else 2))
                if xtile_at(i, p, 1) is not None:
                    par = (p - 1) % 2
                    pe.wait_ge(s["w2_copied"], tile)
                    for h in range(2):
                        pe.wait_ge(s[f"hid_ready{h}"], tile)
                    at_least(pe, s["y_biased"], tile - 2)
                    for c in range(FF // 128):
                        ins = pe.matmul(banks[6 + par][:, 0:D], hidT[:, par, c * 128:(c + 1) * 128],
                                        w2_now[:, par, c * D:(c + 1) * D], start=c == 0, stop=c == FF // 128 - 1)
                    ins.then_inc(s["down_done"], 1)
            expert_steps(pe, expert)


_INS = """x x_txt itok_BS_0_99 itok_BS_1_36498 itok_BS_0_2047 fside_BS_concept_values mask_BS_f1_0 mask_BS_i2_0 L0_tok_W L0_tok_b
L0_tok_pos_emb L0_txt_concept_emb L0_txt_segment_emb L0_txt_w_age L0_txt_phi_age L0_txt_merge_w L0_txt_merge_b L0_txt_proj_w
L0_txt_proj_b L0_attn_W_Q L0_attn_b_Q L0_attn_W_K L0_attn_b_K L0_attn_W_V L0_attn_b_V L0_attn_W_O L0_attn_b_O L0_ffn_ln1_g
L0_ffn_ln1_b L0_ffn_qkv_w L0_ffn_proj_w L0_ffn_proj_b L0_ffn_ln2_g L0_ffn_ln2_b L0_ffn_gate_w L0_ffn_gate_b L0_ffn_w1 L0_ffn_b1
L0_ffn_w2 L0_ffn_b2""".split()


def kernel(**inputs):
    import numpy as _np
    import concourse.bacc as _bacc
    from concourse import mybir as _mybir
    from concourse.bass_utils import run_bass_kernel_spmd as _run

    nc = _bacc.Bacc("TRN2", target_bir_lowering=False, num_devices=1)
    arrays, args = {}, {}

    def give(name, a):
        arrays[f"in_{name}"] = a
        args[name] = nc.dram_tensor(f"in_{name}", a.shape, _mybir.dt.from_np(a.dtype), kind="ExternalInput").ap()
    for name in _INS:
        give(name, _np.ascontiguousarray(inputs[name]))
    freq = _np.exp(_np.arange(0, T_EMB, 2, dtype=_np.float32) * (-math.log(10000.0) / T_EMB)).astype(_np.float32)
    give("pos_freq", _np.repeat(freq, 2)[None, :])
    quarter = _np.zeros((1, 3 * T_EMB), _np.float32)
    quarter[0, 2 * T_EMB + 1::2] = 1.0
    give("quarter", quarter)
    out = nc.dram_tensor("out_0", (B, S, D), _mybir.dt.float32, kind="ExternalOutput").ap()
    program(nc, args, out)
    r = _run(nc, [arrays], core_ids=[0])
    return r.results[0]["out_0"]
```
